# Optimizing a Trainium2 kernel written in Bass

```python
import numpy as np
import jax
import jax.numpy as jnp

def _softmax(x, axis=-1):
    return jax.nn.softmax(x, axis=axis)

def _gelu(x):
    return jax.nn.gelu(x, approximate=True)

def _silu(x):
    return jax.nn.silu(x)

def _sigmoid(x):
    return jax.nn.sigmoid(x)

def _layernorm(x, axis=-1, eps=1e-05):
    m = jnp.mean(x, axis=axis, keepdims=True)
    v = jnp.var(x, axis=axis, keepdims=True)
    return (x - m) / jnp.sqrt(v + eps)

def _scatter_add(tgt, idx, src, axis=0):
    return tgt.at[idx].add(src)

def _segment_sum(src, seg, n):
    return jax.ops.segment_sum(src, seg, n)
kernel_name = 'mk_seq_preln_d1_jaxref_r4_23611e'

def setup_inputs(seed: int=0):
    np.random.seed(seed)
    _w = jnp.asarray

    def _L0_attn_setup():
        import jax, jax.numpy as jnp
        import numpy as np
        import math
        NUM_HEADS = 4
        NUM_MEM = 4
        TOPK = 2
        CAPACITY = 0.5
        GATE_NORM = 16.0
        EPS = 1e-05
        B, S, D = (4, 512, 256)
        DK, DV = (128, 256)
        HDK, HDV = (DK // NUM_HEADS, DV // NUM_HEADS)
        LOW = 16

        def _transform(x, routing_mask, sel):
            b, s0, d = x.shape
            k = sel.shape[2]
            xr = jnp.repeat(x, k, axis=1)
            s = s0 * k
            mem_flat = sel.reshape(b, -1).reshape(-1)
            batch_idx = jnp.repeat(jnp.arange(b), s)
            combined = batch_idx * NUM_MEM + mem_flat
            sorted_idx = jnp.argsort(combined)
            x_sorted = xr.reshape(b * s, d)[sorted_idx]
            counts = routing_mask.sum(1)
            offset = jnp.cumsum(counts, axis=1)
            flat_off = (offset + jnp.arange(b)[:, None] * s).reshape(-1)
            cap_len = math.ceil(s0 * CAPACITY)
            prev = jnp.concatenate([jnp.zeros((1,), flat_off.dtype), flat_off[:-1]])
            idx = jnp.arange(cap_len)[None, :] + prev[:, None]
            trunc = idx + counts.reshape(-1)[:, None] - cap_len
            mask = (trunc < flat_off[:, None]) & (trunc >= 0) & (trunc >= prev[:, None])
            trunc = jnp.where(mask, trunc, 0)
            gathered = x_sorted[trunc.reshape(-1)]
            tx = gathered.reshape(b * NUM_MEM, cap_len, d) * mask[..., None]
            tx = tx.reshape(b, NUM_MEM, cap_len, d).transpose(1, 0, 2, 3)
            return (tx, trunc, sorted_idx, mask)

        def _reconstruct(ty, trunc, sorted_idx, rw, mask, b, s0):
            M, _, cap, H, dv = ty.shape
            g = ty.transpose(1, 0, 2, 3, 4).reshape(b * M * cap, H, dv)
            g = g * mask.reshape(-1)[:, None, None]
            res = jnp.zeros((b * s0 * TOPK, H, dv), ty.dtype).at[trunc.reshape(-1)].add(g)
            inv = jnp.argsort(sorted_idx)
            out = res[inv].reshape(b, s0, TOPK, H, dv)
            return (out * rw[..., None, None]).sum(2)

        def _gla(q, k, v, gk):

            def step(Smat, inp):
                qt, kt, vt, gt = inp
                Smat = Smat * jnp.exp(gt)[..., None] + kt[..., None] * vt[..., None, :]
                o = jnp.einsum('...k,...kv->...v', qt, Smat)
                return (Smat, o)
            S0 = jnp.zeros(q.shape[1:-1] + (q.shape[-1], v.shape[-1]), q.dtype)
            _, o = jax.lax.scan(step, S0, (q, k, v, gk))
            return o

        def _forward(x, w_gate, w_q, w_k, w_v, w_gk1, w_gk2, b_gk, w_ks, w_vs, w_gk1s, w_gk2s, b_gks, w_g, w_o, norm_w):
            b, s0, d = x.shape
            scale = HDK ** (-0.5)
            probs = jax.nn.softmax(x @ w_gate, -1)
            rw, sel = jax.lax.top_k(probs, TOPK)
            rw = rw / rw.sum(-1, keepdims=True)
            routing_mask = jax.nn.one_hot(sel, NUM_MEM, dtype=jnp.int32).sum(2)
            tx, trunc, sorted_idx, mask = _transform(x, routing_mask, sel)
            cap = tx.shape[2]
            q = jnp.einsum('mbtd,dk->mbtk', tx, w_q).reshape(NUM_MEM, b, cap, NUM_HEADS, HDK) * scale
            k = jnp.einsum('mbtd,mdk->mbtk', tx, w_k).reshape(NUM_MEM, b, cap, NUM_HEADS, HDK)
            v = jnp.einsum('mbtd,mdk->mbtk', tx, w_v).reshape(NUM_MEM, b, cap, NUM_HEADS, HDV)
            gk = jnp.einsum('mbtr,mrk->mbtk', jnp.einsum('mbtd,mdr->mbtr', tx, w_gk1), w_gk2) + b_gk[:, None, None, :]
            gk = (jax.nn.log_sigmoid(gk) / GATE_NORM).reshape(NUM_MEM, b, cap, NUM_HEADS, HDK)
            to_t = lambda a: jnp.moveaxis(a, 2, 0)
            o_mem = jnp.moveaxis(_gla(to_t(q), to_t(k), to_t(v), to_t(gk)), 0, 2)
            o_rout = _reconstruct(o_mem, trunc, sorted_idx, rw, mask, b, s0)
            qs = (x @ w_q).reshape(b, s0, NUM_HEADS, HDK) * scale
            ks = (x @ w_ks).reshape(b, s0, NUM_HEADS, HDK)
            vs = (x @ w_vs).reshape(b, s0, NUM_HEADS, HDV)
            gks = (jax.nn.log_sigmoid(x @ w_gk1s @ w_gk2s + b_gks) / GATE_NORM).reshape(b, s0, NUM_HEADS, HDK)
            tt = lambda a: jnp.moveaxis(a, 1, 0)
            o_sh = jnp.moveaxis(_gla(tt(qs), tt(ks), tt(vs), tt(gks)), 0, 1)
            o = o_rout + o_sh
            g = (x @ w_g).reshape(b, s0, NUM_HEADS, HDV)
            o = o * jax.lax.rsqrt(jnp.mean(o * o, -1, keepdims=True) + EPS) * norm_w
            o = o * (g * jax.nn.sigmoid(g))
            return o.reshape(b, s0, DV) @ w_o
        key = jax.random.key(seed)
        ks = jax.random.split(key, 17)
        n = lambda i, shp: 0.02 * jax.random.normal(ks[i], shp, dtype=jnp.float32)
        return {'x': jax.random.normal(ks[0], (B, S, D), dtype=jnp.float32), 'w_gate': n(1, (D, NUM_MEM)), 'w_q': n(2, (D, DK)), 'w_k': n(3, (NUM_MEM, D, DK)), 'w_v': n(4, (NUM_MEM, D, DV)), 'w_gk1': n(5, (NUM_MEM, D, LOW)), 'w_gk2': n(6, (NUM_MEM, LOW, DK)), 'b_gk': n(7, (NUM_MEM, DK)), 'w_ks': n(8, (D, DK)), 'w_vs': n(9, (D, DV)), 'w_gk1s': n(10, (D, LOW)), 'w_gk2s': n(11, (LOW, DK)), 'b_gks': n(12, (DK,)), 'w_g': n(13, (D, DV)), 'w_o': n(14, (DV, D)), 'norm_w': jnp.ones((HDV,), dtype=jnp.float32)}
    _L0_attn_in = _L0_attn_setup()

    def _L0_ffn_setup():
        import jax, jax.numpy as jnp
        import numpy as np
        CAPACITY_FACTOR = 1.0
        key = jax.random.key(seed)
        ks = jax.random.split(key, 5)
        B, S, D, E, F = (2, 512, 256, 8, 1024)
        x = jax.random.normal(ks[0], (B, S, D), dtype=jnp.float32)
        Ws = jax.random.normal(ks[1], (D, E), dtype=jnp.float32) * (1.0 / np.sqrt(D))
        bs = jnp.zeros((E,), dtype=jnp.float32)
        W1 = jax.random.normal(ks[2], (E, D, F), dtype=jnp.float32) * (1.0 / np.sqrt(D))
        b1 = jnp.zeros((E, F), dtype=jnp.float32)
        W2 = jax.random.normal(ks[3], (E, F, D), dtype=jnp.float32) * (1.0 / np.sqrt(F))
        b2 = jnp.zeros((E, D), dtype=jnp.float32)
        return {'x': x, 'Ws': Ws, 'bs': bs, 'W1': W1, 'b1': b1, 'W2': W2, 'b2': b2}
    _L0_ffn_in = _L0_ffn_setup()
    _d = {'L0_attn_x': _L0_attn_in['x'], 'L0_attn_w_gate': _L0_attn_in['w_gate'], 'L0_attn_w_q': _L0_attn_in['w_q'], 'L0_attn_w_k': _L0_attn_in['w_k'], 'L0_attn_w_v': _L0_attn_in['w_v'], 'L0_attn_w_gk1': _L0_attn_in['w_gk1'], 'L0_attn_w_gk2': _L0_attn_in['w_gk2'], 'L0_attn_b_gk': _L0_attn_in['b_gk'], 'L0_attn_w_ks': _L0_attn_in['w_ks'], 'L0_attn_w_vs': _L0_attn_in['w_vs'], 'L0_attn_w_gk1s': _L0_attn_in['w_gk1s'], 'L0_attn_w_gk2s': _L0_attn_in['w_gk2s'], 'L0_attn_b_gks': _L0_attn_in['b_gks'], 'L0_attn_w_g': _L0_attn_in['w_g'], 'L0_attn_w_o': _L0_attn_in['w_o'], 'L0_attn_norm_w': _L0_attn_in['norm_w'], 'L0_ffn_Ws': _L0_ffn_in['Ws'], 'L0_ffn_bs': _L0_ffn_in['bs'], 'L0_ffn_W1': _L0_ffn_in['W1'], 'L0_ffn_b1': _L0_ffn_in['b1'], 'L0_ffn_W2': _L0_ffn_in['W2'], 'L0_ffn_b2': _L0_ffn_in['b2']}
    _x0 = _d['L0_attn_x']
    _d['L0_attn_x'] = jax.random.normal(jax.random.fold_in(jax.random.key(seed), 1), (8, 512, 256), dtype=_x0.dtype)
    del _x0
    return _d

def reference(L0_attn_x, L0_attn_w_gate, L0_attn_w_q, L0_attn_w_k, L0_attn_w_v, L0_attn_w_gk1, L0_attn_w_gk2, L0_attn_b_gk, L0_attn_w_ks, L0_attn_w_vs, L0_attn_w_gk1s, L0_attn_w_gk2s, L0_attn_b_gks, L0_attn_w_g, L0_attn_w_o, L0_attn_norm_w, L0_ffn_Ws, L0_ffn_bs, L0_ffn_W1, L0_ffn_b1, L0_ffn_W2, L0_ffn_b2):

    def _L0_attn_ref(x, w_gate, w_q, w_k, w_v, w_gk1, w_gk2, b_gk, w_ks, w_vs, w_gk1s, w_gk2s, b_gks, w_g, w_o, norm_w):
        import jax, jax.numpy as jnp
        import numpy as np
        import math
        NUM_HEADS = 4
        NUM_MEM = 4
        TOPK = 2
        CAPACITY = 0.5
        GATE_NORM = 16.0
        EPS = 1e-05
        B, S, D = (4, 512, 256)
        DK, DV = (128, 256)
        HDK, HDV = (DK // NUM_HEADS, DV // NUM_HEADS)
        LOW = 16

        def _transform(x, routing_mask, sel):
            b, s0, d = x.shape
            k = sel.shape[2]
            xr = jnp.repeat(x, k, axis=1)
            s = s0 * k
            mem_flat = sel.reshape(b, -1).reshape(-1)
            batch_idx = jnp.repeat(jnp.arange(b), s)
            combined = batch_idx * NUM_MEM + mem_flat
            sorted_idx = jnp.argsort(combined)
            x_sorted = xr.reshape(b * s, d)[sorted_idx]
            counts = routing_mask.sum(1)
            offset = jnp.cumsum(counts, axis=1)
            flat_off = (offset + jnp.arange(b)[:, None] * s).reshape(-1)
            cap_len = math.ceil(s0 * CAPACITY)
            prev = jnp.concatenate([jnp.zeros((1,), flat_off.dtype), flat_off[:-1]])
            idx = jnp.arange(cap_len)[None, :] + prev[:, None]
            trunc = idx + counts.reshape(-1)[:, None] - cap_len
            mask = (trunc < flat_off[:, None]) & (trunc >= 0) & (trunc >= prev[:, None])
            trunc = jnp.where(mask, trunc, 0)
            gathered = x_sorted[trunc.reshape(-1)]
            tx = gathered.reshape(b * NUM_MEM, cap_len, d) * mask[..., None]
            tx = tx.reshape(b, NUM_MEM, cap_len, d).transpose(1, 0, 2, 3)
            return (tx, trunc, sorted_idx, mask)

        def _reconstruct(ty, trunc, sorted_idx, rw, mask, b, s0):
            M, _, cap, H, dv = ty.shape
            g = ty.transpose(1, 0, 2, 3, 4).reshape(b * M * cap, H, dv)
            g = g * mask.reshape(-1)[:, None, None]
            res = jnp.zeros((b * s0 * TOPK, H, dv), ty.dtype).at[trunc.reshape(-1)].add(g)
            inv = jnp.argsort(sorted_idx)
            out = res[inv].reshape(b, s0, TOPK, H, dv)
            return (out * rw[..., None, None]).sum(2)

        def _gla(q, k, v, gk):

            def step(Smat, inp):
                qt, kt, vt, gt = inp
                Smat = Smat * jnp.exp(gt)[..., None] + kt[..., None] * vt[..., None, :]
                o = jnp.einsum('...k,...kv->...v', qt, Smat)
                return (Smat, o)
            S0 = jnp.zeros(q.shape[1:-1] + (q.shape[-1], v.shape[-1]), q.dtype)
            _, o = jax.lax.scan(step, S0, (q, k, v, gk))
            return o

        def _forward(x, w_gate, w_q, w_k, w_v, w_gk1, w_gk2, b_gk, w_ks, w_vs, w_gk1s, w_gk2s, b_gks, w_g, w_o, norm_w):
            b, s0, d = x.shape
            scale = HDK ** (-0.5)
            probs = jax.nn.softmax(x @ w_gate, -1)
            rw, sel = jax.lax.top_k(probs, TOPK)
            rw = rw / rw.sum(-1, keepdims=True)
            routing_mask = jax.nn.one_hot(sel, NUM_MEM, dtype=jnp.int32).sum(2)
            tx, trunc, sorted_idx, mask = _transform(x, routing_mask, sel)
            cap = tx.shape[2]
            q = jnp.einsum('mbtd,dk->mbtk', tx, w_q).reshape(NUM_MEM, b, cap, NUM_HEADS, HDK) * scale
            k = jnp.einsum('mbtd,mdk->mbtk', tx, w_k).reshape(NUM_MEM, b, cap, NUM_HEADS, HDK)
            v = jnp.einsum('mbtd,mdk->mbtk', tx, w_v).reshape(NUM_MEM, b, cap, NUM_HEADS, HDV)
            gk = jnp.einsum('mbtr,mrk->mbtk', jnp.einsum('mbtd,mdr->mbtr', tx, w_gk1), w_gk2) + b_gk[:, None, None, :]
            gk = (jax.nn.log_sigmoid(gk) / GATE_NORM).reshape(NUM_MEM, b, cap, NUM_HEADS, HDK)
            to_t = lambda a: jnp.moveaxis(a, 2, 0)
            o_mem = jnp.moveaxis(_gla(to_t(q), to_t(k), to_t(v), to_t(gk)), 0, 2)
            o_rout = _reconstruct(o_mem, trunc, sorted_idx, rw, mask, b, s0)
            qs = (x @ w_q).reshape(b, s0, NUM_HEADS, HDK) * scale
            ks = (x @ w_ks).reshape(b, s0, NUM_HEADS, HDK)
            vs = (x @ w_vs).reshape(b, s0, NUM_HEADS, HDV)
            gks = (jax.nn.log_sigmoid(x @ w_gk1s @ w_gk2s + b_gks) / GATE_NORM).reshape(b, s0, NUM_HEADS, HDK)
            tt = lambda a: jnp.moveaxis(a, 1, 0)
            o_sh = jnp.moveaxis(_gla(tt(qs), tt(ks), tt(vs), tt(gks)), 0, 1)
            o = o_rout + o_sh
            g = (x @ w_g).reshape(b, s0, NUM_HEADS, HDV)
            o = o * jax.lax.rsqrt(jnp.mean(o * o, -1, keepdims=True) + EPS) * norm_w
            o = o * (g * jax.nn.sigmoid(g))
            return o.reshape(b, s0, DV) @ w_o
        return _forward(x, w_gate, w_q, w_k, w_v, w_gk1, w_gk2, b_gk, w_ks, w_vs, w_gk1s, w_gk2s, b_gks, w_g, w_o, norm_w)

    def _L0_ffn_ref(x, Ws, bs, W1, b1, W2, b2):
        import jax, jax.numpy as jnp
        import numpy as np
        CAPACITY_FACTOR = 1.0
        B, S, D = x.shape
        E = Ws.shape[1]
        N = B * S
        k = int(CAPACITY_FACTOR * N / E)
        xf = x.reshape(N, D)
        route_prob = jax.nn.softmax(xf @ Ws + bs, axis=-1).T
        route_vals, routes = jax.lax.top_k(route_prob, k)
        xin = xf[routes]
        h = jax.nn.gelu(jnp.einsum('ekd,edf->ekf', xin, W1) + b1[:, None, :])
        out = jnp.einsum('ekf,efd->ekd', h, W2) + b2[:, None, :]
        out = out * route_vals[..., None]
        final = jnp.zeros((N, D), dtype=x.dtype).at[routes.reshape(-1)].add(out.reshape(-1, D))
        return final.reshape(B, S, D)
    x = L0_attn_x
    x = x + _L0_attn_ref(_layernorm(x, axis=-1), L0_attn_w_gate, L0_attn_w_q, L0_attn_w_k, L0_attn_w_v, L0_attn_w_gk1, L0_attn_w_gk2, L0_attn_b_gk, L0_attn_w_ks, L0_attn_w_vs, L0_attn_w_gk1s, L0_attn_w_gk2s, L0_attn_b_gks, L0_attn_w_g, L0_attn_w_o, L0_attn_norm_w)
    x = x + _L0_ffn_ref(_layernorm(x, axis=-1), L0_ffn_Ws, L0_ffn_bs, L0_ffn_W1, L0_ffn_b1, L0_ffn_W2, L0_ffn_b2)
    return x

_drawn_inputs = setup_inputs


def setup_inputs(seed=0):
    import zlib

    import numpy as np

    out = dict(_drawn_inputs(seed))
    spreads = {'L0_attn_norm_w': (1.0, 0.6),
     'L0_ffn_bs': (0.0, 0.1),
     'L0_ffn_b1': (0.0, 0.3),
     'L0_ffn_b2': (0.0, 0.1)}
    factors = {'L0_attn_w_gk1': 28.525,
     'L0_attn_w_gk2': 29.896,
     'L0_attn_b_gk': 200.0,
     'L0_attn_w_gk1s': 25.26,
     'L0_attn_w_gk2s': 24.391,
     'L0_attn_b_gks': 200.0}
    for name, (base, spread) in spreads.items():
        noise = np.random.default_rng([zlib.crc32(name.encode()), seed]).standard_normal(out[name].shape)
        drawn = base * np.exp(spread * noise) if base else spread * noise
        out[name] = jnp.asarray(drawn.astype(out[name].dtype))
    for name, factor in factors.items():
        out[name] = (out[name] * factor).astype(out[name].dtype)
    return out
```

```python
from contextlib import ExitStack

import concourse.bass as bass
from concourse import mybir

F32 = mybir.dt.float32
BF16 = mybir.dt.bfloat16
I32 = mybir.dt.int32
ALU = mybir.AluOpType
ACT = mybir.ActivationFunctionType
AX = mybir.AxisListType

P = 128
B, S, D = 8, 512, 256
NT = B * S // P
TB = S // P
NH, HDK, HDV = 4, 32, 64
M, CAP = 4, 256
LOW = 16
NS = M + 1
SHARED = M
CH = 64
HALVES = ((CH // 2, 0, CH // 2), (CH, CH // 2, CH))
NU_SH = NT
NU = NU_SH + B * M * CAP // P
ROWS = NU * P
QKL = 2 * P + LOW
E, F = 8, 1024
KTOP = B * S // E
JT = KTOP // P
FT = F // P
GN = 16.0
EPS = 1e-5
EXP_LIM = 85.0
ARENA = 15 * 1024
OUT_OF_RANGE = float(1 << 20)


class Unit:

    def __init__(self, c, i=0, stride=0):
        self.c = c
        self.n = c + i * stride if stride else c
        self.quad = c // 4 + i * (stride // 4) if stride else c // 4
        self.r4, self.r2 = c % 4, c % 2
        if c < NU_SH:
            self.stream, self.first = SHARED, c % TB == 0
        else:
            pos = (c - NU_SH) % (2 * M)
            self.stream, self.first = pos // 2, pos % 2 == 0


def unit_slots(eng, slot, last_slot):
    def static(s):
        slot(lambda k: Unit(s - k) if 0 <= s - k < NU else None)

    for s in range(8):
        static(s)
    with eng.Fori(0, (NU_SH - 8) // 4) as i:
        for u in range(4):
            slot(lambda k: Unit(8 + u - k, i, 4))
    for s in range(NU_SH, NU_SH + 8):
        static(s)
    with eng.Fori(0, (NU - NU_SH - 8) // 8) as i:
        for u in range(8):
            slot(lambda k: Unit(NU_SH + 8 + u - k, i, 8))
    for s in range(NU, last_slot + 1):
        static(s)


def build(nc, x, w_gate, w_q, w_k, w_v, w_gk1, w_gk2, b_gk, w_ks, w_vs, w_gk1s, w_gk2s, b_gks, w_g, w_o,
          norm_w, Ws, bs, W1, b1, W2, b2, out):
    xf = x.rearrange("b s d -> (b s) d")
    outf = out.rearrange("b s d -> (b s) d")
    x_c = nc.dram_tensor("x_c", (ROWS, D), F32, kind="Internal").ap()
    o_c = nc.dram_tensor("o_c", (ROWS, D), F32, kind="Internal").ap()
    x_p = nc.dram_tensor("x_p", (B * S, D + E), F32, kind="Internal").ap()
    idx_d = nc.dram_tensor("idx_d", (E, KTOP), I32, kind="Internal").ap()

    with ExitStack() as ctx:
        def sb(name, shape, dt=F32):
            return ctx.enter_context(nc.sbuf_tensor(name, shape, dt))

        def sem(name):
            return ctx.enter_context(nc.semaphore(name))

        def sems(name, n):
            return [sem(f"{name}{i}") for i in range(n)]

        bank = [ctx.enter_context(nc.psum_tensor(f"bank{i}", [P, 512], F32)) for i in range(8)]

        ident = sb("ident", [P, P])
        relm = sb("relm", [P, P])
        spanm = sb("spanm", [P, 4])
        headm = sb("headm", [P, NH, P])
        causal = sb("causal", [P, CH])
        after = sb("after", [P, P])
        ones = sb("ones", [P, P])
        ones_bf = sb("ones_bf", [P, P], BF16)
        before_bf = sb("before_bf", [P, P], BF16)
        zeros = sb("zeros", [P, 2048])
        ibuf = sb("ibuf", [P, B, TB, M], I32)
        lastrow = sb("lastrow", [P, B, TB, M])
        i32f = sb("i32f", [P, 32])
        pidx = sb("pidx", [P, 1])
        scanm = sb("scanm", [P, 2, E, NT])
        epst = sb("epst", [P, 1])

        wgg = sb("wgg", [P, 2, D + M])
        wo = sb("wo", [P, 2, D])
        nwb = sb("nwb", [P, D])
        wsb = sb("wsb", [P, 2, E])
        bsb = sb("bsb", [P, E])
        b1r = sb("b1r", [E * FT, P])
        b1c = sb("b1c", [P, E * FT])
        b2b = sb("b2b", [P, E, D])

        xres = sb("xres", [P, NT, D])
        big = sb("big", [P, NT * D])
        xn = big[:, :].rearrange("p (t d) -> p t d", d=D)
        gs = sb("gs", [P, NT, D])

        st6 = sb("st6", [P, TB, 6])
        mv = sb("mv", [P, TB, 2])
        held = sb("held", [P, 1])
        lnv = sb("lnv", [P, TB])
        rstd = sb("rstd", [P, TB])
        xta = sb("xta", [P, 2, 2, P])
        eg = sb("eg", [P, 2, D])
        eg1 = sb("eg1", [P, D])
        eg2 = sb("eg2", [P, D])
        eg3 = sb("eg3", [P, D])
        lg = sb("lg", [P, NT, M])

        rt = [sb(f"rt{i}", [P, NT, M]) for i in range(10)]
        rs = [sb(f"rs{i}", [P, NT]) for i in range(12)]
        wt = sb("wt", [P, 2, NT])
        sidx = sb("sidx", [P, 2, NT], I32)
        gidx = sb("gidx", [P, 2, NT], I32)
        keyw = sb("keyw", [P, M])

        arena = sb("arena", [P, ARENA])
        arena_at = [0]

        def carve(shape, dt=F32, of=None):
            n = 1
            for d in shape[1:]:
                n *= d
            words = n * (2 if dt == BF16 else 4) // 4
            ap = arena[:, arena_at[0]:arena_at[0] + words]
            arena_at[0] += words
            assert arena_at[0] <= ARENA
            if dt != F32:
                ap = ap.bitcast(dt)
            names = "abcd"[:len(shape) - 1]
            if len(names) > 1:
                ap = ap.rearrange(f"p ({' '.join(names)}) -> p {' '.join(names)}",
                                  **dict(zip(names[1:], shape[2:])))
            return ap

        dv = lambda name, shape, dt=F32: carve(shape, dt)

        wqk = dv("wqk", [P, NS, 2, QKL])
        wv = dv("wv", [P, NS, 2, D])
        w2g = dv("w2g", [P, NS, P])
        xin = dv("xin", [P, 4, D])
        xt = dv("xt", [P, 2, 2, P])
        qks = dv("qks", [P, 2, 288])
        vv = dv("vv", [P, 4, D])
        lowt = dv("lowt", [P, 2, P])
        zab = dv("zab", [P, P])
        zex = dv("zex", [P, P])
        zln = dv("zln", [P, P])
        gg = dv("gg", [P, P])
        rp = dv("rp", [P, 132])
        rm = dv("rm", [P, P])
        ee = dv("ee", [P, 4, 264])
        qkt = dv("qkt", [P, 2, 2 * P])
        qbd = dv("qbd", [P, 2, NH, P])
        kt = dv("kt", [P, P])
        am = dv("am", [P, 2, NH, P])
        s0 = dv("s0", [P, 2, HDV])
        s1 = dv("s1", [P, 2, HDV])
        wa = dv("wa", [P, HDV])
        wb = dv("wb", [P, HDV])
        ob = dv("ob", [P, 4, D])

        osh = big[:, 0:2048].rearrange("p (r j d) -> p r j d", r=2, j=TB)
        og = big[:, 2048:6144].rearrange("p (r k j d) -> p r k j d", r=2, k=2, j=TB)
        oa = big[:, 6144:7168].rearrange("p (j d) -> p j d", j=TB)
        osq = big[:, 7168:8192].rearrange("p (j d) -> p j d", j=TB)
        arena_at[0] = 0
        hs = dv("hs", [P, TB * NH])
        hl = dv("hl", [P, TB * NH])
        hr = dv("hr", [P, TB * NH])
        on = dv("on", [P, TB, D])
        on2 = dv("on2", [P, TB, D])
        ont = dv("ont", [P, 2, TB * P])
        x1 = dv("x1", [P, TB, D])
        xn2 = dv("xn2", [P, TB, D])
        xn2t = dv("xn2t", [P, 2, TB * P])

        arena_at[0] = 8320
        l8 = dv("l8", [P, NT, E])
        pr = dv("pr", [P, NT, E])
        p8 = dv("p8", [P, NT, E])
        thr = dv("thr", [P, E], I32)
        bitv = dv("bitv", [P, E], I32)
        cand = dv("cand", [P, E], I32)
        take = dv("take", [P, E], I32)
        cmp = dv("cmp", [P, 2, NT, E], BF16)
        cnt8 = dv("cnt8", [P, E])
        tot = dv("tot", [P, 2, E, NT])
        incl = dv("incl", [P, 2, E, NT])
        pos = dv("pos", [P, 2, NT, E])
        sel = dv("sel", [P, 2, NT, E])
        posi = dv("posi", [P, NT, E], I32)
        hii = dv("hii", [P, NT, E], I32)
        loi = dv("loi", [P, NT, E], I32)
        hif = dv("hif", [P, NT, E])
        lof = dv("lof", [P, NT, E])
        oha = gs[:, :, :].rearrange("p t d -> p (t d)")[:, 0:4096].bitcast(BF16).rearrange(
            "p (n c) -> p n c", c=32)
        ohb = gs[:, :, :].rearrange("p t d -> p (t d)")[:, 4096:8192].bitcast(BF16).rearrange(
            "p (n c) -> p n c", c=32)
        cidx = sb("cidx", [P, 2, P])
        idxc = sb("idxc", [P, 2, 16], I32)
        idxs = sb("idxs", [P, E, JT], I32)

        w1s = xres[:, 0:16, :].rearrange("p t d -> p (t d)").rearrange("p (r k f) -> p r k f", r=2, k=2)
        w2s = xres[:, 16:32, :].rearrange("p t d -> p (t d)").rearrange("p (r f d) -> p r f d", r=2, f=FT)
        ht = big[:, :].rearrange("p (r f t) -> p r f t", r=2, f=FT)
        arena_at[0] = 0
        xe = dv("xe", [P, 3, JT, D + E])
        xet = dv("xet", [P, 2, 2, KTOP])
        yb = dv("yb", [P, JT, D])
        ye = dv("ye", [P, 2, JT, D])

        c_step = sem("c_step")
        c_dve = sem("c_dve")
        w_in = sem("w_in")
        w_in2 = sem("w_in2")
        zero_st = sem("zero_st")
        x_in = sems("x_in", 2)
        a_st = sem("a_st"); a_mv = sem("a_mv"); a_lnv = sem("a_lnv"); a_rstd = sem("a_rstd")
        a_xn = sem("a_xn"); xn_st = sem("xn_st")
        a_tp = sem("a_tp"); a_xt = sem("a_xt"); a_g = sem("a_g"); a_eg = sem("a_eg")
        a_lg = sem("a_lg"); a_1 = sem("a_1"); a_2 = sem("a_2"); a_3 = sem("a_3"); a_gs = sem("a_gs")
        r_step = sem("r_step"); r_sub = sem("r_sub"); r_exp = sem("r_exp"); r_rout = sem("r_rout")
        r_suf = sem("r_suf"); r_idx = sem("r_idx"); scat = sem("scat")
        d_in = sems("d_in", 4)
        d_tp = sem("d_tp"); d_xt = sem("d_xt"); d_qk = sem("d_qk"); d_v = sem("d_v")
        d_qks = sem("d_qks"); d_vs = sem("d_vs"); d_lt = sem("d_lt"); d_lts = sem("d_lts"); d_z = sem("d_z")
        d_ab = sem("d_ab"); d_ex = sem("d_ex"); d_ln = sem("d_ln"); d_g = sem("d_g"); d_r = sem("d_r")
        d_rp = sem("d_rp"); d_rm = sem("d_rm"); d_ep = sem("d_ep"); d_em = sem("d_em")
        d_qkt = sem("d_qkt"); d_qT = sem("d_qT"); d_kT = sem("d_kT"); d_qbd = sem("d_qbd"); d_kts = sem("d_kts")
        d_s = sem("d_s"); d_u1 = sem("d_u1"); d_am = sem("d_am")
        d_s0 = sem("d_s0"); d_w0 = sem("d_w0"); d_s1 = sem("d_s1"); d_w1 = sem("d_w1")
        d_o = sem("d_o"); d_ob = sem("d_ob")
        d_st = sems("d_st", 4)
        f_sh = sems("f_sh", 2); f_g = sems("f_g", 2)
        f_a0 = sem("f_a0")
        f_oa = sem("f_oa"); f_sq = sem("f_sq"); f_hs = sem("f_hs"); f_hl = sem("f_hl"); f_hr = sem("f_hr")
        f_on = sem("f_on"); f_on2 = sem("f_on2"); f_tp = sem("f_tp"); f_ont = sem("f_ont")
        f_y = sem("f_y"); f_x1 = sem("f_x1"); out_st = sem("out_st")
        f_st = sem("f_st"); f_mv = sem("f_mv"); f_lnv = sem("f_lnv"); f_rstd = sem("f_rstd")
        f_xn2 = sem("f_xn2"); xp_st = sem("xp_st"); f_tp2 = sem("f_tp2"); f_xt2 = sem("f_xt2")
        f_l = sem("f_l"); f_l8 = sem("f_l8")
        s_step = sem("s_step"); s_sub = sem("s_sub"); s_exp = sem("s_exp"); s_p8 = sem("s_p8"); p8_st = sem("p8_st")
        s_cand = sem("s_cand"); s_cmp = sem("s_cmp"); s_cnt = sem("s_cnt"); s_red = sem("s_red")
        s_take = sem("s_take"); s_thr = sem("s_thr"); s_bit = sem("s_bit")
        s_pre = sem("s_pre"); s_tot = sem("s_tot"); s_oh = sem("s_oh"); s_idx = sem("s_idx"); s_idxc = sem("s_idxc")
        idx_st = sem("idx_st"); idx_in = sem("idx_in")
        b1_t = sem("b1_t"); b1_c = sem("b1_c")
        e_w = sems("e_w", 2); e_x = sems("e_x", 3)
        e_tp = sem("e_tp")
        e_xt = sem("e_xt")
        e_h = sem("e_h"); e_gl = sem("e_gl")
        e_y = sem("e_y"); e_yb = sem("e_yb"); e_ye = sem("e_ye")
        e_st = sem("e_st")

        block = ctx.enter_context(nc.Block())

        @block.gpsimd
        def _(pool):
            done = [0]

            def step(ins):
                done[0] += 1
                ins.then_inc(c_step, 1)
                pool.wait_ge(c_step, done[0])

            def select(ap, pattern, base, mult, op=ALU.is_ge, fill=0.0):
                step(nc.gpsimd.affine_select(out=ap, in_=ap, compare_op=op, fill=fill, base=base,
                                             pattern=pattern, channel_multiplier=mult))

            step(nc.gpsimd.memset(zeros[:, :], 0.0))
            step(nc.gpsimd.memset(ident[:, :], 0.0))
            select(ident[:, :], [[-1, P]], 0, 1, ALU.not_equal, 1.0)
            step(nc.gpsimd.memset(epst[:, :], EPS))
            step(nc.gpsimd.memset(ones[:, :], 1.0))
            step(nc.gpsimd.memset(ones_bf[:, :], 1.0))
            step(nc.gpsimd.memset(after[:, :], 1.0))
            select(after[:, :], [[-1, P]], -1, 1)
            step(nc.gpsimd.memset(before_bf[:, :], 1.0))
            select(before_bf[:, :], [[1, P]], -1, -1)
            for j in range(P // 32):
                blk = relm[:, 32 * j:32 * j + 32]
                step(nc.gpsimd.memset(blk, (1.0 if j % 2 else -1.0) / GN))
                select(blk, [[0, 32]], -32 * j, 1)
                select(blk, [[0, 32]], 32 * j + 31, -1)
                if j % 2:
                    select(blk, [[1, 32]], 32 * j, -1)
                else:
                    select(blk, [[-1, 32]], -32 * j - 1, 1)
            step(nc.gpsimd.memset(spanm[:, :], 0.0))
            for c, (lo, hi) in enumerate(((0, 32), (32, 96), (96, 128))):
                step(nc.gpsimd.memset(spanm[:, c:c + 1], 1.0 / GN))
                select(spanm[:, c:c + 1], [[0, 1]], -lo, 1)
                select(spanm[:, c:c + 1], [[0, 1]], hi - 1, -1)
            step(nc.gpsimd.memset(headm[:, :, :], float(HDK) ** -0.5))
            select(headm[:, :, :], [[-HDK, NH], [0, P]], 0, 1)
            select(headm[:, :, :], [[HDK, NH], [0, P]], HDK - 1, -1)
            step(nc.gpsimd.memset(causal[:, :], 1.0))
            for c in range(2):
                select(causal[CH * c:CH * c + CH, :], [[1, CH]], 0, -1)
            step(nc.gpsimd.iota(ibuf[:, :, :, :], pattern=[[M * CAP, B], [0, TB], [CAP, M]],
                                base=NU_SH * P + CAP - 1, channel_multiplier=0))
            step(nc.gpsimd.tensor_copy(lastrow[:, :, :, :], ibuf[:, :, :, :]))
            ib = ibuf[:, :, :, :].rearrange("p a b c -> p (a b c)")
            step(nc.gpsimd.iota(ib[:, 0:32], pattern=[[1, 32]], base=0, channel_multiplier=0))
            step(nc.gpsimd.tensor_copy(i32f[:, :], ib[:, 0:32]))
            step(nc.gpsimd.iota(ib[:, 32:33], pattern=[[0, 1]], base=0, channel_multiplier=1))
            step(nc.gpsimd.tensor_copy(pidx[:, :], ib[:, 32:33]))
            step(nc.gpsimd.memset(scanm[:, :, :, :], 1.0))
            step(nc.gpsimd.memset(scanm[:, :, :, 0:1], 0.0))
            for m in range(M):
                step(nc.gpsimd.memset(keyw[:, m:m + 1], float(M - m)))
            step(nc.gpsimd.memset(qks[:, :, QKL:288], 0.0))
            step(nc.gpsimd.memset(qks[:, :, QKL:QKL + 1], 1.0))
            step(nc.gpsimd.memset(am[:, :, :, :], 0.0))
            assert done[0] == CONST_STEPS, done[0]

            pool.wait_ge(r_idx, 4)
            pool.wait_ge(zero_st, 16 * 4)
            for t in range(NT):
                for k in range(2):
                    nc.gpsimd.indirect_dma_start(
                        x_c, bass.IndirectOffsetOnAxis(sidx[:, k, t:t + 1], 0), xn[:, t, :], None,
                        bounds_check=ROWS - 1, oob_is_err=False).then_inc(scat, 16)

            for r in range(4):
                pool.wait_ge(d_st[r], 16 * (NU // 4))
            for b in range(B):
                if b >= 2:
                    pool.wait_ge(f_oa, b - 1)
                for j in range(TB):
                    for k in range(2):
                        t = b * TB + j
                        nc.gpsimd.indirect_dma_start(
                            og[:, b % 2, k, j, :], None, o_c,
                            bass.IndirectOffsetOnAxis(gidx[:, k, t:t + 1], 0),
                            bounds_check=ROWS - 1, oob_is_err=False).then_inc(f_g[b % 2], 16)

            pool.wait_ge(idx_in, 16)
            pool.wait_ge(xp_st, 16 * B)
            pool.wait_ge(p8_st, 16)
            pool.wait_ge(out_st, 16 * B)

            def gather(e):
                if e >= 3:
                    pool.wait_ge(e_tp, 2 * (e - 2))
                    pool.wait_ge(e_ye, JT * (e - 2))
                for j in range(JT):
                    nc.gpsimd.indirect_dma_start(
                        xe[:, e % 3, j, :], None, x_p, bass.IndirectOffsetOnAxis(idxs[:, e, j:j + 1], 0),
                        bounds_check=B * S - 1, oob_is_err=False).then_inc(e_x[e % 3], 16)

            gather(0)
            gather(1)
            gather(2)
            for e in range(E):
                if e:
                    pool.wait_ge(e_st, 16 * JT * e)
                for j in range(JT):
                    pool.wait_ge(e_ye, JT * e + j + 1)
                    nc.gpsimd.indirect_dma_start(
                        outf, bass.IndirectOffsetOnAxis(idxs[:, e, j:j + 1], 0), ye[:, e % 2, j, :], None,
                        bounds_check=B * S - 1, oob_is_err=True, compute_op=ALU.add).then_inc(e_st, 16)
                if e + 3 < E:
                    gather(e + 3)
            pool.wait_ge(e_st, 16 * JT * E)

        @block.sync
        def _(sp):
            def load_x(b):
                if b >= 2:
                    sp.wait_ge(x_in[b % 2], 16 * (b // 2))
                sp.dma_start(xres[:, TB * b:TB * b + TB, :],
                             xf[S * b:S * b + S, :].rearrange("(t p) d -> p t d", p=P)).then_inc(x_in[b % 2], 16)

            for b in range(B):
                load_x(b)
            with sp.Fori(0, B) as b:
                sp.wait_ge(a_xn, b * TB + TB)
                sp.dma_start(x_c[bass.ds(b * S, S), :].rearrange("(t p) d -> p t d", p=P),
                             xn[:, bass.ds(b * TB, TB), :]).then_inc(xn_st, 16)
            sp.wait_ge(xn_st, 16 * B)

            def slot(unit):
                u = unit(0)
                if u:
                    if u.c == NU_SH:
                        sp.wait_ge(scat, 16 * 2 * NT)
                    if u.c >= 4:
                        sp.wait_ge(d_tp, u.n - 3)
                    sp.dma_start(xin[:, u.r4, :], x_c[bass.ds(u.n * P, P), :]).then_inc(d_in[u.r4], 16)
                u = unit(7)
                if u:
                    sp.wait_ge(d_ob, u.n + 1)
                    sp.dma_start(o_c[bass.ds(u.n * P, P), :], ob[:, u.r4, :]).then_inc(d_st[u.r4], 16)

            unit_slots(sp, slot, NU + 6)

            for r in range(4):
                sp.wait_ge(d_st[r], 16 * (NU // 4))

            def load_osh(b):
                if b >= 2:
                    sp.wait_ge(f_oa, b - 1)
                sp.dma_start(osh[:, b % 2, :, :], o_c[S * b:S * b + S, :].rearrange("(t p) d -> p t d", p=P))\
                    .then_inc(f_sh[b % 2], 16)

            load_osh(0)
            for b in range(B):
                if b + 1 < B:
                    load_osh(b + 1)
                sp.wait_ge(f_x1, 2 * b + 2)
                sp.dma_start(outf[S * b:S * b + S, :].rearrange("(t p) d -> p t d", p=P), x1[:, :, :])\
                    .then_inc(out_st, 16)
                sp.wait_ge(f_xn2, TB * b + TB)
                sp.dma_start(x_p[S * b:S * b + S, 0:D].rearrange("(t p) d -> p t d", p=P), xn2[:, :, :])\
                    .then_inc(xp_st, 16)

            def load_w(e):
                if e >= 2:
                    sp.wait_ge(e_y, JT * (e - 1))
                sp.dma_start(w1s[:, e % 2, :, :], W1[e].rearrange("(k p) f -> p k f", p=P)).then_inc(e_w[e % 2], 16)
                sp.dma_start(w2s[:, e % 2, :, :], W2[e].rearrange("(f p) d -> p f d", p=P)).then_inc(e_w[e % 2], 16)

            load_w(0)
            load_w(1)
            sp.wait_ge(s_p8, 1)
            sp.dma_start(x_p[:, D:D + E].rearrange("(t p) e -> p t e", p=P), p8[:, :, :],
                         allow_slow_non_contiguous=True).then_inc(p8_st, 16)
            sp.wait_ge(s_idxc, 4)
            for g in range(2):
                sp.dma_start(idx_d[4 * g:4 * g + 4, :].rearrange("e (a c) -> (e a) c", a=32), idxc[:, g, :])\
                    .then_inc(idx_st, 16)
            sp.wait_ge(idx_st, 32)
            sp.dma_start(idxs[:, :, :], idx_d.rearrange("e (p j) -> p e j", p=P),
                         allow_slow_non_contiguous=True).then_inc(idx_in, 16)
            for e in range(2, E):
                load_w(e)

        @block.scalar
        def _(act):
            act.preload_act_table_set("natural_log_exp_and_others")
            kp = lambda w: w.rearrange("(k p) n -> p k n", p=P)
            for m in range(NS):
                wk, wvm, wl, w2, bb = ((w_ks, w_vs, w_gk1s, w_gk2s, b_gks) if m == SHARED else
                                       (w_k[m], w_v[m], w_gk1[m], w_gk2[m], b_gk[m]))
                act.dma_start(wqk[:, m, :, 0:P], kp(w_q)).then_inc(w_in, 16)
                act.dma_start(wqk[:, m, :, P:2 * P], kp(wk)).then_inc(w_in, 16)
                act.dma_start(wqk[:, m, :, 2 * P:QKL], kp(wl)).then_inc(w_in, 16)
                act.dma_start(wv[:, m, :, :], kp(wvm)).then_inc(w_in, 16)
                act.dma_start(w2g[0:LOW, m, :], w2).then_inc(w_in, 16)
                act.dma_start(w2g[LOW:LOW + 1, m, :], bb.rearrange("(a n) -> a n", a=1)).then_inc(w_in, 16)
            act.dma_start(wgg[:, :, 0:D], kp(w_g)).then_inc(w_in, 16)
            act.dma_start(wgg[:, :, D:D + M], kp(w_gate)).then_inc(w_in, 16)
            act.dma_start(nwb[:, :].rearrange("p (h v) -> p h v", h=NH),
                          norm_w.rearrange("(a b n) -> a b n", a=1, b=1).to_broadcast([P, NH, HDV]))\
                .then_inc(w_in, 16)
            act.dma_start(wo[:, :, :], kp(w_o)).then_inc(w_in2, 16)
            act.dma_start(wsb[:, :, :], kp(Ws)).then_inc(w_in2, 16)
            act.dma_start(bsb[:, :], bs.rearrange("(a n) -> a n", a=1).to_broadcast([P, E])).then_inc(w_in2, 16)
            act.dma_start(b1r[:, :], b1.rearrange("e (f p) -> (e f) p", p=P)).then_inc(w_in2, 16)
            act.dma_start(b2b[:, :, :], b2.rearrange("(a e) n -> a e n", a=1).to_broadcast([P, E, D]))\
                .then_inc(w_in2, 16)
            act.wait_ge(c_step, 1)
            for q in range(4):
                act.dma_start(x_c[NU_SH * P + 2048 * q:NU_SH * P + 2048 * q + 2048, :]
                              .rearrange("(p a) d -> p (a d)", p=P).rearrange("p (c d) -> p c d", c=2),
                              zeros[:, :].unsqueeze(1).to_broadcast([P, 2, 2048])).then_inc(zero_st, 16)
            act.wait_ge(c_step, CONST_STEPS)

            def a_slot(b_std, b_tile):
                if b_std is not None:
                    act.wait_ge(a_mv, b_std * TB + TB)
                    nc.scalar.activation(lnv[:, :], mv[:, :, 1], ACT.Ln, bias=epst[:, 0:1]).then_inc(a_lnv, 1)
                    act.wait_ge(a_lnv, b_std + 1)
                    nc.scalar.activation(rstd[:, :], lnv[:, :], ACT.Exp, scale=-0.5).then_inc(a_rstd, 1)
                if b_tile is not None:
                    for j in range(TB):
                        t = b_tile * TB + j
                        act.wait_ge(a_tp, t + 1)
                        nc.scalar.activation(xta[:, j % 2, :, :], bank[j % 2][:, 0:D].rearrange("p (k t) -> p k t", k=2),
                                             ACT.Copy).then_inc(a_xt, 1)
                        act.wait_ge(a_g, t + 1)
                        nc.scalar.activation(eg[:, j % 2, :], bank[2 + j % 2][:, 0:D], ACT.Exp, scale=-1.0)\
                            .then_inc(a_eg, 1)

            a_slot(0, None)
            with act.Fori(1, B) as b:
                a_slot(b, b - 1)
            a_slot(None, B - 1)
            act.wait_ge(r_sub, 1)
            nc.scalar.activation(rt[1][:, :, :], rt[0][:, :, :], ACT.Exp).then_inc(r_exp, 1)

            def slot(unit):
                u = unit(0)
                if u:
                    act.wait_ge(d_tp, u.n + 1)
                    if u.c >= 2:
                        act.wait_ge(d_v, u.n - 1)
                    nc.scalar.activation(xt[:, u.r2, :, :], bank[0][:, 0:D].rearrange("p (k t) -> p k t", k=2),
                                         ACT.Copy).then_inc(d_xt, 1)
                u = unit(2)
                if u:
                    act.wait_ge(d_z, u.n + 1)
                    nc.scalar.activation(zab[:, :], bank[3][:, 0:P], ACT.Abs).then_inc(d_ab, 1)
                    act.wait_ge(d_ab, u.n + 1)
                    nc.scalar.activation(zex[:, :], zab[:, :], ACT.Exp, scale=-1.0).then_inc(d_ex, 1)
                    act.wait_ge(d_ex, u.n + 1)
                    if u.c >= 1:
                        act.wait_ge(d_g, u.n)
                    nc.scalar.activation(zln[:, :], zex[:, :], ACT.Ln, bias=1.0).then_inc(d_ln, 1)
                u = unit(1)
                if u:
                    act.wait_ge(d_qk, u.n + 1)
                    if u.c >= 2:
                        act.wait_ge(d_qkt, u.n - 1)
                    nc.scalar.activation(qks[:, u.r2, 0:QKL], bank[1][:, 0:QKL], ACT.Copy).then_inc(d_qks, 1)
                    act.wait_ge(d_v, u.n + 1)
                    if u.c >= 4:
                        act.wait_ge(d_o, u.n - 3)
                    nc.scalar.activation(vv[:, u.r4, :], bank[2][:, 0:D], ACT.Copy).then_inc(d_vs, 1)
                u = unit(3)
                if u:
                    act.wait_ge(d_kT, u.n + 1)
                    if u.c >= 1:
                        act.wait_ge(d_u1, u.n)
                    nc.scalar.activation(kt[:, :], bank[0][:, 0:P], ACT.Copy).then_inc(d_kts, 1)
                u = unit(2)
                if u:
                    act.wait_ge(d_rp, u.n + 1)
                    if u.c >= 4:
                        act.wait_ge(d_w1, u.n - 2)
                        act.wait_ge(d_qkt, u.n - 3)
                    nc.scalar.activation(ee[:, u.r4, 0:132], rp[:, :], ACT.Exp).then_inc(d_ep, 1)
                    act.wait_ge(d_rm, u.n + 1)
                    nc.scalar.activation(ee[:, u.r4, 132:260], rm[:, :], ACT.Exp, scale=-1.0).then_inc(d_em, 1)
                u = unit(1)
                if u:
                    act.wait_ge(d_lt, u.n + 1)
                    if u.c >= 2:
                        act.wait_ge(d_z, u.n - 1)
                    nc.scalar.activation(lowt[0:32, u.r2, :], bank[3][0:32, P:2 * P], ACT.Copy).then_inc(d_lts, 1)

            unit_slots(act, slot, NU + 3)

            def f_slot(b1_, b2_, b3_):
                if b1_ is not None:
                    act.wait_ge(f_oa, b1_ + 1)
                    nc.scalar.activation(osq[:, :, :], oa[:, :, :], ACT.Square).then_inc(f_sq, 1)
                if b2_ is not None:
                    for k in range(2):
                        act.wait_ge(f_tp, 2 * b2_ + k + 1)
                        nc.scalar.activation(ont[:, k, :], bank[k][:, :], ACT.Copy).then_inc(f_ont, 1)
                if b3_ is not None:
                    for k in range(2):
                        act.wait_ge(f_tp2, 2 * b3_ + k + 1)
                        nc.scalar.activation(xn2t[:, k, :], bank[4 + k][:, :], ACT.Copy).then_inc(f_xt2, 1)
                if b1_ is not None:
                    act.wait_ge(f_hs, b1_ + 1)
                    nc.scalar.activation(hl[:, :], hs[:, :], ACT.Ln, bias=epst[:, 0:1], scale=1.0 / HDV)\
                        .then_inc(f_hl, 1)
                    act.wait_ge(f_hl, b1_ + 1)
                    nc.scalar.activation(hr[:, :], hl[:, :], ACT.Exp, scale=-0.5).then_inc(f_hr, 1)
                if b2_ is not None:
                    act.wait_ge(f_mv, b2_ * TB + TB)
                    nc.scalar.activation(lnv[:, :], mv[:, :, 1], ACT.Ln, bias=epst[:, 0:1]).then_inc(f_lnv, 1)
                    act.wait_ge(f_lnv, b2_ + 1)
                    nc.scalar.activation(rstd[:, :], lnv[:, :], ACT.Exp, scale=-0.5).then_inc(f_rstd, 1)

            f_slot(0, None, None)
            f_slot(1, 0, None)
            with act.Fori(2, B) as b:
                f_slot(b, b - 1, b - 2)
            f_slot(None, B - 1, B - 2)
            f_slot(None, None, B - 1)
            act.wait_ge(s_sub, 1)
            nc.scalar.activation(pr[:, :, :], l8[:, :, :], ACT.Exp).then_inc(s_exp, 1)

            act.wait_ge(b1_t, 1)
            nc.scalar.activation(b1c[:, :], bank[7][:, 0:E * FT], ACT.Copy).then_inc(b1_c, 1)
            act.wait_ge(b1_c, 1)

            def rows_t(e, r):
                for k in range(2):
                    act.wait_ge(e_tp, 2 * e + k + 1)
                    nc.scalar.activation(xet[:, r, k, :], bank[k][:, :], ACT.Copy).then_inc(e_xt, 1)

            def e_slot(e, r, first, last, col):
                if not first:
                    act.wait_ge(e_y, JT * (e - 1))
                for f in range(FT):
                    act.wait_ge(e_h, FT * e + f + 1)
                    nc.scalar.activation(ht[:, r, f, :], bank[2 + f % 4][:, :], ACT.Gelu_apprx_tanh,
                                         bias=b1c[:, col(f)]).then_inc(e_gl, 1)
                    if f == 3 and not last:
                        rows_t(e + 1, 1 - r)

            rows_t(0, 0)
            for e in range(E):
                e_slot(e, e % 2, e < 2, e == E - 1, lambda f: slice(e * FT + f, e * FT + f + 1))

        @block.vector
        def _(dve):
            dve.wait_ge(c_step, CONST_STEPS)

            def norm_tiles(src, dst, b, st_sem, mv_sem, rs_sem, xn_sem):
                for j in range(TB):
                    nc.vector.bn_stats(st6[:, j, :], src(j)).then_inc(st_sem, 1)
                dve.wait_ge(st_sem, b * TB + TB)
                nc.vector.memset(held[:, :], 0.0)
                for j in range(TB):
                    nc.vector.bn_aggr(mv[:, j, :], st6[:, j, :]).then_inc(mv_sem, 1)
                dve.wait_ge(rs_sem, b + 1)
                for j in range(TB):
                    nc.vector.tensor_scalar(dst(j), src(j), mv[:, j, 0:1], rstd[:, j:j + 1],
                                            ALU.subtract, ALU.mult).then_inc(xn_sem, 1)

            def gate_tiles(b):
                for j in range(TB):
                    t = b * TB + j
                    pg = bank[2 + j % 2]
                    dve.wait_ge(a_eg, t + 1)
                    nc.vector.tensor_copy(lg[:, t, :], pg[:, D:D + M]).then_inc(a_lg, 1)
                    dve.wait_ge(a_2, t) if (not isinstance(b, int) or t) else None
                    nc.vector.tensor_scalar(eg1[:, :], eg[:, j % 2, :], 1.0, None, ALU.add).then_inc(a_1, 1)
                    dve.wait_ge(a_1, t + 1)
                    nc.vector.reciprocal(eg2[:, :], eg1[:, :]).then_inc(a_2, 1)
                    dve.wait_ge(a_2, t + 1)
                    nc.vector.tensor_tensor(eg3[:, :], pg[:, 0:D], eg2[:, :], ALU.mult).then_inc(a_3, 1)
                    dve.wait_ge(a_3, t + 1)
                    nc.vector.tensor_tensor(gs[:, t, :], eg3[:, :], nwb[:, :], ALU.mult).then_inc(a_gs, 1)

            def load_wait(r, n):
                dve.wait_ge(x_in[r], 16 * n)

            def norm_a(b):
                norm_tiles(lambda j: xres[:, b * TB + j, :], lambda j: xn[:, b * TB + j, :], b,
                           a_st, a_mv, a_rstd, a_xn)

            load_wait(0, 1)
            norm_a(0)
            dve.wait_ge(w_in, 16 * W_IN)
            load_wait(1, 1)
            norm_a(1)
            gate_tiles(0)
            with dve.Fori(1, B // 2) as i:
                load_wait(0, i + 1)
                norm_a(i * 2)
                gate_tiles(i * 2 - 1)
                load_wait(1, i + 1)
                norm_a(i * 2 + 1)
                gate_tiles(i * 2)
            gate_tiles(B - 1)

            done = [0]

            def step(ins):
                done[0] += 1
                ins.then_inc(r_step, 1)
                dve.wait_ge(r_step, done[0])

            per_m = lambda a: a.unsqueeze(2).to_broadcast([P, NT, M])
            dve.wait_ge(a_lg, NT)
            step(nc.vector.tensor_reduce(rs[0][:, :], lg[:, :, :], AX.X, ALU.max))
            nc.vector.tensor_tensor(rt[0][:, :, :], lg[:, :, :], per_m(rs[0][:, :]), ALU.subtract).then_inc(r_sub, 1)
            dve.wait_ge(r_exp, 1)
            step(nc.vector.tensor_reduce(rs[1][:, :], rt[1][:, :, :], AX.X, ALU.add))
            step(nc.vector.reciprocal(rs[2][:, :], rs[1][:, :]))
            step(nc.vector.tensor_tensor(rt[2][:, :, :], rt[1][:, :, :], per_m(rs[2][:, :]), ALU.mult))
            prob, value = rt[2], [rs[3], rs[4]]
            pick = [rt[4], rt[5]]
            keyb = keyw[:, :].unsqueeze(1).to_broadcast([P, NT, M])
            for k in range(2):
                step(nc.vector.tensor_reduce(value[k][:, :], prob[:, :, :], AX.X, ALU.max))
                step(nc.vector.tensor_tensor(rt[3][:, :, :], prob[:, :, :], per_m(value[k][:, :]), ALU.is_equal))
                step(nc.vector.tensor_tensor(rt[6][:, :, :], rt[3][:, :, :], keyb, ALU.mult))
                step(nc.vector.tensor_reduce(rs[5][:, :], rt[6][:, :, :], AX.X, ALU.max))
                step(nc.vector.tensor_tensor(pick[k][:, :, :], rt[6][:, :, :], per_m(rs[5][:, :]), ALU.is_equal))
                if k == 0:
                    step(nc.vector.scalar_tensor_tensor(rt[7][:, :, :], pick[0][:, :, :], -4.0, prob[:, :, :],
                                                        ALU.mult, ALU.add))
                    prob = rt[7]
            nc.vector.tensor_tensor(rt[8][:, :, :], pick[0][:, :, :], pick[1][:, :, :], ALU.add).then_inc(r_rout, 1)
            step(nc.vector.tensor_tensor(rs[6][:, :], value[0][:, :], value[1][:, :], ALU.add))
            step(nc.vector.reciprocal(rs[7][:, :], rs[6][:, :]))
            dve.wait_ge(r_suf, 1)
            suf = bank[4][:, 0:NT * M].rearrange("p (t m) -> p t m", m=M)
            step(nc.vector.tensor_scalar(rt[0][:, :, :], suf, float(CAP - 1), None, ALU.is_le))
            lastr = lastrow[:, :, :, :].rearrange("p b j m -> p (b j) m")
            step(nc.vector.tensor_tensor(rt[1][:, :, :], lastr, suf, ALU.subtract))
            for k in range(2):
                step(nc.vector.tensor_tensor(rt[2][:, :, :], pick[k][:, :, :], rt[0][:, :, :], ALU.mult))
                step(nc.vector.tensor_reduce(rs[8][:, :], rt[2][:, :, :], AX.X, ALU.add))
                step(nc.vector.tensor_tensor(rt[3][:, :, :], rt[2][:, :, :], rt[1][:, :, :], ALU.mult))
                step(nc.vector.tensor_reduce(rs[9][:, :], rt[3][:, :, :], AX.X, ALU.add))
                step(nc.vector.tensor_tensor(rs[10][:, :], value[k][:, :], rs[7][:, :], ALU.mult))
                step(nc.vector.tensor_tensor(wt[:, k, :], rs[10][:, :], rs[8][:, :], ALU.mult))
                nc.vector.tensor_copy(gidx[:, k, :], rs[9][:, :]).then_inc(r_idx, 1)
                step(nc.vector.tensor_scalar(rs[10][:, :], rs[8][:, :], -OUT_OF_RANGE, OUT_OF_RANGE,
                                             ALU.mult, ALU.add))
                step(nc.vector.tensor_tensor(rs[11][:, :], rs[10][:, :], rs[9][:, :], ALU.add))
                nc.vector.tensor_copy(sidx[:, k, :], rs[11][:, :]).then_inc(r_idx, 1)

            def slot(unit):
                u = unit(2)
                if u:
                    dve.wait_ge(d_ln, u.n + 1)
                    if u.c >= 1:
                        dve.wait_ge(d_r, u.n)
                    nc.vector.scalar_tensor_tensor(gg[:, :], bank[3][:, 0:P], 0.0, zln[:, :],
                                                   ALU.min, ALU.subtract).then_inc(d_g, 1)
                u = unit(3)
                if u:
                    dve.wait_ge(d_qT, u.n + 1)
                    if u.c >= 2:
                        dve.wait_ge(d_o, u.n - 1)
                    nc.vector.tensor_tensor(qbd[:, u.r2, :, :],
                                            bank[5][:, 0:P].unsqueeze(1).to_broadcast([P, NH, P]),
                                            headm[:, :, :], ALU.mult).then_inc(d_qbd, 1)
                u = unit(2)
                if u:
                    dve.wait_ge(d_r, u.n + 1)
                    if u.c >= 1:
                        dve.wait_ge(d_ep, u.n)
                        dve.wait_ge(d_em, u.n)
                    nc.vector.tensor_scalar(rp[:, :], bank[4][:, 0:132], EXP_LIM, None, ALU.min).then_inc(d_rp, 1)
                    dve.wait_ge(d_rp, u.n + 1)
                    nc.vector.tensor_scalar(rm[:, :], rp[:, 0:P], -EXP_LIM, None, ALU.max).then_inc(d_rm, 1)
                    dve.wait_ge(d_em, u.n + 1)
                    dve.wait_ge(d_qks, u.n + 1)
                    if u.c >= 2:
                        dve.wait_ge(d_u1, u.n - 1)
                    nc.vector.tensor_tensor(
                        qkt[:, u.r2, :].rearrange("p (a c) -> p a c", a=2),
                        qks[:, u.r2, 0:2 * P].rearrange("p (a c) -> p a c", a=2),
                        ee[:, u.r4, :].rearrange("p (a c) -> p a c", a=2)[:, :, 0:P], ALU.mult).then_inc(d_qkt, 1)
                u = unit(4)
                if u:
                    dve.wait_ge(d_o, u.n + 1)
                    if u.c >= 4:
                        dve.wait_ge(d_st[u.r4], u.quad * 16)
                    nc.vector.tensor_copy(ob[:, u.r4, :], bank[7][:, 0:D]).then_inc(d_ob, 1)
                u = unit(3)
                if u:
                    dve.wait_ge(d_s, u.n + 1)
                    for c in range(2):
                        for lo, t0, t1 in HALVES:
                            h = slice(CH * c, CH * c + lo)
                            ins = nc.vector.tensor_tensor(
                                am[h, u.r2, :, CH * c + t0:CH * c + t1],
                                bank[6][h, 0:NH * CH].rearrange("p (h t) -> p h t", h=NH)[:, :, t0:t1],
                                causal[h, t0:t1].unsqueeze(1).to_broadcast([lo, NH, t1 - t0]), ALU.mult)
                    ins.then_inc(d_am, 1)
                    if u.first:
                        nc.vector.memset(s0[:, u.r2, :], 0.0).then_inc(d_s0, 1)
                    else:
                        dve.wait_ge(d_w1, u.n)
                        dve.wait_ge(d_ep, u.n + 1)
                        nc.vector.tensor_scalar(s0[:, u.r2, :], wb[:, :], ee[:, u.r4, P:P + 1],
                                                ee[:, (u.r4 - 1) % 4, P + 2:P + 3], ALU.mult, ALU.mult)\
                            .then_inc(d_s0, 1)
                    dve.wait_ge(d_s0, u.n + 1)
                    nc.vector.tensor_tensor(wa[:, :], bank[6][:, 256:256 + HDV], s0[:, u.r2, :], ALU.add)\
                        .then_inc(d_w0, 1)
                    dve.wait_ge(d_w0, u.n + 1)
                    nc.vector.tensor_scalar(s1[:, u.r2, :], wa[:, :], ee[:, u.r4, P + 1:P + 2], None, ALU.mult)\
                        .then_inc(d_s1, 1)
                    dve.wait_ge(d_s1, u.n + 1)
                    dve.wait_ge(d_u1, u.n + 1)
                    nc.vector.tensor_tensor(wb[:, :], bank[5][:, 256:256 + HDV], s1[:, u.r2, :], ALU.add)\
                        .then_inc(d_w1, 1)

            unit_slots(dve, slot, NU + 3)

            def combine(b, r, nload):
                dve.wait_ge(f_sh[r], 16 * nload)
                dve.wait_ge(f_g[r], 16 * 2 * TB * nload)
                if not (isinstance(b, int) and b == 0):
                    dve.wait_ge(f_sq, b)
                    dve.wait_ge(f_on, b)
                for j in range(TB):
                    nc.vector.scalar_tensor_tensor(oa[:, j, :], og[:, r, 0, j, :], wcol(0, b * TB + j),
                                                   osh[:, r, j, :], ALU.mult, ALU.add).then_inc(f_a0, 1)
                for j in range(TB):
                    dve.wait_ge(f_a0, b * TB + j + 1)
                    ins = nc.vector.scalar_tensor_tensor(oa[:, j, :], og[:, r, 1, j, :], wcol(1, b * TB + j),
                                                         oa[:, j, :], ALU.mult, ALU.add)
                ins.then_inc(f_oa, 1)

            def wcol(k, t):
                return wt[:, k, t:t + 1] if isinstance(t, int) else wt[:, k, bass.ds(t, 1)]

            def residual(b):
                if not (isinstance(b, int) and b == 0):
                    dve.wait_ge(out_st, 16 * b)
                    dve.wait_ge(xp_st, 16 * b)
                    dve.wait_ge(f_tp2, 2 * b)
                for q in range(2):
                    dve.wait_ge(f_y, 2 * b + q + 1)
                    nc.vector.tensor_tensor(x1[:, 2 * q:2 * q + 2, :],
                                            bank[2 + q][:, :].rearrange("p (j d) -> p j d", j=2),
                                            xres[:, bass.ds(b * TB + 2 * q, 2), :], ALU.add).then_inc(f_x1, 1)
                dve.wait_ge(f_x1, 2 * b + 2)
                for j in range(TB):
                    nc.vector.bn_stats(st6[:, j, :], x1[:, j, :]).then_inc(f_st, 1)
                dve.wait_ge(f_st, b * TB + TB)
                nc.vector.memset(held[:, :], 0.0)
                for j in range(TB):
                    nc.vector.bn_aggr(mv[:, j, :], st6[:, j, :]).then_inc(f_mv, 1)

            def head_norm(b):
                dve.wait_ge(f_sq, b + 1)
                nc.vector.tensor_reduce(hs[:, :], osq[:, :, :].rearrange("p j (h v) -> p (j h) v", h=NH),
                                        AX.X, ALU.add).then_inc(f_hs, 1)
                dve.wait_ge(f_hr, b + 1)
                nc.vector.tensor_tensor(on[:, :, :].rearrange("p j (h v) -> p (j h) v", h=NH),
                                        oa[:, :, :].rearrange("p j (h v) -> p (j h) v", h=NH),
                                        hr[:, :].unsqueeze(2).to_broadcast([P, TB * NH, HDV]), ALU.mult)\
                    .then_inc(f_on, 1)
                dve.wait_ge(f_on, b + 1)
                if not (isinstance(b, int) and b == 0):
                    dve.wait_ge(f_tp, 2 * b)
                nc.vector.tensor_tensor(on2[:, :, :], on[:, :, :], gs[:, bass.ds(b * TB, TB), :], ALU.mult)\
                    .then_inc(f_on2, 1)

            def norm2(b):
                dve.wait_ge(f_rstd, b + 1)
                for j in range(TB):
                    nc.vector.tensor_scalar(xn2[:, j, :], x1[:, j, :], mv[:, j, 0:1], rstd[:, j:j + 1],
                                            ALU.subtract, ALU.mult).then_inc(f_xn2, 1)

            def router(b):
                dve.wait_ge(f_l, b + 1)
                nc.vector.tensor_tensor(l8[:, bass.ds(b * TB, TB), :],
                                        bank[6][:, 0:TB * E].rearrange("p (j e) -> p j e", e=E),
                                        bsb[:, :].unsqueeze(1).to_broadcast([P, TB, E]), ALU.add).then_inc(f_l8, 1)

            def f_slot(b1_, r, nload, b2_, b3_):
                if b1_ is not None:
                    combine(b1_, r, nload)
                if b2_ is not None:
                    residual(b2_)
                if b1_ is not None:
                    head_norm(b1_)
                if b2_ is not None:
                    norm2(b2_)
                if b3_ is not None:
                    router(b3_)

            dve.wait_ge(w_in2, 16 * 5)
            f_slot(0, 0, 1, None, None)
            f_slot(1, 1, 1, 0, None)
            with dve.Fori(1, B // 2) as i:
                f_slot(i * 2, 0, i + 1, i * 2 - 1, i * 2 - 2)
                f_slot(i * 2 + 1, 1, i + 1, i * 2, i * 2 - 1)
            f_slot(None, 0, 0, B - 1, B - 2)
            f_slot(None, 0, 0, None, B - 1)

            done[0] = 0

            def sstep(ins):
                done[0] += 1
                ins.then_inc(s_step, 1)
                dve.wait_ge(s_step, done[0])

            per_e = lambda a: a.unsqueeze(2).to_broadcast([P, NT, E])
            dve.wait_ge(f_l8, B)
            sstep(nc.vector.tensor_reduce(rs[0][:, :], l8[:, :, :], AX.X, ALU.max))
            nc.vector.tensor_tensor(l8[:, :, :], l8[:, :, :], per_e(rs[0][:, :]), ALU.subtract).then_inc(s_sub, 1)
            dve.wait_ge(s_exp, 1)
            sstep(nc.vector.tensor_reduce(rs[1][:, :], pr[:, :, :], AX.X, ALU.add))
            sstep(nc.vector.reciprocal(rs[2][:, :], rs[1][:, :]))
            nc.vector.tensor_tensor(p8[:, :, :], pr[:, :, :], per_e(rs[2][:, :]), ALU.mult).then_inc(s_p8, 1)

            nc.vector.memset(thr[:, :], 0).then_inc(s_thr, 1)
            nc.vector.memset(bitv[:, :], 1 << 29).then_inc(s_bit, 1)
            dve.wait_ge(s_p8, 1)
            with dve.Fori(0, 30) as i:
                dve.wait_ge(s_thr, i + 1)
                dve.wait_ge(s_bit, i + 1)
                nc.vector.tensor_tensor(cand[:, :], thr[:, :], bitv[:, :], ALU.bitwise_or).then_inc(s_cand, 1)
                dve.wait_ge(s_cand, i + 1)
                nc.vector.tensor_tensor(cmp[:, 0, :, :], p8[:, :, :],
                                        cand[:, :].bitcast(F32).unsqueeze(1).to_broadcast([P, NT, E]), ALU.is_ge)\
                    .then_inc(s_cmp, 1)
                dve.wait_ge(s_cnt, i + 1)
                nc.vector.tensor_reduce(cnt8[:, :], bank[0][:, 0:NT * E].rearrange("p (t e) -> p e t", e=E),
                                        AX.X, ALU.add).then_inc(s_red, 1)
                dve.wait_ge(s_red, i + 1)
                nc.vector.scalar_tensor_tensor(take[:, :], cnt8[:, :], float(KTOP), bitv[:, :],
                                               ALU.is_ge, ALU.mult).then_inc(s_take, 1)
                dve.wait_ge(s_take, i + 1)
                nc.vector.tensor_tensor(thr[:, :], thr[:, :], take[:, :], ALU.bitwise_or).then_inc(s_thr, 1)
                nc.vector.tensor_scalar(bitv[:, :], bitv[:, :], 1, None, ALU.logical_shift_right).then_inc(s_bit, 1)
            dve.wait_ge(s_thr, 31)
            dve.wait_ge(s_bit, 31)

            thrb = thr[:, :].bitcast(F32).unsqueeze(1).to_broadcast([P, NT, E])
            sstep(nc.vector.tensor_tensor(cmp[:, 0, :, :], p8[:, :, :], thrb, ALU.is_gt))
            nc.vector.tensor_tensor(cmp[:, 1, :, :], p8[:, :, :], thrb, ALU.is_equal).then_inc(s_pre, 1)
            dve.wait_ge(s_tot, 1)
            te = lambda a: a.rearrange("p (k t e) -> p k e t", k=2, e=E)
            sstep(nc.vector.tensor_copy(tot[:, 0, :, :], te(bank[1][:, :])[:, 0]))
            sstep(nc.vector.tensor_copy(tot[:, 1, :, :], te(bank[1][:, :])[:, 1]))
            flat = lambda a: a[:, :, :, :].rearrange("p k e t -> p (k e t)")
            sstep(nc.vector.tensor_tensor_scan(flat(incl), flat(scanm), flat(tot), 0.0, ALU.mult, ALU.add))
            sstep(nc.vector.tensor_tensor(flat(tot), flat(incl), flat(tot), ALU.subtract))
            sstep(nc.vector.tensor_tensor(tot[:, 1, :, :], tot[:, 1, :, :],
                                          incl[:, 0, :, NT - 1:NT].to_broadcast([P, E, NT]), ALU.add))
            for k in range(2):
                sstep(nc.vector.tensor_tensor(pos[:, k, :, :],
                                              bank[2][:, k * 256:k * 256 + 256].rearrange("p (t e) -> p t e", e=E),
                                              tot[:, k, :, :].rearrange("p e t -> p t e"), ALU.add))
            sstep(nc.vector.scalar_tensor_tensor(sel[:, 1, :, :], pos[:, 1, :, :], float(KTOP), cmp[:, 1, :, :],
                                                 ALU.is_lt, ALU.mult))
            sstep(nc.vector.scalar_tensor_tensor(pos[:, 1, :, :], pos[:, 1, :, :], 1.0, sel[:, 1, :, :],
                                                 ALU.add, ALU.mult))
            sstep(nc.vector.scalar_tensor_tensor(pos[:, 0, :, :], pos[:, 0, :, :], 1.0, cmp[:, 0, :, :],
                                                 ALU.add, ALU.mult))
            sstep(nc.vector.tensor_tensor(pos[:, 0, :, :], pos[:, 0, :, :], pos[:, 1, :, :], ALU.add))
            sstep(nc.vector.tensor_scalar(posi[:, :, :], pos[:, 0, :, :], -1.0, None, ALU.add))
            sstep(nc.vector.tensor_scalar(hii[:, :, :], posi[:, :, :], 4, None, ALU.arith_shift_right))
            sstep(nc.vector.tensor_scalar(loi[:, :, :], posi[:, :, :], 15, None, ALU.bitwise_and))
            sstep(nc.vector.tensor_copy(hif[:, :, :], hii[:, :, :]))
            sstep(nc.vector.tensor_copy(lof[:, :, :], loi[:, :, :]))
            flat3 = lambda a: a[:, :, :].rearrange("p t e -> p (t e)").unsqueeze(2)
            iot = i32f[:, :].unsqueeze(1)
            sstep(nc.vector.tensor_tensor(oha[:, :, :], flat3(hif).to_broadcast([P, 256, 32]),
                                          iot.to_broadcast([P, 256, 32]), ALU.is_equal))
            sstep(nc.vector.tensor_tensor(ohb[:, :, 0:16], flat3(lof).to_broadcast([P, 256, 16]),
                                          iot[:, :, 0:16].to_broadcast([P, 256, 16]), ALU.is_equal))
            ohb4 = ohb[:, :, :].rearrange("p (t e) c -> p t e c", e=E)
            for e in range(E):
                sstep(nc.vector.tensor_tensor(ohb4[:, :, e, 16:32], ohb4[:, :, e, 0:16],
                                              i32f[:, :].unsqueeze(2).to_broadcast([P, NT, 16]), ALU.mult))
            nc.vector.tensor_scalar(ohb[:, :, 0:16], ohb[:, :, 0:16], pidx[:, 0:1], None, ALU.mult).then_inc(s_oh, 1)
            dve.wait_ge(s_idx, 1)
            sstep(nc.vector.tensor_copy(cidx[:, :, :], bank[3][:, 0:256].rearrange("p (g c) -> p g c", g=2)))
            for e in range(4):
                q = slice(32 * e, 32 * e + 32)
                nc.vector.scalar_tensor_tensor(idxc[q, :, :], cidx[q, :, 32 * e + 16:32 * e + 32], float(P),
                                               cidx[q, :, 32 * e:32 * e + 16], ALU.mult, ALU.add)\
                    .then_inc(s_idxc, 1)

            for e in range(E):
                r = e % 2
                if e:
                    dve.wait_ge(e_ye, JT * e)
                for j in range(JT):
                    n = JT * e + j
                    dve.wait_ge(e_y, n + 1)
                    nc.vector.tensor_tensor(yb[:, j, :], bank[6 + j % 2][:, 0:D], b2b[:, e, :], ALU.add)\
                        .then_inc(e_yb, 1)
                    dve.wait_ge(e_yb, n + 1)
                    if e >= 2 and j == 0:
                        dve.wait_ge(e_st, 16 * JT * (e - 1))
                    nc.vector.tensor_scalar(ye[:, r, j, :], yb[:, j, :], xe[:, e % 3, j, D + e:D + e + 1], None,
                                            ALU.mult).then_inc(e_ye, 1)

        @block.tensor
        def _(pe):
            pe.wait_ge(c_step, CONST_STEPS)
            pe.wait_ge(w_in, 16 * W_IN)

            def a_tiles(b, skip):
                for j in range(TB):
                    t = b * TB + j
                    pe.wait_ge(a_xn, t + 1)
                    if not (skip and j < 2):
                        pe.wait_ge(a_xt, t - 1)
                    for k in range(2):
                        ins = nc.tensor.transpose(bank[j % 2][:, P * k:P * k + P], xn_lhs(b, j, k), ident[:, :])
                    ins.then_inc(a_tp, 1)
                    pe.wait_ge(a_xt, t + 1)
                    if not (skip and j < 2):
                        pe.wait_ge(a_3, t - 1)
                    for k in range(2):
                        ins = nc.tensor.matmul(bank[2 + j % 2][:, 0:D + M], xta[:, j % 2, k, :], wgg[:, k, :],
                                               start=(k == 0), stop=(k == 1))
                    ins.then_inc(a_g, 1)

            def xn_lhs(b, j, k):
                return xn[:, b * TB + j, P * k:P * k + P]

            for b in range(B):
                a_tiles(b, b == 0)

            pe.wait_ge(r_rout, 1)
            cnt = bank[4][:, 0:NT * M]
            rflat = rt[8][:, :, :].rearrange("p t m -> p (t m)")
            nc.tensor.matmul(cnt, after[:, :], rflat, start=True, stop=False, skip_group_check=True)
            r4 = rflat.rearrange("p (b j m) -> p b j m", b=B, m=M)
            c4 = cnt.rearrange("p (b j m) -> p b j m", b=B, m=M)
            for d in range(1, TB):
                ins = nc.tensor.matmul(c4[:, :, 0:TB - d, :], ones[:, :], r4[:, :, d:TB, :], start=False,
                                       stop=(d == TB - 1), skip_group_check=True)
            ins.then_inc(r_suf, 1)
            pe.wait_ge(r_idx, 4)

            def mm(out_, l, r, a=True, z=True):
                return nc.tensor.matmul(out_, l, r, start=a, stop=z, skip_group_check=True)

            def slot(unit):
                u = unit(0)
                if u:
                    pe.wait_ge(d_in[u.r4], 16 * u.quad + 16)
                    if u.c >= 4:
                        pe.wait_ge(d_kts, u.n - 3)
                    elif u.c >= 1:
                        pe.wait_ge(d_xt, u.n)
                    for k in range(2):
                        ins = nc.tensor.transpose(bank[0][:, P * k:P * k + P], xin[:, u.r4, P * k:P * k + P],
                                                  ident[:, :])
                    ins.then_inc(d_tp, 1)
                u = unit(2)
                if u:
                    pe.wait_ge(d_lts, u.n + 1)
                    mm(bank[3][:, 0:P], lowt[0:LOW + 1, u.r2, :], w2g[0:LOW + 1, u.stream, :]).then_inc(d_z, 1)
                u = unit(1)
                if u:
                    pe.wait_ge(d_xt, u.n + 1)
                    if u.c >= 1:
                        pe.wait_ge(d_qks, u.n)
                        pe.wait_ge(d_vs, u.n)
                    for k in range(2):
                        ins = mm(bank[1][:, 0:QKL], xt[:, u.r2, k, :], wqk[:, u.stream, k, :], k == 0, k == 1)
                    ins.then_inc(d_qk, 1)
                    for k in range(2):
                        ins = mm(bank[2][:, 0:D], xt[:, u.r2, k, :], wv[:, u.stream, k, :], k == 0, k == 1)
                    ins.then_inc(d_v, 1)
                u = unit(3)
                if u:
                    pe.wait_ge(d_qkt, u.n + 1)
                    if u.c >= 1:
                        pe.wait_ge(d_w1, u.n)
                    nc.tensor.transpose(bank[5][:, 0:P], qkt[:, u.r2, 0:P], ident[:, :]).then_inc(d_qT, 1)
                    if unit(0):
                        pe.wait_ge(d_xt, u.n + 4)
                    else:
                        pe.wait_ge(d_kts, u.n)
                    nc.tensor.transpose(bank[0][:, 0:P], qkt[:, u.r2, P:2 * P], ident[:, :]).then_inc(d_kT, 1)
                u = unit(2)
                if u:
                    pe.wait_ge(d_g, u.n + 1)
                    if u.c >= 1:
                        pe.wait_ge(d_rm, u.n)
                    mm(bank[4][:, 0:P], relm[:, :], gg[:, :])
                    mm(bank[4][:, P:P + 4], gg[:, :], spanm[:, :]).then_inc(d_r, 1)
                u = unit(1)
                if u:
                    pe.wait_ge(d_qks, u.n + 1)
                    if u.c >= 1:
                        pe.wait_ge(d_g, u.n)
                    nc.tensor.transpose(bank[3][0:32, P:2 * P], qks[:, u.r2, 2 * P:2 * P + 32], ident[:, :])\
                        .then_inc(d_lt, 1)
                u = unit(4)
                if u:
                    pe.wait_ge(d_am, u.n + 1)
                    pe.wait_ge(d_s1, u.n + 1)
                    if u.c >= 1:
                        pe.wait_ge(d_ob, u.n)
                    for g in range(NH):
                        mm(bank[7][:, HDV * g:HDV * g + HDV], am[:, u.r2, g, :],
                           vv[:, u.r4, HDV * g:HDV * g + HDV], g == 0, False)
                    for c in range(2):
                        if c == 0 and u.first:
                            continue
                        h = slice(CH * c, CH * c + CH)
                        for g in range(NH):
                            ins = mm(bank[7][h, HDV * g:HDV * g + HDV], qbd[:, u.r2, g, h],
                                     (s1 if c else s0)[:, u.r2, :], False, True)
                    ins.then_inc(d_o, 1)
                u = unit(3)
                if u:
                    pe.wait_ge(d_qbd, u.n + 1)
                    pe.wait_ge(d_kts, u.n + 1)
                    if u.c >= 1:
                        pe.wait_ge(d_w0, u.n)
                    for c in range(2):
                        for lo, t0, t1 in HALVES:
                            h = slice(CH * c, CH * c + lo)
                            mm(bank[6][h, 0:NH * CH].rearrange("p (h t) -> p h t", h=NH)[:, :, t0:t1],
                               kt[:, h], qbd[:, u.r2, :, CH * c + t0:CH * c + t1])
                    for c in range(2):
                        h = slice(CH * c, CH * c + CH)
                        for g in range(NH):
                            ins = mm(bank[6 - c][HDK * g:HDK * g + HDK, 256:256 + HDV],
                                     qkt[h, u.r2, P + HDK * g:P + HDK * g + HDK],
                                     vv[h, u.r4, HDV * g:HDV * g + HDV])
                        ins.then_inc(d_u1 if c else d_s, 1)

            unit_slots(pe, slot, NU + 3)
            pe.wait_ge(d_ob, NU)

            pe.wait_ge(w_in2, 16 * 5)

            def project(b):
                pe.wait_ge(f_on2, b + 1)
                for k in range(2):
                    for j in range(TB):
                        ins = nc.tensor.transpose(bank[k][:, P * j:P * j + P], on2[:, j, P * k:P * k + P],
                                                  ident[:, :])
                    ins.then_inc(f_tp, 1)
                pe.wait_ge(f_ont, 2 * b + 2)
                if not (isinstance(b, int) and b == 0):
                    pe.wait_ge(f_x1, 2 * b)
                for j in range(TB):
                    for k in range(2):
                        ins = mm(bank[2 + j // 2][:, D * (j % 2):D * (j % 2) + D], ont[:, k, P * j:P * j + P],
                                 wo[:, k, :], k == 0, k == 1)
                    if j % 2:
                        ins.then_inc(f_y, 1)

            def route(b):
                pe.wait_ge(f_xn2, b * TB + TB)
                for k in range(2):
                    for j in range(TB):
                        ins = nc.tensor.transpose(bank[4 + k][:, P * j:P * j + P], xn2[:, j, P * k:P * k + P],
                                                  ident[:, :])
                    ins.then_inc(f_tp2, 1)
                pe.wait_ge(f_xt2, 2 * b + 2)
                if not (isinstance(b, int) and b == 0):
                    pe.wait_ge(f_l8, b)
                for j in range(TB):
                    for k in range(2):
                        ins = mm(bank[6][:, E * j:E * j + E], xn2t[:, k, P * j:P * j + P], wsb[:, k, :],
                                 k == 0, k == 1)
                ins.then_inc(f_l, 1)

            project(0)
            with pe.Fori(1, B) as b:
                project(b)
                route(b - 1)
            route(B - 1)
            nc.tensor.transpose(bank[7][:, 0:E * FT], b1r[:, :], ident[0:E * FT, 0:E * FT]).then_inc(b1_t, 1)

            with pe.Fori(0, 30) as i:
                pe.wait_ge(s_cmp, i + 1)
                nc.tensor.matmul(bank[0][:, 0:NT * E], ones_bf[:, :], cmp[:, 0, :, :].rearrange("p t e -> p (t e)"),
                                 start=True, stop=True).then_inc(s_cnt, 1)
            pe.wait_ge(s_pre, 1)
            pe.wait_ge(s_step, 4)
            cflat = cmp[:, :, :, :].rearrange("p k t e -> p (k t e)")
            nc.tensor.matmul(bank[2][:, :], before_bf[:, :], cflat, start=True, stop=True)
            nc.tensor.matmul(bank[1][:, :], ones_bf[:, :], cflat, start=True, stop=True).then_inc(s_tot, 1)
            pe.wait_ge(s_oh, 1)
            a4 = oha[:, :, :].rearrange("p (t g) c -> p t g c", g=E)
            b4 = ohb[:, :, :].rearrange("p (t g) c -> p t g c", g=E)

            def digits(t, first, last):
                for g in range(2):
                    ins = mm(bank[3][:, P * g:P * g + P], a4[:, t, 4 * g:4 * g + 4, :].rearrange("p e c -> p (e c)"),
                             b4[:, t, 4 * g:4 * g + 4, :].rearrange("p e c -> p (e c)"),
                             first and g == 0, last)
                return ins

            digits(0, True, False)
            with pe.Fori(1, NT - 1) as t:
                digits(t, False, False)
            digits(NT - 1, False, True).then_inc(s_idx, 1)
            pe.wait_ge(b1_c, 1)
            pe.wait_ge(s_idxc, 4)

            def rows_t(e):
                pe.wait_ge(e_x[e % 3], 16 * JT * (e // 3 + 1))
                if e >= 1:
                    pe.wait_ge(e_xt, 2 * e)
                if e >= 2:
                    pe.wait_ge(e_h, FT * (e - 1))
                for k in range(2):
                    for j in range(JT):
                        ins = nc.tensor.transpose(bank[k][:, P * j:P * j + P], xe[:, e % 3, j, P * k:P * k + P],
                                                  ident[:, :])
                    ins.then_inc(e_tp, 1)

            def hidden(e, r):
                pe.wait_ge(e_w[r], 32 * (e // 2 + 1))
                pe.wait_ge(e_xt, 2 * e + 2)
                for f in range(FT):
                    if e or f >= 4:
                        pe.wait_ge(e_gl, FT * e + f - 3)
                    for k in range(2):
                        ins = mm(bank[2 + f % 4][:, :], w1s[:, r, k, P * f:P * f + P], xet[:, r, k, :],
                                 k == 0, k == 1)
                    ins.then_inc(e_h, 1)
                    if f == 3 and e + 1 < E:
                        rows_t(e + 1)

            def output(e, r):
                pe.wait_ge(e_gl, FT * e + FT)
                for j in range(JT):
                    n = JT * e + j
                    if n >= 2:
                        pe.wait_ge(e_yb, n - 1)
                    for f in range(FT):
                        ins = mm(bank[6 + j % 2][:, 0:D], ht[:, r, f, P * j:P * j + P], w2s[:, r, f, :],
                                 f == 0, f == FT - 1)
                    ins.then_inc(e_y, 1)

            rows_t(0)
            hidden(0, 0)
            for e in range(1, E):
                hidden(e, e % 2)
                output(e - 1, (e - 1) % 2)
            output(E - 1, (E - 1) % 2)


CONST_STEPS = 57
W_IN = 6 * NS + 3

_INS = ['x', 'w_gate', 'w_q', 'w_k', 'w_v', 'w_gk1', 'w_gk2', 'b_gk', 'w_ks', 'w_vs', 'w_gk1s', 'w_gk2s', 'b_gks',
        'w_g', 'w_o', 'norm_w']
_INS = ['L0_attn_' + n for n in _INS] + ['L0_ffn_' + n for n in ['Ws', 'bs', 'W1', 'b1', 'W2', 'b2']]
_OUTS = [((B, S, D), 'float32')]


def kernel(**inputs):
    import numpy as _np
    import concourse.bacc as _bacc
    from concourse import mybir as _mybir
    from concourse.bass_utils import run_bass_kernel_spmd as _run

    nc = _bacc.Bacc("TRN2", target_bir_lowering=False, num_devices=1)
    arrays, args = {}, []
    for name in _INS:
        a = _np.ascontiguousarray(inputs[name])
        arrays[f"in_{name}_dram"] = a
        args.append(nc.dram_tensor(f"in_{name}_dram", a.shape, _mybir.dt.from_np(a.dtype), kind="ExternalInput").ap())
    for i, (shape, dtype) in enumerate(_OUTS):
        dt = _mybir.dt.from_np(_np.dtype(dtype))
        args.append(nc.dram_tensor(f"out_{i}_dram", shape, dt, kind="ExternalOutput").ap())
    build(nc, *args)
    r = _run(nc, [arrays], core_ids=[0])
    got = tuple(r.results[0][f"out_{i}_dram"] for i in range(len(_OUTS)))
    return got[0]
```

```python
from contextlib import ExitStack

import concourse.bass as bass
from concourse import mybir

F32 = mybir.dt.float32
BF16 = mybir.dt.bfloat16
I32 = mybir.dt.int32
ALU = mybir.AluOpType
ACT = mybir.ActivationFunctionType
AX = mybir.AxisListType

P = 128
B, S, D = 8, 512, 256
NT = B * S // P
TB = S // P
NH, HDK, HDV = 4, 32, 64
M, CAP = 4, 256
LOW = 16
NS = M + 1
SHARED = M
CH = 64
HALVES = ((CH // 2, 0, CH // 2), (CH, CH // 2, CH))
NU_SH = NT
NU = NU_SH + B * M * CAP // P
ROWS = NU * P
HALF_B = B // 2
HALF_ROWS = HALF_B * M * CAP
QKL = 2 * P + LOW
E, F = 8, 1024
NW = 4
KTOP = B * S // E
JT = KTOP // P
FT = F // P
GN = 16.0
EPS = 1e-5
EXP_LIM = 85.0
ARENA = 15 * 1024
OUT_OF_RANGE = float(1 << 20)


class Unit:

    def __init__(self, c, i=0, stride=0, least=0):
        self.c = c
        self.half = int(c + stride * least >= NU_SH + (NU - NU_SH) // 2)
        self.n = c + i * stride if stride else c
        self.quad = c // 4 + i * (stride // 4) if stride else c // 4
        self.r4, self.r2 = c % 4, c % 2
        if c < NU_SH:
            self.stream, self.first = SHARED, c % TB == 0
        else:
            pos = (c - NU_SH) % (2 * M)
            self.stream, self.first = pos // 2, pos % 2 == 0


def unit_slots(eng, slot, last_slot, peeled=None):
    def static(s):
        slot(lambda k: Unit(s - k) if 0 <= s - k < NU else None)

    for s in range(8):
        static(s)
    with eng.Fori(0, (NU_SH - 8) // 4) as i:
        for u in range(4):
            slot(lambda k: Unit(8 + u - k, i, 4))
    for s in range(NU_SH, NU_SH + 8):
        static(s)
    rounds = (NU - NU_SH - 8) // 8
    for lo, hi in ((0, rounds),) if peeled is None else ((0, peeled), (peeled + 1, rounds)):
        with eng.Fori(lo, hi) as i:
            for u in range(8):
                slot(lambda k: Unit(NU_SH + 8 + u - k, i, 8, lo))
        if hi == peeled:
            for u in range(8):
                static(NU_SH + 8 + 8 * peeled + u)
    for s in range(NU, last_slot + 1):
        static(s)


def build(nc, x, w_gate, w_q, w_k, w_v, w_gk1, w_gk2, b_gk, w_ks, w_vs, w_gk1s, w_gk2s, b_gks, w_g, w_o,
          norm_w, Ws, bs, W1, b1, W2, b2, out):
    xf = x.rearrange("b s d -> (b s) d")
    outf = out.rearrange("b s d -> (b s) d")
    x_c = nc.dram_tensor("x_c", (ROWS, D), F32, kind="Internal").ap()
    o_s = nc.dram_tensor("o_s", (B * S, D), F32, kind="Internal").ap()
    o_m = [nc.dram_tensor(f"o_m{h}", (HALF_ROWS, D), F32, kind="Internal").ap() for h in range(2)]
    x_p = nc.dram_tensor("x_p", (B * S, D + E), F32, kind="Internal").ap()
    idx_d = nc.dram_tensor("idx_d", (E, KTOP), I32, kind="Internal").ap()

    with ExitStack() as ctx:
        def sb(name, shape, dt=F32):
            return ctx.enter_context(nc.sbuf_tensor(name, shape, dt))

        def sem(name):
            return ctx.enter_context(nc.semaphore(name))

        def sems(name, n):
            return [sem(f"{name}{i}") for i in range(n)]

        bank = [ctx.enter_context(nc.psum_tensor(f"bank{i}", [P, 512], F32)) for i in range(8)]

        ident = sb("ident", [P, P])
        relm = sb("relm", [P, P])
        spanm = sb("spanm", [P, 4])
        headm = sb("headm", [P, NH, P])
        causal = sb("causal", [P, CH])
        after = sb("after", [P, P])
        ones = sb("ones", [P, P])
        ones_bf = sb("ones_bf", [P, P], BF16)
        before_bf = sb("before_bf", [P, P], BF16)
        zeros = sb("zeros", [P, 2048])
        ibuf = sb("ibuf", [P, B, TB, M], I32)
        lastrow = sb("lastrow", [P, B, TB, M])
        i32f = sb("i32f", [P, 32])
        pidx = sb("pidx", [P, 1])
        scanm = sb("scanm", [P, 2, E, NT])
        epst = sb("epst", [P, 1])

        wgg = sb("wgg", [P, 2, D + M])
        wo = sb("wo", [P, 2, D])
        nwb = sb("nwb", [P, D])
        wsb = sb("wsb", [P, 2, E])
        bsb = sb("bsb", [P, E])
        b1r = sb("b1r", [E * FT, P])
        b1c = sb("b1c", [P, E * FT])
        b2b = sb("b2b", [P, E, D])

        xres = sb("xres", [P, NT, D])
        big = sb("big", [P, NT * D])
        xn = big[:, :].rearrange("p (t d) -> p t d", d=D)
        gs = sb("gs", [P, NT, D])

        st6 = sb("st6", [P, TB, 6])
        mv = sb("mv", [P, TB, 2])
        held = sb("held", [P, 1])
        lnv = sb("lnv", [P, TB])
        rstd = sb("rstd", [P, TB])
        xta = sb("xta", [P, 2, 2, P])
        eg = sb("eg", [P, 2, D])
        eg1 = sb("eg1", [P, D])
        eg2 = sb("eg2", [P, D])
        eg3 = sb("eg3", [P, D])
        lg = sb("lg", [P, NT, M])

        rt = [sb(f"rt{i}", [P, NT, M]) for i in range(10)]
        rs = [sb(f"rs{i}", [P, NT]) for i in range(12)]
        wt = sb("wt", [P, 2, NT])
        sidx = sb("sidx", [P, 2, NT], I32)
        gidx = sb("gidx", [P, 2, NT], I32)
        keyw = sb("keyw", [P, M])

        arena = sb("arena", [P, ARENA])
        arena_at = [0]

        def carve(shape, dt=F32, of=None):
            n = 1
            for d in shape[1:]:
                n *= d
            words = n * (2 if dt == BF16 else 4) // 4
            ap = arena[:, arena_at[0]:arena_at[0] + words]
            arena_at[0] += words
            assert arena_at[0] <= ARENA
            if dt != F32:
                ap = ap.bitcast(dt)
            names = "abcd"[:len(shape) - 1]
            if len(names) > 1:
                ap = ap.rearrange(f"p ({' '.join(names)}) -> p {' '.join(names)}",
                                  **dict(zip(names[1:], shape[2:])))
            return ap

        dv = lambda name, shape, dt=F32: carve(shape, dt)

        wqk = dv("wqk", [P, NS, 2, QKL])
        wv = dv("wv", [P, NS, 2, D])
        w2g = dv("w2g", [P, NS, P])
        xin = dv("xin", [P, 4, D])
        xt = dv("xt", [P, 2, 2, P])
        qks = dv("qks", [P, 2, 288])
        vv = dv("vv", [P, 4, D])
        lowt = dv("lowt", [P, 2, P])
        zab = dv("zab", [P, P])
        zex = dv("zex", [P, P])
        zln = dv("zln", [P, P])
        gg = dv("gg", [P, P])
        rp = dv("rp", [P, 132])
        rm = dv("rm", [P, P])
        ee = dv("ee", [P, 4, 264])
        qkt = dv("qkt", [P, 2, 2 * P])
        qbd = dv("qbd", [P, 2, NH, P])
        kt = dv("kt", [P, P])
        am = dv("am", [P, 2, NH, P])
        s0 = dv("s0", [P, 2, HDV])
        s1 = dv("s1", [P, 2, HDV])
        wa = dv("wa", [P, HDV])
        wb = dv("wb", [P, HDV])
        ob = dv("ob", [P, 4, D])

        og = big[:, :].rearrange("p (r k j d) -> p r k j d", r=4, k=2, j=TB)
        arena_at[0] = 0
        hs = dv("hs", [P, TB * NH])
        hl = dv("hl", [P, TB * NH])
        hr = dv("hr", [P, TB * NH])
        on = dv("on", [P, TB, D])
        on2 = dv("on2", [P, TB, D])
        ont = dv("ont", [P, 2, TB * P])
        x1 = dv("x1", [P, 2, TB, D])
        xn2 = dv("xn2", [P, 2, TB, D])
        xn2t = dv("xn2t", [P, 2, TB * P])
        arena_at[0] = 8320 + NT * E
        osh = dv("osh", [P, 3, TB, D])
        oa = dv("oa", [P, TB, D])
        osq = dv("osq", [P, TB, D])

        arena_at[0] = 8320
        l8 = dv("l8", [P, NT, E])
        pr = dv("pr", [P, NT, E])
        p8 = dv("p8", [P, NT, E])
        thr = dv("thr", [P, E], I32)
        bitv = dv("bitv", [P, E], I32)
        cand = dv("cand", [P, E], I32)
        take = dv("take", [P, E], I32)
        cmp = dv("cmp", [P, 2, NT, E], BF16)
        cnt8 = dv("cnt8", [P, E])
        tot = dv("tot", [P, 2, E, NT])
        incl = dv("incl", [P, 2, E, NT])
        pos = dv("pos", [P, 2, NT, E])
        sel = dv("sel", [P, 2, NT, E])
        posi = dv("posi", [P, NT, E], I32)
        hii = dv("hii", [P, NT, E], I32)
        loi = dv("loi", [P, NT, E], I32)
        hif = dv("hif", [P, NT, E])
        lof = dv("lof", [P, NT, E])
        oha = gs[:, :, :].rearrange("p t d -> p (t d)")[:, 0:4096].bitcast(BF16).rearrange(
            "p (n c) -> p n c", c=32)
        ohb = gs[:, :, :].rearrange("p t d -> p (t d)")[:, 4096:8192].bitcast(BF16).rearrange(
            "p (n c) -> p n c", c=32)
        cidx = sb("cidx", [P, 2, P])
        idxc = sb("idxc", [P, 2, 16], I32)
        idxs = sb("idxs", [P, E, JT], I32)

        w_room = [at[:, 16 * h:16 * h + 16, :].rearrange("p t d -> p (t d)") for at in (xres, gs) for h in range(2)]
        w1s = [r[:, 0:2 * F].rearrange("p (k f) -> p k f", k=2) for r in w_room]
        w2s = [r[:, 2 * F:2 * F + FT * D].rearrange("p (f d) -> p f d", f=FT) for r in w_room]
        ht = big[:, :].rearrange("p (r f t) -> p r f t", r=2, f=FT)
        arena_at[0] = 0
        xe = dv("xe", [P, 3, JT, D + E])
        xet = dv("xet", [P, 2, 2, KTOP])
        yb = dv("yb", [P, JT, D])
        ye = dv("ye", [P, 2, JT, D])

        c_step = sem("c_step")
        c_dve = sem("c_dve")
        w_in = sem("w_in")
        w_in2 = sem("w_in2")
        zero_st = sem("zero_st")
        x_in = sems("x_in", 2)
        a_st = sem("a_st"); a_mv = sem("a_mv"); a_lnv = sem("a_lnv"); a_rstd = sem("a_rstd")
        a_xn = sem("a_xn"); xn_st = sem("xn_st")
        a_tp = sem("a_tp"); a_xt = sem("a_xt"); a_g = sem("a_g"); a_eg = sem("a_eg")
        a_lg = sem("a_lg"); a_1 = sem("a_1"); a_2 = sem("a_2"); a_3 = sem("a_3"); a_gs = sem("a_gs")
        r_step = sem("r_step"); r_sub = sem("r_sub"); r_exp = sem("r_exp"); r_rout = sem("r_rout")
        r_suf = sem("r_suf"); r_idx = sem("r_idx"); scat = sem("scat")
        d_in = sems("d_in", 4)
        d_tp = sem("d_tp"); d_xt = sem("d_xt"); d_qk = sem("d_qk"); d_v = sem("d_v")
        d_qks = sem("d_qks"); d_vs = sem("d_vs"); d_lt = sem("d_lt"); d_lts = sem("d_lts"); d_z = sem("d_z")
        d_ab = sem("d_ab"); d_ex = sem("d_ex"); d_ln = sem("d_ln"); d_g = sem("d_g"); d_r = sem("d_r")
        d_rp = sem("d_rp"); d_rm = sem("d_rm"); d_ep = sem("d_ep"); d_em = sem("d_em")
        d_qkt = sem("d_qkt"); d_qT = sem("d_qT"); d_kT = sem("d_kT"); d_qbd = sem("d_qbd"); d_kts = sem("d_kts")
        d_s = sem("d_s"); d_u1 = sem("d_u1"); d_am = sem("d_am")
        d_s0 = sem("d_s0"); d_w0 = sem("d_w0"); d_s1 = sem("d_s1"); d_w1 = sem("d_w1")
        d_o = sem("d_o"); d_ob = sem("d_ob")
        d_st = sems("d_st", 4)
        f_sh = sems("f_sh", 3); f_g = sems("f_g", 4)
        f_a0 = sem("f_a0")
        f_oa = sem("f_oa"); f_sq = sem("f_sq"); f_hs = sem("f_hs"); f_hl = sem("f_hl"); f_hr = sem("f_hr")
        f_on = sem("f_on"); f_on2 = sem("f_on2"); f_tp = sem("f_tp"); f_ont = sem("f_ont")
        f_y = sem("f_y"); f_x1 = sem("f_x1"); out_st = sems("out_st", 2)
        f_st = sem("f_st"); f_mv = sem("f_mv"); f_lnv = sem("f_lnv"); f_rstd = sem("f_rstd")
        f_xn2 = sem("f_xn2"); xp_st = sems("xp_st", 2); f_tp2 = sem("f_tp2"); f_xt2 = sem("f_xt2")
        f_l = sem("f_l"); f_l8 = sem("f_l8")
        s_step = sem("s_step"); s_sub = sem("s_sub"); s_exp = sem("s_exp"); s_p8 = sem("s_p8"); p8_st = sem("p8_st")
        s_cand = sem("s_cand"); s_cmp = sem("s_cmp"); s_cnt = sem("s_cnt"); s_red = sem("s_red")
        s_take = sem("s_take"); s_thr = sem("s_thr"); s_bit = sem("s_bit")
        s_pre = sem("s_pre"); s_tot = sem("s_tot"); s_oh = sem("s_oh"); s_idx = sem("s_idx"); s_idxc = sem("s_idxc")
        idx_st = sem("idx_st"); idx_in = sem("idx_in")
        b1_t = sem("b1_t"); b1_c = sem("b1_c")
        e_w = sems("e_w", NW); e_x = sems("e_x", 3)
        e_tp = sem("e_tp")
        e_xt = sem("e_xt")
        e_h = sem("e_h"); e_gl = sem("e_gl")
        e_y = sem("e_y"); e_yb = sem("e_yb"); e_ye = sem("e_ye")
        e_st = sem("e_st")

        block = ctx.enter_context(nc.Block())

        @block.gpsimd
        def _(pool):
            done = [0]

            def step(ins):
                done[0] += 1
                ins.then_inc(c_step, 1)
                pool.wait_ge(c_step, done[0])

            def select(ap, pattern, base, mult, op=ALU.is_ge, fill=0.0):
                step(nc.gpsimd.affine_select(out=ap, in_=ap, compare_op=op, fill=fill, base=base,
                                             pattern=pattern, channel_multiplier=mult))

            step(nc.gpsimd.memset(zeros[:, :], 0.0))
            step(nc.gpsimd.memset(ident[:, :], 0.0))
            select(ident[:, :], [[-1, P]], 0, 1, ALU.not_equal, 1.0)
            step(nc.gpsimd.memset(epst[:, :], EPS))
            step(nc.gpsimd.memset(ones[:, :], 1.0))
            step(nc.gpsimd.memset(ones_bf[:, :], 1.0))
            step(nc.gpsimd.memset(after[:, :], 1.0))
            select(after[:, :], [[-1, P]], -1, 1)
            step(nc.gpsimd.memset(before_bf[:, :], 1.0))
            select(before_bf[:, :], [[1, P]], -1, -1)
            for j in range(P // 32):
                blk = relm[:, 32 * j:32 * j + 32]
                step(nc.gpsimd.memset(blk, (1.0 if j % 2 else -1.0) / GN))
                select(blk, [[0, 32]], -32 * j, 1)
                select(blk, [[0, 32]], 32 * j + 31, -1)
                if j % 2:
                    select(blk, [[1, 32]], 32 * j, -1)
                else:
                    select(blk, [[-1, 32]], -32 * j - 1, 1)
            step(nc.gpsimd.memset(spanm[:, :], 0.0))
            for c, (lo, hi) in enumerate(((0, 32), (32, 96), (96, 128))):
                step(nc.gpsimd.memset(spanm[:, c:c + 1], 1.0 / GN))
                select(spanm[:, c:c + 1], [[0, 1]], -lo, 1)
                select(spanm[:, c:c + 1], [[0, 1]], hi - 1, -1)
            step(nc.gpsimd.memset(headm[:, :, :], float(HDK) ** -0.5))
            select(headm[:, :, :], [[-HDK, NH], [0, P]], 0, 1)
            select(headm[:, :, :], [[HDK, NH], [0, P]], HDK - 1, -1)
            step(nc.gpsimd.memset(causal[:, :], 1.0))
            for c in range(2):
                select(causal[CH * c:CH * c + CH, :], [[1, CH]], 0, -1)
            for h in range(2):
                step(nc.gpsimd.iota(ibuf[:, HALF_B * h:HALF_B * h + HALF_B, :, :],
                                    pattern=[[M * CAP, HALF_B], [0, TB], [CAP, M]],
                                    base=CAP - 1, channel_multiplier=0))
            step(nc.gpsimd.tensor_copy(lastrow[:, :, :, :], ibuf[:, :, :, :]))
            ib = ibuf[:, :, :, :].rearrange("p a b c -> p (a b c)")
            step(nc.gpsimd.iota(ib[:, 0:32], pattern=[[1, 32]], base=0, channel_multiplier=0))
            step(nc.gpsimd.tensor_copy(i32f[:, :], ib[:, 0:32]))
            step(nc.gpsimd.iota(ib[:, 32:33], pattern=[[0, 1]], base=0, channel_multiplier=1))
            step(nc.gpsimd.tensor_copy(pidx[:, :], ib[:, 32:33]))
            step(nc.gpsimd.memset(scanm[:, :, :, :], 1.0))
            step(nc.gpsimd.memset(scanm[:, :, :, 0:1], 0.0))
            for m in range(M):
                step(nc.gpsimd.memset(keyw[:, m:m + 1], float(M - m)))
            step(nc.gpsimd.memset(qks[:, :, QKL:288], 0.0))
            step(nc.gpsimd.memset(qks[:, :, QKL:QKL + 1], 1.0))
            step(nc.gpsimd.memset(am[:, :, :, :], 0.0))
            assert done[0] == CONST_STEPS, done[0]

            pool.wait_ge(r_idx, 4)
            pool.wait_ge(zero_st, 16 * 4)
            for t in range(NT):
                for k in range(2):
                    nc.gpsimd.indirect_dma_start(
                        x_c, bass.IndirectOffsetOnAxis(sidx[:, k, t:t + 1], 0), xn[:, t, :], None,
                        bounds_check=ROWS - 1, oob_is_err=False).then_inc(scat, 16)

            for b in range(B):
                if b % HALF_B == 0:
                    for r in range(4):
                        pool.wait_ge(d_st[r], 16 * (NU_SH + (NU - NU_SH) // 2 * (b // HALF_B + 1)) // 4)
                if b >= 4:
                    pool.wait_ge(f_oa, b - 3)
                for j in range(TB):
                    for k in range(2):
                        t = b * TB + j
                        nc.gpsimd.indirect_dma_start(
                            og[:, b % 4, k, j, :], None, o_m[b // HALF_B],
                            bass.IndirectOffsetOnAxis(gidx[:, k, t:t + 1], 0),
                            bounds_check=HALF_ROWS - 1, oob_is_err=False).then_inc(f_g[b % 4], 16)

            pool.wait_ge(idx_in, 16)
            pool.wait_ge(p8_st, 16)
            for r in range(2):
                pool.wait_ge(xp_st[r], 16 * B // 2)
                pool.wait_ge(out_st[r], 16 * B // 2)

            def gather(e):
                if e >= 3:
                    pool.wait_ge(e_tp, 2 * (e - 2))
                    pool.wait_ge(e_ye, JT * (e - 2))
                for j in range(JT):
                    nc.gpsimd.indirect_dma_start(
                        xe[:, e % 3, j, :], None, x_p, bass.IndirectOffsetOnAxis(idxs[:, e, j:j + 1], 0),
                        bounds_check=B * S - 1, oob_is_err=False).then_inc(e_x[e % 3], 16)

            gather(0)
            gather(1)
            gather(2)
            for e in range(E):
                if e:
                    pool.wait_ge(e_st, 16 * JT * e)
                for j in range(JT):
                    pool.wait_ge(e_ye, JT * e + j + 1)
                    nc.gpsimd.indirect_dma_start(
                        outf, bass.IndirectOffsetOnAxis(idxs[:, e, j:j + 1], 0), ye[:, e % 2, j, :], None,
                        bounds_check=B * S - 1, oob_is_err=True, compute_op=ALU.add).then_inc(e_st, 16)
                if e + 3 < E:
                    gather(e + 3)
            pool.wait_ge(e_st, 16 * JT * E)

        @block.sync
        def _(sp):
            def load_x(b):
                if b >= 2:
                    sp.wait_ge(x_in[b % 2], 16 * (b // 2))
                sp.dma_start(xres[:, TB * b:TB * b + TB, :],
                             xf[S * b:S * b + S, :].rearrange("(t p) d -> p t d", p=P)).then_inc(x_in[b % 2], 16)

            for b in range(B):
                load_x(b)
            with sp.Fori(0, B) as b:
                sp.wait_ge(a_xn, b * TB + TB)
                sp.dma_start(x_c[bass.ds(b * S, S), :].rearrange("(t p) d -> p t d", p=P),
                             xn[:, bass.ds(b * TB, TB), :]).then_inc(xn_st, 16)
            sp.wait_ge(xn_st, 16 * B)

            def slot(unit):
                u = unit(0)
                if u:
                    if u.c == NU_SH:
                        sp.wait_ge(scat, 16 * 2 * NT)
                    if u.c >= 4:
                        sp.wait_ge(d_tp, u.n - 3)
                    sp.dma_start(xin[:, u.r4, :], x_c[bass.ds(u.n * P, P), :]).then_inc(d_in[u.r4], 16)
                u = unit(7)
                if u:
                    sp.wait_ge(d_ob, u.n + 1)
                    to, first = (o_s, 0) if u.stream == SHARED else (o_m[u.half], NU_SH * P + u.half * HALF_ROWS)
                    sp.dma_start(to[bass.ds(u.n * P - first, P), :], ob[:, u.r4, :]).then_inc(d_st[u.r4], 16)

            unit_slots(sp, slot, NU + 6, peeled=HALF_B - 1)

            for r in range(4):
                sp.wait_ge(d_st[r], 16 * (NU // 4))

            def load_osh(b):
                if b >= 3:
                    sp.wait_ge(f_oa, b - 2)
                sp.dma_start(osh[:, b % 3, :, :], o_s[S * b:S * b + S, :].rearrange("(t p) d -> p t d", p=P))\
                    .then_inc(f_sh[b % 3], 16)

            load_osh(0)
            load_osh(1)
            for b in range(B):
                if b + 2 < B:
                    load_osh(b + 2)
                sp.wait_ge(f_x1, 2 * b + 2)
                sp.dma_start(outf[S * b:S * b + S, :].rearrange("(t p) d -> p t d", p=P), x1[:, b % 2, :, :])\
                    .then_inc(out_st[b % 2], 16)
                sp.wait_ge(f_xn2, TB * b + TB)
                sp.dma_start(x_p[S * b:S * b + S, 0:D].rearrange("(t p) d -> p t d", p=P), xn2[:, b % 2, :, :])\
                    .then_inc(xp_st[b % 2], 16)

            def load_w(e):
                if e == 2:
                    sp.wait_ge(s_idx, 1)
                if e >= NW:
                    sp.wait_ge(e_y, JT * (e - NW + 1))
                sp.dma_start(w1s[e % NW], W1[e].rearrange("(k p) f -> p k f", p=P)).then_inc(e_w[e % NW], 16)
                sp.dma_start(w2s[e % NW], W2[e].rearrange("(f p) d -> p f d", p=P)).then_inc(e_w[e % NW], 16)

            load_w(0)
            load_w(1)
            sp.wait_ge(s_p8, 1)
            sp.dma_start(x_p[:, D:D + E].rearrange("(t p) e -> p t e", p=P), p8[:, :, :],
                         allow_slow_non_contiguous=True).then_inc(p8_st, 16)
            sp.wait_ge(s_idxc, 4)
            for g in range(2):
                sp.dma_start(idx_d[4 * g:4 * g + 4, :].rearrange("e (a c) -> (e a) c", a=32), idxc[:, g, :])\
                    .then_inc(idx_st, 16)
            sp.wait_ge(idx_st, 32)
            sp.dma_start(idxs[:, :, :], idx_d.rearrange("e (p j) -> p e j", p=P),
                         allow_slow_non_contiguous=True).then_inc(idx_in, 16)
            for e in range(2, E):
                load_w(e)

        @block.scalar
        def _(act):
            act.preload_act_table_set("natural_log_exp_and_others")
            kp = lambda w: w.rearrange("(k p) n -> p k n", p=P)
            for m in range(NS):
                wk, wvm, wl, w2, bb = ((w_ks, w_vs, w_gk1s, w_gk2s, b_gks) if m == SHARED else
                                       (w_k[m], w_v[m], w_gk1[m], w_gk2[m], b_gk[m]))
                act.dma_start(wqk[:, m, :, 0:P], kp(w_q)).then_inc(w_in, 16)
                act.dma_start(wqk[:, m, :, P:2 * P], kp(wk)).then_inc(w_in, 16)
                act.dma_start(wqk[:, m, :, 2 * P:QKL], kp(wl)).then_inc(w_in, 16)
                act.dma_start(wv[:, m, :, :], kp(wvm)).then_inc(w_in, 16)
                act.dma_start(w2g[0:LOW, m, :], w2).then_inc(w_in, 16)
                act.dma_start(w2g[LOW:LOW + 1, m, :], bb.rearrange("(a n) -> a n", a=1)).then_inc(w_in, 16)
            act.dma_start(wgg[:, :, 0:D], kp(w_g)).then_inc(w_in, 16)
            act.dma_start(wgg[:, :, D:D + M], kp(w_gate)).then_inc(w_in, 16)
            act.dma_start(nwb[:, :].rearrange("p (h v) -> p h v", h=NH),
                          norm_w.rearrange("(a b n) -> a b n", a=1, b=1).to_broadcast([P, NH, HDV]))\
                .then_inc(w_in, 16)
            act.dma_start(wo[:, :, :], kp(w_o)).then_inc(w_in2, 16)
            act.dma_start(wsb[:, :, :], kp(Ws)).then_inc(w_in2, 16)
            act.dma_start(bsb[:, :], bs.rearrange("(a n) -> a n", a=1).to_broadcast([P, E])).then_inc(w_in2, 16)
            act.dma_start(b1r[:, :], b1.rearrange("e (f p) -> (e f) p", p=P)).then_inc(w_in2, 16)
            act.dma_start(b2b[:, :, :], b2.rearrange("(a e) n -> a e n", a=1).to_broadcast([P, E, D]))\
                .then_inc(w_in2, 16)
            act.wait_ge(c_step, 1)
            for q in range(4):
                act.dma_start(x_c[NU_SH * P + 2048 * q:NU_SH * P + 2048 * q + 2048, :]
                              .rearrange("(p a) d -> p (a d)", p=P).rearrange("p (c d) -> p c d", c=2),
                              zeros[:, :].unsqueeze(1).to_broadcast([P, 2, 2048])).then_inc(zero_st, 16)
            act.wait_ge(c_step, CONST_STEPS)

            def a_slot(b_std, b_tile):
                if b_std is not None:
                    act.wait_ge(a_mv, b_std * TB + TB)
                    nc.scalar.activation(lnv[:, :], mv[:, :, 1], ACT.Ln, bias=epst[:, 0:1]).then_inc(a_lnv, 1)
                    act.wait_ge(a_lnv, b_std + 1)
                    nc.scalar.activation(rstd[:, :], lnv[:, :], ACT.Exp, scale=-0.5).then_inc(a_rstd, 1)
                if b_tile is not None:
                    for j in range(TB):
                        t = b_tile * TB + j
                        act.wait_ge(a_tp, t + 1)
                        nc.scalar.activation(xta[:, j % 2, :, :], bank[j % 2][:, 0:D].rearrange("p (k t) -> p k t", k=2),
                                             ACT.Copy).then_inc(a_xt, 1)
                        act.wait_ge(a_g, t + 1)
                        nc.scalar.activation(eg[:, j % 2, :], bank[2 + j % 2][:, 0:D], ACT.Exp, scale=-1.0)\
                            .then_inc(a_eg, 1)

            a_slot(0, None)
            with act.Fori(1, B) as b:
                a_slot(b, b - 1)
            a_slot(None, B - 1)
            act.wait_ge(r_sub, 1)
            nc.scalar.activation(rt[1][:, :, :], rt[0][:, :, :], ACT.Exp).then_inc(r_exp, 1)

            def slot(unit):
                u = unit(0)
                if u:
                    act.wait_ge(d_tp, u.n + 1)
                    if u.c >= 2:
                        act.wait_ge(d_v, u.n - 1)
                    nc.scalar.activation(xt[:, u.r2, :, :], bank[0][:, 0:D].rearrange("p (k t) -> p k t", k=2),
                                         ACT.Copy).then_inc(d_xt, 1)
                u = unit(2)
                if u:
                    act.wait_ge(d_z, u.n + 1)
                    nc.scalar.activation(zab[:, :], bank[3][:, 0:P], ACT.Abs).then_inc(d_ab, 1)
                    act.wait_ge(d_ab, u.n + 1)
                    nc.scalar.activation(zex[:, :], zab[:, :], ACT.Exp, scale=-1.0).then_inc(d_ex, 1)
                    act.wait_ge(d_ex, u.n + 1)
                    if u.c >= 1:
                        act.wait_ge(d_g, u.n)
                    nc.scalar.activation(zln[:, :], zex[:, :], ACT.Ln, bias=1.0).then_inc(d_ln, 1)
                u = unit(1)
                if u:
                    act.wait_ge(d_qk, u.n + 1)
                    if u.c >= 2:
                        act.wait_ge(d_qkt, u.n - 1)
                    nc.scalar.activation(qks[:, u.r2, 0:QKL], bank[1][:, 0:QKL], ACT.Copy).then_inc(d_qks, 1)
                    act.wait_ge(d_v, u.n + 1)
                    if u.c >= 4:
                        act.wait_ge(d_o, u.n - 3)
                    nc.scalar.activation(vv[:, u.r4, :], bank[2][:, 0:D], ACT.Copy).then_inc(d_vs, 1)
                u = unit(3)
                if u:
                    act.wait_ge(d_kT, u.n + 1)
                    if u.c >= 1:
                        act.wait_ge(d_u1, u.n)
                    nc.scalar.activation(kt[:, :], bank[0][:, 0:P], ACT.Copy).then_inc(d_kts, 1)
                u = unit(2)
                if u:
                    act.wait_ge(d_rp, u.n + 1)
                    if u.c >= 4:
                        act.wait_ge(d_w1, u.n - 2)
                        act.wait_ge(d_qkt, u.n - 3)
                    nc.scalar.activation(ee[:, u.r4, 0:132], rp[:, :], ACT.Exp).then_inc(d_ep, 1)
                    act.wait_ge(d_rm, u.n + 1)
                    nc.scalar.activation(ee[:, u.r4, 132:260], rm[:, :], ACT.Exp, scale=-1.0).then_inc(d_em, 1)
                u = unit(1)
                if u:
                    act.wait_ge(d_lt, u.n + 1)
                    if u.c >= 2:
                        act.wait_ge(d_z, u.n - 1)
                    nc.scalar.activation(lowt[0:32, u.r2, :], bank[3][0:32, P:2 * P], ACT.Copy).then_inc(d_lts, 1)

            unit_slots(act, slot, NU + 3)

            def squares(b):
                act.wait_ge(f_oa, b + 1)
                nc.scalar.activation(osq[:, :, :], oa[:, :, :], ACT.Square).then_inc(f_sq, 1)

            def head_rstd(b):
                act.wait_ge(f_hs, b + 1)
                nc.scalar.activation(hl[:, :], hs[:, :], ACT.Ln, bias=epst[:, 0:1], scale=1.0 / HDV)\
                    .then_inc(f_hl, 1)
                act.wait_ge(f_hl, b + 1)
                nc.scalar.activation(hr[:, :], hl[:, :], ACT.Exp, scale=-0.5).then_inc(f_hr, 1)

            def row_rstd(b):
                act.wait_ge(f_mv, b * TB + TB)
                nc.scalar.activation(lnv[:, :], mv[:, :, 1], ACT.Ln, bias=epst[:, 0:1]).then_inc(f_lnv, 1)
                act.wait_ge(f_lnv, b + 1)
                nc.scalar.activation(rstd[:, :], lnv[:, :], ACT.Exp, scale=-0.5).then_inc(f_rstd, 1)

            def out_t(b):
                for k in range(2):
                    act.wait_ge(f_tp, 2 * b + k + 1)
                    nc.scalar.activation(ont[:, k, :], bank[k][:, :], ACT.Copy).then_inc(f_ont, 1)

            def norm_t(b):
                for k in range(2):
                    act.wait_ge(f_tp2, 2 * b + k + 1)
                    nc.scalar.activation(xn2t[:, k, :], bank[4 + k][:, :], ACT.Copy).then_inc(f_xt2, 1)

            for b in range(B + 1):
                if b < B:
                    squares(b)
                    head_rstd(b)
                if b >= 1:
                    row_rstd(b - 1)
                if b < B:
                    out_t(b)
                if b >= 1:
                    norm_t(b - 1)
            act.wait_ge(s_sub, 1)
            nc.scalar.activation(pr[:, :, :], l8[:, :, :], ACT.Exp).then_inc(s_exp, 1)

            act.wait_ge(b1_t, 1)
            nc.scalar.activation(b1c[:, :], bank[7][:, 0:E * FT], ACT.Copy).then_inc(b1_c, 1)
            act.wait_ge(b1_c, 1)

            def rows_t(e, r):
                for k in range(2):
                    act.wait_ge(e_tp, 2 * e + k + 1)
                    nc.scalar.activation(xet[:, r, k, :], bank[k][:, :], ACT.Copy).then_inc(e_xt, 1)

            def e_slot(e, r, first, last, col):
                if not first:
                    act.wait_ge(e_y, JT * (e - 1))
                for f in range(FT):
                    act.wait_ge(e_h, FT * e + f + 1)
                    nc.scalar.activation(ht[:, r, f, :], bank[2 + f % 4][:, :], ACT.Gelu_apprx_tanh,
                                         bias=b1c[:, col(f)]).then_inc(e_gl, 1)
                    if f == 3 and not last:
                        rows_t(e + 1, 1 - r)

            rows_t(0, 0)
            for e in range(E):
                e_slot(e, e % 2, e < 2, e == E - 1, lambda f: slice(e * FT + f, e * FT + f + 1))

        @block.vector
        def _(dve):
            dve.wait_ge(c_step, CONST_STEPS)

            def norm_tiles(src, dst, b, st_sem, mv_sem, rs_sem, xn_sem):
                for j in range(TB):
                    nc.vector.bn_stats(st6[:, j, :], src(j)).then_inc(st_sem, 1)
                dve.wait_ge(st_sem, b * TB + TB)
                nc.vector.memset(held[:, :], 0.0)
                for j in range(TB):
                    nc.vector.bn_aggr(mv[:, j, :], st6[:, j, :]).then_inc(mv_sem, 1)
                dve.wait_ge(rs_sem, b + 1)
                for j in range(TB):
                    nc.vector.tensor_scalar(dst(j), src(j), mv[:, j, 0:1], rstd[:, j:j + 1],
                                            ALU.subtract, ALU.mult).then_inc(xn_sem, 1)

            def gate_tiles(b):
                for j in range(TB):
                    t = b * TB + j
                    pg = bank[2 + j % 2]
                    dve.wait_ge(a_eg, t + 1)
                    nc.vector.tensor_copy(lg[:, t, :], pg[:, D:D + M]).then_inc(a_lg, 1)
                    dve.wait_ge(a_2, t) if (not isinstance(b, int) or t) else None
                    nc.vector.tensor_scalar(eg1[:, :], eg[:, j % 2, :], 1.0, None, ALU.add).then_inc(a_1, 1)
                    dve.wait_ge(a_1, t + 1)
                    nc.vector.reciprocal(eg2[:, :], eg1[:, :]).then_inc(a_2, 1)
                    dve.wait_ge(a_2, t + 1)
                    nc.vector.tensor_tensor(eg3[:, :], pg[:, 0:D], eg2[:, :], ALU.mult).then_inc(a_3, 1)
                    dve.wait_ge(a_3, t + 1)
                    nc.vector.tensor_tensor(gs[:, t, :], eg3[:, :], nwb[:, :], ALU.mult).then_inc(a_gs, 1)

            def load_wait(r, n):
                dve.wait_ge(x_in[r], 16 * n)

            def norm_a(b):
                norm_tiles(lambda j: xres[:, b * TB + j, :], lambda j: xn[:, b * TB + j, :], b,
                           a_st, a_mv, a_rstd, a_xn)

            load_wait(0, 1)
            norm_a(0)
            dve.wait_ge(w_in, 16 * W_IN)
            load_wait(1, 1)
            norm_a(1)
            gate_tiles(0)
            with dve.Fori(1, B // 2) as i:
                load_wait(0, i + 1)
                norm_a(i * 2)
                gate_tiles(i * 2 - 1)
                load_wait(1, i + 1)
                norm_a(i * 2 + 1)
                gate_tiles(i * 2)
            gate_tiles(B - 1)

            done = [0]

            def step(ins):
                done[0] += 1
                ins.then_inc(r_step, 1)
                dve.wait_ge(r_step, done[0])

            per_m = lambda a: a.unsqueeze(2).to_broadcast([P, NT, M])
            dve.wait_ge(a_lg, NT)
            step(nc.vector.tensor_reduce(rs[0][:, :], lg[:, :, :], AX.X, ALU.max))
            nc.vector.tensor_tensor(rt[0][:, :, :], lg[:, :, :], per_m(rs[0][:, :]), ALU.subtract).then_inc(r_sub, 1)
            dve.wait_ge(r_exp, 1)
            step(nc.vector.tensor_reduce(rs[1][:, :], rt[1][:, :, :], AX.X, ALU.add))
            step(nc.vector.reciprocal(rs[2][:, :], rs[1][:, :]))
            step(nc.vector.tensor_tensor(rt[2][:, :, :], rt[1][:, :, :], per_m(rs[2][:, :]), ALU.mult))
            prob, value = rt[2], [rs[3], rs[4]]
            pick = [rt[4], rt[5]]
            keyb = keyw[:, :].unsqueeze(1).to_broadcast([P, NT, M])
            for k in range(2):
                step(nc.vector.tensor_reduce(value[k][:, :], prob[:, :, :], AX.X, ALU.max))
                step(nc.vector.tensor_tensor(rt[3][:, :, :], prob[:, :, :], per_m(value[k][:, :]), ALU.is_equal))
                step(nc.vector.tensor_tensor(rt[6][:, :, :], rt[3][:, :, :], keyb, ALU.mult))
                step(nc.vector.tensor_reduce(rs[5][:, :], rt[6][:, :, :], AX.X, ALU.max))
                step(nc.vector.tensor_tensor(pick[k][:, :, :], rt[6][:, :, :], per_m(rs[5][:, :]), ALU.is_equal))
                if k == 0:
                    step(nc.vector.scalar_tensor_tensor(rt[7][:, :, :], pick[0][:, :, :], -4.0, prob[:, :, :],
                                                        ALU.mult, ALU.add))
                    prob = rt[7]
            nc.vector.tensor_tensor(rt[8][:, :, :], pick[0][:, :, :], pick[1][:, :, :], ALU.add).then_inc(r_rout, 1)
            step(nc.vector.tensor_tensor(rs[6][:, :], value[0][:, :], value[1][:, :], ALU.add))
            step(nc.vector.reciprocal(rs[7][:, :], rs[6][:, :]))
            dve.wait_ge(r_suf, 1)
            suf = bank[4][:, 0:NT * M].rearrange("p (t m) -> p t m", m=M)
            step(nc.vector.tensor_scalar(rt[0][:, :, :], suf, float(CAP - 1), None, ALU.is_le))
            lastr = lastrow[:, :, :, :].rearrange("p b j m -> p (b j) m")
            step(nc.vector.tensor_tensor(rt[1][:, :, :], lastr, suf, ALU.subtract))
            for k in range(2):
                step(nc.vector.tensor_tensor(rt[2][:, :, :], pick[k][:, :, :], rt[0][:, :, :], ALU.mult))
                step(nc.vector.tensor_reduce(rs[8][:, :], rt[2][:, :, :], AX.X, ALU.add))
                step(nc.vector.tensor_tensor(rt[3][:, :, :], rt[2][:, :, :], rt[1][:, :, :], ALU.mult))
                step(nc.vector.tensor_reduce(rs[9][:, :], rt[3][:, :, :], AX.X, ALU.add))
                step(nc.vector.tensor_tensor(rs[10][:, :], value[k][:, :], rs[7][:, :], ALU.mult))
                step(nc.vector.tensor_tensor(wt[:, k, :], rs[10][:, :], rs[8][:, :], ALU.mult))
                nc.vector.tensor_copy(gidx[:, k, :], rs[9][:, :]).then_inc(r_idx, 1)
                for h in range(2):
                    tiles = slice(NT // 2 * h, NT // 2 * h + NT // 2)
                    step(nc.vector.tensor_scalar(rs[10][:, tiles], rs[8][:, tiles], -OUT_OF_RANGE,
                                                 OUT_OF_RANGE + NU_SH * P + HALF_ROWS * h, ALU.mult, ALU.add))
                step(nc.vector.tensor_tensor(rs[11][:, :], rs[10][:, :], rs[9][:, :], ALU.add))
                nc.vector.tensor_copy(sidx[:, k, :], rs[11][:, :]).then_inc(r_idx, 1)

            def slot(unit):
                u = unit(2)
                if u:
                    dve.wait_ge(d_ln, u.n + 1)
                    if u.c >= 1:
                        dve.wait_ge(d_r, u.n)
                    nc.vector.scalar_tensor_tensor(gg[:, :], bank[3][:, 0:P], 0.0, zln[:, :],
                                                   ALU.min, ALU.subtract).then_inc(d_g, 1)
                u = unit(3)
                if u:
                    dve.wait_ge(d_qT, u.n + 1)
                    if u.c >= 2:
                        dve.wait_ge(d_o, u.n - 1)
                    nc.vector.tensor_tensor(qbd[:, u.r2, :, :],
                                            bank[5][:, 0:P].unsqueeze(1).to_broadcast([P, NH, P]),
                                            headm[:, :, :], ALU.mult).then_inc(d_qbd, 1)
                u = unit(2)
                if u:
                    dve.wait_ge(d_r, u.n + 1)
                    if u.c >= 1:
                        dve.wait_ge(d_ep, u.n)
                        dve.wait_ge(d_em, u.n)
                    nc.vector.tensor_scalar(rp[:, :], bank[4][:, 0:132], EXP_LIM, None, ALU.min).then_inc(d_rp, 1)
                    dve.wait_ge(d_rp, u.n + 1)
                    nc.vector.tensor_scalar(rm[:, :], rp[:, 0:P], -EXP_LIM, None, ALU.max).then_inc(d_rm, 1)
                    dve.wait_ge(d_em, u.n + 1)
                    dve.wait_ge(d_qks, u.n + 1)
                    if u.c >= 2:
                        dve.wait_ge(d_u1, u.n - 1)
                    nc.vector.tensor_tensor(
                        qkt[:, u.r2, :].rearrange("p (a c) -> p a c", a=2),
                        qks[:, u.r2, 0:2 * P].rearrange("p (a c) -> p a c", a=2),
                        ee[:, u.r4, :].rearrange("p (a c) -> p a c", a=2)[:, :, 0:P], ALU.mult).then_inc(d_qkt, 1)
                u = unit(4)
                if u:
                    dve.wait_ge(d_o, u.n + 1)
                    if u.c >= 4:
                        dve.wait_ge(d_st[u.r4], u.quad * 16)
                    nc.vector.tensor_copy(ob[:, u.r4, :], bank[7][:, 0:D]).then_inc(d_ob, 1)
                u = unit(3)
                if u:
                    dve.wait_ge(d_s, u.n + 1)
                    for c in range(2):
                        for lo, t0, t1 in HALVES:
                            h = slice(CH * c, CH * c + lo)
                            ins = nc.vector.tensor_tensor(
                                am[h, u.r2, :, CH * c + t0:CH * c + t1],
                                bank[6][h, 0:NH * CH].rearrange("p (h t) -> p h t", h=NH)[:, :, t0:t1],
                                causal[h, t0:t1].unsqueeze(1).to_broadcast([lo, NH, t1 - t0]), ALU.mult)
                    ins.then_inc(d_am, 1)
                    if u.first:
                        nc.vector.memset(s0[:, u.r2, :], 0.0).then_inc(d_s0, 1)
                    else:
                        dve.wait_ge(d_w1, u.n)
                        dve.wait_ge(d_ep, u.n + 1)
                        nc.vector.tensor_scalar(s0[:, u.r2, :], wb[:, :], ee[:, u.r4, P:P + 1],
                                                ee[:, (u.r4 - 1) % 4, P + 2:P + 3], ALU.mult, ALU.mult)\
                            .then_inc(d_s0, 1)
                    dve.wait_ge(d_s0, u.n + 1)
                    nc.vector.tensor_tensor(wa[:, :], bank[6][:, 256:256 + HDV], s0[:, u.r2, :], ALU.add)\
                        .then_inc(d_w0, 1)
                    dve.wait_ge(d_w0, u.n + 1)
                    nc.vector.tensor_scalar(s1[:, u.r2, :], wa[:, :], ee[:, u.r4, P + 1:P + 2], None, ALU.mult)\
                        .then_inc(d_s1, 1)
                    dve.wait_ge(d_s1, u.n + 1)
                    dve.wait_ge(d_u1, u.n + 1)
                    nc.vector.tensor_tensor(wb[:, :], bank[5][:, 256:256 + HDV], s1[:, u.r2, :], ALU.add)\
                        .then_inc(d_w1, 1)

            unit_slots(dve, slot, NU + 3)

            def combine(b):
                dve.wait_ge(f_sh[b % 3], 16 * (b // 3 + 1))
                dve.wait_ge(f_g[b % 4], 16 * 2 * TB * (b // 4 + 1))
                if b:
                    dve.wait_ge(f_sq, b)
                    dve.wait_ge(f_on, b)
                for j in range(TB):
                    t = b * TB + j
                    nc.vector.scalar_tensor_tensor(oa[:, j, :], og[:, b % 4, 0, j, :], wt[:, 0, t:t + 1],
                                                   osh[:, b % 3, j, :], ALU.mult, ALU.add).then_inc(f_a0, 1)
                for j in range(TB):
                    t = b * TB + j
                    dve.wait_ge(f_a0, t + 1)
                    ins = nc.vector.scalar_tensor_tensor(oa[:, j, :], og[:, b % 4, 1, j, :], wt[:, 1, t:t + 1],
                                                         oa[:, j, :], ALU.mult, ALU.add)
                ins.then_inc(f_oa, 1)

            def head_squares(b):
                dve.wait_ge(f_sq, b + 1)
                nc.vector.tensor_reduce(hs[:, :], osq[:, :, :].rearrange("p j (h v) -> p (j h) v", h=NH),
                                        AX.X, ALU.add).then_inc(f_hs, 1)

            def gated(b):
                dve.wait_ge(f_hr, b + 1)
                nc.vector.tensor_tensor(on[:, :, :].rearrange("p j (h v) -> p (j h) v", h=NH),
                                        oa[:, :, :].rearrange("p j (h v) -> p (j h) v", h=NH),
                                        hr[:, :].unsqueeze(2).to_broadcast([P, TB * NH, HDV]), ALU.mult)\
                    .then_inc(f_on, 1)
                dve.wait_ge(f_on, b + 1)
                if b:
                    dve.wait_ge(f_tp, 2 * b)
                nc.vector.tensor_tensor(on2[:, :, :], on[:, :, :], gs[:, b * TB:b * TB + TB, :], ALU.mult)\
                    .then_inc(f_on2, 1)

            def residual(b):
                if b >= 2:
                    dve.wait_ge(out_st[b % 2], 16 * (b // 2))
                for q in range(2):
                    dve.wait_ge(f_y, 2 * b + q + 1)
                    nc.vector.tensor_tensor(x1[:, b % 2, 2 * q:2 * q + 2, :],
                                            bank[2 + q][:, :].rearrange("p (j d) -> p j d", j=2),
                                            xres[:, b * TB + 2 * q:b * TB + 2 * q + 2, :], ALU.add).then_inc(f_x1, 1)
                dve.wait_ge(f_x1, 2 * b + 2)
                for j in range(TB):
                    nc.vector.bn_stats(st6[:, j, :], x1[:, b % 2, j, :]).then_inc(f_st, 1)
                dve.wait_ge(f_st, b * TB + TB)
                for j in range(TB):
                    nc.vector.bn_aggr(mv[:, j, :], st6[:, j, :]).then_inc(f_mv, 1)

            def norm2(b):
                dve.wait_ge(f_rstd, b + 1)
                if b >= 2:
                    dve.wait_ge(xp_st[b % 2], 16 * (b // 2))
                for j in range(TB):
                    nc.vector.tensor_scalar(xn2[:, b % 2, j, :], x1[:, b % 2, j, :], mv[:, j, 0:1],
                                            rstd[:, j:j + 1], ALU.subtract, ALU.mult).then_inc(f_xn2, 1)

            def router(b):
                dve.wait_ge(f_l, b + 1)
                nc.vector.tensor_tensor(l8[:, b * TB:b * TB + TB, :],
                                        bank[6][:, 0:TB * E].rearrange("p (j e) -> p j e", e=E),
                                        bsb[:, :].unsqueeze(1).to_broadcast([P, TB, E]), ALU.add).then_inc(f_l8, 1)

            dve.wait_ge(w_in2, 16 * 5)
            for b in range(B + 2):
                if b < B:
                    combine(b)
                if b >= 2:
                    router(b - 2)
                if b < B:
                    head_squares(b)
                if 1 <= b <= B:
                    residual(b - 1)
                if b < B:
                    gated(b)
                if 1 <= b <= B:
                    norm2(b - 1)

            done[0] = 0

            def sstep(ins):
                done[0] += 1
                ins.then_inc(s_step, 1)
                dve.wait_ge(s_step, done[0])

            per_e = lambda a: a.unsqueeze(2).to_broadcast([P, NT, E])
            dve.wait_ge(f_l8, B)
            sstep(nc.vector.tensor_reduce(rs[0][:, :], l8[:, :, :], AX.X, ALU.max))
            nc.vector.tensor_tensor(l8[:, :, :], l8[:, :, :], per_e(rs[0][:, :]), ALU.subtract).then_inc(s_sub, 1)
            dve.wait_ge(s_exp, 1)
            sstep(nc.vector.tensor_reduce(rs[1][:, :], pr[:, :, :], AX.X, ALU.add))
            sstep(nc.vector.reciprocal(rs[2][:, :], rs[1][:, :]))
            nc.vector.tensor_tensor(p8[:, :, :], pr[:, :, :], per_e(rs[2][:, :]), ALU.mult).then_inc(s_p8, 1)

            nc.vector.memset(thr[:, :], 0).then_inc(s_thr, 1)
            nc.vector.memset(bitv[:, :], 1 << 29).then_inc(s_bit, 1)
            dve.wait_ge(s_p8, 1)
            with dve.Fori(0, 30) as i:
                dve.wait_ge(s_thr, i + 1)
                dve.wait_ge(s_bit, i + 1)
                nc.vector.tensor_tensor(cand[:, :], thr[:, :], bitv[:, :], ALU.bitwise_or).then_inc(s_cand, 1)
                dve.wait_ge(s_cand, i + 1)
                nc.vector.tensor_tensor(cmp[:, 0, :, :], p8[:, :, :],
                                        cand[:, :].bitcast(F32).unsqueeze(1).to_broadcast([P, NT, E]), ALU.is_ge)\
                    .then_inc(s_cmp, 1)
                dve.wait_ge(s_cnt, i + 1)
                nc.vector.tensor_reduce(cnt8[:, :], bank[0][:, 0:NT * E].rearrange("p (t e) -> p e t", e=E),
                                        AX.X, ALU.add).then_inc(s_red, 1)
                dve.wait_ge(s_red, i + 1)
                nc.vector.scalar_tensor_tensor(take[:, :], cnt8[:, :], float(KTOP), bitv[:, :],
                                               ALU.is_ge, ALU.mult).then_inc(s_take, 1)
                dve.wait_ge(s_take, i + 1)
                nc.vector.tensor_tensor(thr[:, :], thr[:, :], take[:, :], ALU.bitwise_or).then_inc(s_thr, 1)
                nc.vector.tensor_scalar(bitv[:, :], bitv[:, :], 1, None, ALU.logical_shift_right).then_inc(s_bit, 1)
            dve.wait_ge(s_thr, 31)
            dve.wait_ge(s_bit, 31)

            thrb = thr[:, :].bitcast(F32).unsqueeze(1).to_broadcast([P, NT, E])
            sstep(nc.vector.tensor_tensor(cmp[:, 0, :, :], p8[:, :, :], thrb, ALU.is_gt))
            nc.vector.tensor_tensor(cmp[:, 1, :, :], p8[:, :, :], thrb, ALU.is_equal).then_inc(s_pre, 1)
            dve.wait_ge(s_tot, 1)
            te = lambda a: a.rearrange("p (k t e) -> p k e t", k=2, e=E)
            sstep(nc.vector.tensor_copy(tot[:, 0, :, :], te(bank[1][:, :])[:, 0]))
            sstep(nc.vector.tensor_copy(tot[:, 1, :, :], te(bank[1][:, :])[:, 1]))
            flat = lambda a: a[:, :, :, :].rearrange("p k e t -> p (k e t)")
            sstep(nc.vector.tensor_tensor_scan(flat(incl), flat(scanm), flat(tot), 0.0, ALU.mult, ALU.add))
            sstep(nc.vector.tensor_tensor(flat(tot), flat(incl), flat(tot), ALU.subtract))
            sstep(nc.vector.tensor_tensor(tot[:, 1, :, :], tot[:, 1, :, :],
                                          incl[:, 0, :, NT - 1:NT].to_broadcast([P, E, NT]), ALU.add))
            for k in range(2):
                sstep(nc.vector.tensor_tensor(pos[:, k, :, :],
                                              bank[2][:, k * 256:k * 256 + 256].rearrange("p (t e) -> p t e", e=E),
                                              tot[:, k, :, :].rearrange("p e t -> p t e"), ALU.add))
            sstep(nc.vector.scalar_tensor_tensor(sel[:, 1, :, :], pos[:, 1, :, :], float(KTOP), cmp[:, 1, :, :],
                                                 ALU.is_lt, ALU.mult))
            sstep(nc.vector.scalar_tensor_tensor(pos[:, 1, :, :], pos[:, 1, :, :], 1.0, sel[:, 1, :, :],
                                                 ALU.add, ALU.mult))
            sstep(nc.vector.scalar_tensor_tensor(pos[:, 0, :, :], pos[:, 0, :, :], 1.0, cmp[:, 0, :, :],
                                                 ALU.add, ALU.mult))
            sstep(nc.vector.tensor_tensor(pos[:, 0, :, :], pos[:, 0, :, :], pos[:, 1, :, :], ALU.add))
            sstep(nc.vector.tensor_scalar(posi[:, :, :], pos[:, 0, :, :], -1.0, None, ALU.add))
            sstep(nc.vector.tensor_scalar(hii[:, :, :], posi[:, :, :], 4, None, ALU.arith_shift_right))
            sstep(nc.vector.tensor_scalar(loi[:, :, :], posi[:, :, :], 15, None, ALU.bitwise_and))
            sstep(nc.vector.tensor_copy(hif[:, :, :], hii[:, :, :]))
            sstep(nc.vector.tensor_copy(lof[:, :, :], loi[:, :, :]))
            flat3 = lambda a: a[:, :, :].rearrange("p t e -> p (t e)").unsqueeze(2)
            iot = i32f[:, :].unsqueeze(1)
            sstep(nc.vector.tensor_tensor(oha[:, :, :], flat3(hif).to_broadcast([P, 256, 32]),
                                          iot.to_broadcast([P, 256, 32]), ALU.is_equal))
            sstep(nc.vector.tensor_tensor(ohb[:, :, 0:16], flat3(lof).to_broadcast([P, 256, 16]),
                                          iot[:, :, 0:16].to_broadcast([P, 256, 16]), ALU.is_equal))
            ohb4 = ohb[:, :, :].rearrange("p (t e) c -> p t e c", e=E)
            for e in range(E):
                sstep(nc.vector.tensor_tensor(ohb4[:, :, e, 16:32], ohb4[:, :, e, 0:16],
                                              i32f[:, :].unsqueeze(2).to_broadcast([P, NT, 16]), ALU.mult))
            nc.vector.tensor_scalar(ohb[:, :, 0:16], ohb[:, :, 0:16], pidx[:, 0:1], None, ALU.mult).then_inc(s_oh, 1)
            dve.wait_ge(s_idx, 1)
            sstep(nc.vector.tensor_copy(cidx[:, :, :], bank[3][:, 0:256].rearrange("p (g c) -> p g c", g=2)))
            for e in range(4):
                q = slice(32 * e, 32 * e + 32)
                nc.vector.scalar_tensor_tensor(idxc[q, :, :], cidx[q, :, 32 * e + 16:32 * e + 32], float(P),
                                               cidx[q, :, 32 * e:32 * e + 16], ALU.mult, ALU.add)\
                    .then_inc(s_idxc, 1)

            for e in range(E):
                r = e % 2
                if e:
                    dve.wait_ge(e_ye, JT * e)
                for j in range(JT):
                    n = JT * e + j
                    dve.wait_ge(e_y, n + 1)
                    nc.vector.tensor_tensor(yb[:, j, :], bank[6 + j % 2][:, 0:D], b2b[:, e, :], ALU.add)\
                        .then_inc(e_yb, 1)
                    dve.wait_ge(e_yb, n + 1)
                    if e >= 2 and j == 0:
                        dve.wait_ge(e_st, 16 * JT * (e - 1))
                    nc.vector.tensor_scalar(ye[:, r, j, :], yb[:, j, :], xe[:, e % 3, j, D + e:D + e + 1], None,
                                            ALU.mult).then_inc(e_ye, 1)

        @block.tensor
        def _(pe):
            pe.wait_ge(c_step, CONST_STEPS)
            pe.wait_ge(w_in, 16 * W_IN)

            def a_tiles(b, skip):
                for j in range(TB):
                    t = b * TB + j
                    pe.wait_ge(a_xn, t + 1)
                    if not (skip and j < 2):
                        pe.wait_ge(a_xt, t - 1)
                    for k in range(2):
                        ins = nc.tensor.transpose(bank[j % 2][:, P * k:P * k + P], xn_lhs(b, j, k), ident[:, :])
                    ins.then_inc(a_tp, 1)
                    pe.wait_ge(a_xt, t + 1)
                    if not (skip and j < 2):
                        pe.wait_ge(a_3, t - 1)
                    for k in range(2):
                        ins = nc.tensor.matmul(bank[2 + j % 2][:, 0:D + M], xta[:, j % 2, k, :], wgg[:, k, :],
                                               start=(k == 0), stop=(k == 1))
                    ins.then_inc(a_g, 1)

            def xn_lhs(b, j, k):
                return xn[:, b * TB + j, P * k:P * k + P]

            for b in range(B):
                a_tiles(b, b == 0)

            pe.wait_ge(r_rout, 1)
            cnt = bank[4][:, 0:NT * M]
            rflat = rt[8][:, :, :].rearrange("p t m -> p (t m)")
            nc.tensor.matmul(cnt, after[:, :], rflat, start=True, stop=False, skip_group_check=True)
            r4 = rflat.rearrange("p (b j m) -> p b j m", b=B, m=M)
            c4 = cnt.rearrange("p (b j m) -> p b j m", b=B, m=M)
            for d in range(1, TB):
                ins = nc.tensor.matmul(c4[:, :, 0:TB - d, :], ones[:, :], r4[:, :, d:TB, :], start=False,
                                       stop=(d == TB - 1), skip_group_check=True)
            ins.then_inc(r_suf, 1)
            pe.wait_ge(r_idx, 4)

            def mm(out_, l, r, a=True, z=True):
                return nc.tensor.matmul(out_, l, r, start=a, stop=z, skip_group_check=True)

            def slot(unit):
                u = unit(0)
                if u:
                    pe.wait_ge(d_in[u.r4], 16 * u.quad + 16)
                    if u.c >= 4:
                        pe.wait_ge(d_kts, u.n - 3)
                    elif u.c >= 1:
                        pe.wait_ge(d_xt, u.n)
                    for k in range(2):
                        ins = nc.tensor.transpose(bank[0][:, P * k:P * k + P], xin[:, u.r4, P * k:P * k + P],
                                                  ident[:, :])
                    ins.then_inc(d_tp, 1)
                u = unit(2)
                if u:
                    pe.wait_ge(d_lts, u.n + 1)
                    mm(bank[3][:, 0:P], lowt[0:LOW + 1, u.r2, :], w2g[0:LOW + 1, u.stream, :]).then_inc(d_z, 1)
                u = unit(1)
                if u:
                    pe.wait_ge(d_xt, u.n + 1)
                    if u.c >= 1:
                        pe.wait_ge(d_qks, u.n)
                        pe.wait_ge(d_vs, u.n)
                    for k in range(2):
                        ins = mm(bank[1][:, 0:QKL], xt[:, u.r2, k, :], wqk[:, u.stream, k, :], k == 0, k == 1)
                    ins.then_inc(d_qk, 1)
                    for k in range(2):
                        ins = mm(bank[2][:, 0:D], xt[:, u.r2, k, :], wv[:, u.stream, k, :], k == 0, k == 1)
                    ins.then_inc(d_v, 1)
                u = unit(3)
                if u:
                    pe.wait_ge(d_qkt, u.n + 1)
                    if u.c >= 1:
                        pe.wait_ge(d_w1, u.n)
                    nc.tensor.transpose(bank[5][:, 0:P], qkt[:, u.r2, 0:P], ident[:, :]).then_inc(d_qT, 1)
                    if unit(0):
                        pe.wait_ge(d_xt, u.n + 4)
                    else:
                        pe.wait_ge(d_kts, u.n)
                    nc.tensor.transpose(bank[0][:, 0:P], qkt[:, u.r2, P:2 * P], ident[:, :]).then_inc(d_kT, 1)
                u = unit(2)
                if u:
                    pe.wait_ge(d_g, u.n + 1)
                    if u.c >= 1:
                        pe.wait_ge(d_rm, u.n)
                    mm(bank[4][:, 0:P], relm[:, :], gg[:, :])
                    mm(bank[4][:, P:P + 4], gg[:, :], spanm[:, :]).then_inc(d_r, 1)
                u = unit(1)
                if u:
                    pe.wait_ge(d_qks, u.n + 1)
                    if u.c >= 1:
                        pe.wait_ge(d_g, u.n)
                    nc.tensor.transpose(bank[3][0:32, P:2 * P], qks[:, u.r2, 2 * P:2 * P + 32], ident[:, :])\
                        .then_inc(d_lt, 1)
                u = unit(4)
                if u:
                    pe.wait_ge(d_am, u.n + 1)
                    pe.wait_ge(d_s1, u.n + 1)
                    if u.c >= 1:
                        pe.wait_ge(d_ob, u.n)
                    for g in range(NH):
                        mm(bank[7][:, HDV * g:HDV * g + HDV], am[:, u.r2, g, :],
                           vv[:, u.r4, HDV * g:HDV * g + HDV], g == 0, False)
                    for c in range(2):
                        if c == 0 and u.first:
                            continue
                        h = slice(CH * c, CH * c + CH)
                        for g in range(NH):
                            ins = mm(bank[7][h, HDV * g:HDV * g + HDV], qbd[:, u.r2, g, h],
                                     (s1 if c else s0)[:, u.r2, :], False, True)
                    ins.then_inc(d_o, 1)
                u = unit(3)
                if u:
                    pe.wait_ge(d_qbd, u.n + 1)
                    pe.wait_ge(d_kts, u.n + 1)
                    if u.c >= 1:
                        pe.wait_ge(d_w0, u.n)
                    for c in range(2):
                        for lo, t0, t1 in HALVES:
                            h = slice(CH * c, CH * c + lo)
                            mm(bank[6][h, 0:NH * CH].rearrange("p (h t) -> p h t", h=NH)[:, :, t0:t1],
                               kt[:, h], qbd[:, u.r2, :, CH * c + t0:CH * c + t1])
                    for c in range(2):
                        h = slice(CH * c, CH * c + CH)
                        for g in range(NH):
                            ins = mm(bank[6 - c][HDK * g:HDK * g + HDK, 256:256 + HDV],
                                     qkt[h, u.r2, P + HDK * g:P + HDK * g + HDK],
                                     vv[h, u.r4, HDV * g:HDV * g + HDV])
                        ins.then_inc(d_u1 if c else d_s, 1)

            unit_slots(pe, slot, NU + 3)
            pe.wait_ge(d_ob, NU)

            pe.wait_ge(w_in2, 16 * 5)

            def project(b):
                pe.wait_ge(f_on2, b + 1)
                for k in range(2):
                    if b:
                        pe.wait_ge(f_ont, 2 * b)
                    for j in range(TB):
                        ins = nc.tensor.transpose(bank[k][:, P * j:P * j + P], on2[:, j, P * k:P * k + P],
                                                  ident[:, :])
                    ins.then_inc(f_tp, 1)
                pe.wait_ge(f_ont, 2 * b + 2)
                if b:
                    pe.wait_ge(f_x1, 2 * b)
                for j in range(TB):
                    for k in range(2):
                        ins = mm(bank[2 + j // 2][:, D * (j % 2):D * (j % 2) + D], ont[:, k, P * j:P * j + P],
                                 wo[:, k, :], k == 0, k == 1)
                    if j % 2:
                        ins.then_inc(f_y, 1)

            def route(b):
                pe.wait_ge(f_xn2, b * TB + TB)
                for k in range(2):
                    for j in range(TB):
                        ins = nc.tensor.transpose(bank[4 + k][:, P * j:P * j + P],
                                                  xn2[:, b % 2, j, P * k:P * k + P], ident[:, :])
                    ins.then_inc(f_tp2, 1)
                pe.wait_ge(f_xt2, 2 * b + 2)
                if b:
                    pe.wait_ge(f_l8, b)
                for j in range(TB):
                    for k in range(2):
                        ins = mm(bank[6][:, E * j:E * j + E], xn2t[:, k, P * j:P * j + P], wsb[:, k, :],
                                 k == 0, k == 1)
                ins.then_inc(f_l, 1)

            for b in range(B + 1):
                if b < B:
                    project(b)
                if b:
                    route(b - 1)
            nc.tensor.transpose(bank[7][:, 0:E * FT], b1r[:, :], ident[0:E * FT, 0:E * FT]).then_inc(b1_t, 1)

            with pe.Fori(0, 30) as i:
                pe.wait_ge(s_cmp, i + 1)
                nc.tensor.matmul(bank[0][:, 0:NT * E], ones_bf[:, :], cmp[:, 0, :, :].rearrange("p t e -> p (t e)"),
                                 start=True, stop=True).then_inc(s_cnt, 1)
            pe.wait_ge(s_pre, 1)
            pe.wait_ge(s_step, 4)
            cflat = cmp[:, :, :, :].rearrange("p k t e -> p (k t e)")
            nc.tensor.matmul(bank[2][:, :], before_bf[:, :], cflat, start=True, stop=True)
            nc.tensor.matmul(bank[1][:, :], ones_bf[:, :], cflat, start=True, stop=True).then_inc(s_tot, 1)
            pe.wait_ge(s_oh, 1)
            a4 = oha[:, :, :].rearrange("p (t g) c -> p t g c", g=E)
            b4 = ohb[:, :, :].rearrange("p (t g) c -> p t g c", g=E)

            def digits(t, first, last):
                for g in range(2):
                    ins = mm(bank[3][:, P * g:P * g + P], a4[:, t, 4 * g:4 * g + 4, :].rearrange("p e c -> p (e c)"),
                             b4[:, t, 4 * g:4 * g + 4, :].rearrange("p e c -> p (e c)"),
                             first and g == 0, last)
                return ins

            for t in range(NT):
                ins = digits(t, t == 0, t == NT - 1)
            ins.then_inc(s_idx, 1)
            pe.wait_ge(b1_c, 1)
            pe.wait_ge(s_idxc, 4)

            def rows_t(e):
                pe.wait_ge(e_x[e % 3], 16 * JT * (e // 3 + 1))
                if e >= 1:
                    pe.wait_ge(e_xt, 2 * e)
                if e >= 2:
                    pe.wait_ge(e_h, FT * (e - 1))
                for k in range(2):
                    for j in range(JT):
                        ins = nc.tensor.transpose(bank[k][:, P * j:P * j + P], xe[:, e % 3, j, P * k:P * k + P],
                                                  ident[:, :])
                    ins.then_inc(e_tp, 1)

            def hidden(e, r):
                pe.wait_ge(e_w[e % NW], 32 * (e // NW + 1))
                pe.wait_ge(e_xt, 2 * e + 2)
                for f in range(FT):
                    if e or f >= 4:
                        pe.wait_ge(e_gl, FT * e + f - 3)
                    for k in range(2):
                        ins = mm(bank[2 + f % 4][:, :], w1s[e % NW][:, k, P * f:P * f + P], xet[:, r, k, :],
                                 k == 0, k == 1)
                    ins.then_inc(e_h, 1)
                    if f == 3 and e + 1 < E:
                        rows_t(e + 1)

            def output(e, r):
                pe.wait_ge(e_gl, FT * e + FT)
                for j in range(JT):
                    n = JT * e + j
                    if n >= 2:
                        pe.wait_ge(e_yb, n - 1)
                    for f in range(FT):
                        ins = mm(bank[6 + j % 2][:, 0:D], ht[:, r, f, P * j:P * j + P], w2s[e % NW][:, f, :],
                                 f == 0, f == FT - 1)
                    ins.then_inc(e_y, 1)

            rows_t(0)
            hidden(0, 0)
            for e in range(1, E):
                hidden(e, e % 2)
                output(e - 1, (e - 1) % 2)
            output(E - 1, (E - 1) % 2)


CONST_STEPS = 58
W_IN = 6 * NS + 3

_INS = ['x', 'w_gate', 'w_q', 'w_k', 'w_v', 'w_gk1', 'w_gk2', 'b_gk', 'w_ks', 'w_vs', 'w_gk1s', 'w_gk2s', 'b_gks',
        'w_g', 'w_o', 'norm_w']
_INS = ['L0_attn_' + n for n in _INS] + ['L0_ffn_' + n for n in ['Ws', 'bs', 'W1', 'b1', 'W2', 'b2']]
_OUTS = [((B, S, D), 'float32')]


def kernel(**inputs):
    import numpy as _np
    import concourse.bacc as _bacc
    from concourse import mybir as _mybir
    from concourse.bass_utils import run_bass_kernel_spmd as _run

    nc = _bacc.Bacc("TRN2", target_bir_lowering=False, num_devices=1)
    arrays, args = {}, []
    for name in _INS:
        a = _np.ascontiguousarray(inputs[name])
        arrays[f"in_{name}_dram"] = a
        args.append(nc.dram_tensor(f"in_{name}_dram", a.shape, _mybir.dt.from_np(a.dtype), kind="ExternalInput").ap())
    for i, (shape, dtype) in enumerate(_OUTS):
        dt = _mybir.dt.from_np(_np.dtype(dtype))
        args.append(nc.dram_tensor(f"out_{i}_dram", shape, dt, kind="ExternalOutput").ap())
    build(nc, *args)
    r = _run(nc, [arrays], core_ids=[0])
    got = tuple(r.results[0][f"out_{i}_dram"] for i in range(len(_OUTS)))
    return got[0]
```

```python
from contextlib import ExitStack

import concourse.bass as bass
from concourse import mybir

F32 = mybir.dt.float32
BF16 = mybir.dt.bfloat16
I32 = mybir.dt.int32
ALU = mybir.AluOpType
ACT = mybir.ActivationFunctionType
AX = mybir.AxisListType

P = 128
B, S, D = 8, 512, 256
NT = B * S // P
TB = S // P
NH, HDK, HDV = 4, 32, 64
M, CAP = 4, 256
LOW = 16
NS = M + 1
SHARED = M
CH = 64
HALVES = ((CH // 2, 0, CH // 2), (CH, CH // 2, CH))
NU_SH = NT
NU = NU_SH + B * M * CAP // P
ROWS = NU * P
HALF_B = B // 2
HALF_ROWS = HALF_B * M * CAP
QKL = 2 * P + LOW
E, F = 8, 1024
ASSIGN_SLOTS = (1, 2)
POOL_DIGITS = 12
NW = 4
KTOP = B * S // E
JT = KTOP // P
FT = F // P
GN = 16.0
EPS = 1e-5
EXP_LIM = 85.0
ARENA = 15 * 1024
OUT_OF_RANGE = float(1 << 20)


class Unit:

    def __init__(self, c, i=0, stride=0, least=0):
        self.c = c
        self.half = int(c + stride * least >= NU_SH + (NU - NU_SH) // 2)
        self.n = c + i * stride if stride else c
        self.quad = c // 4 + i * (stride // 4) if stride else c // 4
        self.r4, self.r2 = c % 4, c % 2
        if c < NU_SH:
            self.stream, self.first = SHARED, c % TB == 0
        else:
            pos = (c - NU_SH) % (2 * M)
            self.stream, self.first = pos // 2, pos % 2 == 0


def unit_slots(eng, slot, last_slot, peeled=None):
    def static(s):
        slot(lambda k: Unit(s - k) if 0 <= s - k < NU else None)

    for s in range(8):
        static(s)
    with eng.Fori(0, (NU_SH - 8) // 4) as i:
        for u in range(4):
            slot(lambda k: Unit(8 + u - k, i, 4))
    for s in range(NU_SH, NU_SH + 8):
        static(s)
    rounds = (NU - NU_SH - 8) // 8
    for lo, hi in ((0, rounds),) if peeled is None else ((0, peeled), (peeled + 1, rounds)):
        with eng.Fori(lo, hi) as i:
            for u in range(8):
                slot(lambda k: Unit(NU_SH + 8 + u - k, i, 8, lo))
        if hi == peeled:
            for u in range(8):
                static(NU_SH + 8 + 8 * peeled + u)
    for s in range(NU, last_slot + 1):
        static(s)


def routed(b):
    if b < B - 1:
        return range(max(b - 3, 0), b - 2)
    return range(b - 3 if b == B - 1 else b - 2, min(b - 1, B))


def build(nc, x, w_gate, w_q, w_k, w_v, w_gk1, w_gk2, b_gk, w_ks, w_vs, w_gk1s, w_gk2s, b_gks, w_g, w_o,
          norm_w, Ws, bs, W1, b1, W2, b2, out):
    xf = x.rearrange("b s d -> (b s) d")
    outf = out.rearrange("b s d -> (b s) d")
    x_c = nc.dram_tensor("x_c", (ROWS, D), F32, kind="Internal").ap()
    o_s = nc.dram_tensor("o_s", (B * S, D), F32, kind="Internal").ap()
    o_m = [nc.dram_tensor(f"o_m{h}", (HALF_ROWS, D), F32, kind="Internal").ap() for h in range(2)]
    x_p = nc.dram_tensor("x_p", (B * S, D + E), F32, kind="Internal").ap()

    with ExitStack() as ctx:
        def sb(name, shape, dt=F32):
            return ctx.enter_context(nc.sbuf_tensor(name, shape, dt))

        def sem(name):
            return ctx.enter_context(nc.semaphore(name))

        def sems(name, n):
            return [sem(f"{name}{i}") for i in range(n)]

        bank = [ctx.enter_context(nc.psum_tensor(f"bank{i}", [P, 512], F32)) for i in range(8)]

        ident = sb("ident", [P, P])
        relm = sb("relm", [P, P])
        spanm = sb("spanm", [P, 4])
        headm = sb("headm", [P, NH, P])
        causal = sb("causal", [P, CH])
        after = sb("after", [P, P])
        ones = sb("ones", [P, P])
        same = sb("same", [P, P])
        below = sb("below", [P, P])
        tile_no = sb("tile_no", [P, NT * E], BF16)
        lane = sb("lane", [P, P], I32)
        zeros = sb("zeros", [P, 2048])
        ibuf = sb("ibuf", [P, B, TB, M], I32)
        lastrow = sb("lastrow", [P, B, TB, M])
        pidx = sb("pidx", [P, 1])
        ones_w = sb("ones_w", [P, NT * E])
        epst = sb("epst", [P, 1])

        wgg = sb("wgg", [P, 2, D + M])
        wo = sb("wo", [P, 2, D])
        nwb = sb("nwb", [P, D])
        wsb = sb("wsb", [P, 2, E])
        bsb = sb("bsb", [P, E])
        b1r = sb("b1r", [E * FT, P])
        b1c = sb("b1c", [P, E * FT])
        b2b = sb("b2b", [P, E, D])

        xres = sb("xres", [P, NT, D])
        big = sb("big", [P, NT * D])
        xn = big[:, :].rearrange("p (t d) -> p t d", d=D)
        gs = sb("gs", [P, NT, D])

        st6 = sb("st6", [P, TB, 6])
        mv = sb("mv", [P, TB, 2])
        held = sb("held", [P, 1])
        lnv = sb("lnv", [P, TB])
        rstd = sb("rstd", [P, TB])
        xta = sb("xta", [P, 2, 2, P])
        eg = sb("eg", [P, D])
        eg1 = sb("eg1", [P, D])
        eg2 = sb("eg2", [P, 2, D])
        eg3 = sb("eg3", [P, 2, D])
        lg = sb("lg", [P, NT, M])

        rt = [sb(f"rt{i}", [P, NT, M]) for i in range(10)]
        rs = [sb(f"rs{i}", [P, NT]) for i in range(12)]
        wt = sb("wt", [P, 2, NT])
        sidx = sb("sidx", [P, 2, NT], I32)
        gidx = sb("gidx", [P, 2, NT], I32)
        keyw = sb("keyw", [P, M])

        arena = sb("arena", [P, ARENA])
        arena_at = [0]

        def carve(shape, dt=F32, of=None):
            n = 1
            for d in shape[1:]:
                n *= d
            words = n * (2 if dt == BF16 else 4) // 4
            ap = arena[:, arena_at[0]:arena_at[0] + words]
            arena_at[0] += words
            assert arena_at[0] <= ARENA
            if dt != F32:
                ap = ap.bitcast(dt)
            names = "abcd"[:len(shape) - 1]
            if len(names) > 1:
                ap = ap.rearrange(f"p ({' '.join(names)}) -> p {' '.join(names)}",
                                  **dict(zip(names[1:], shape[2:])))
            return ap

        dv = lambda name, shape, dt=F32: carve(shape, dt)

        ob = dv("ob", [P, 4, D])
        wqk = dv("wqk", [P, NS, 2, QKL])
        wv = dv("wv", [P, NS, 2, D])
        w2g = dv("w2g", [P, NS, P])
        xin = dv("xin", [P, 4, D])
        xt = dv("xt", [P, 2, 2, P])
        qks = dv("qks", [P, 2, 288])
        vv = dv("vv", [P, 4, D])
        lowt = dv("lowt", [P, 2, P])
        zab = dv("zab", [P, P])
        zex = dv("zex", [P, P])
        zln = dv("zln", [P, P])
        gg = dv("gg", [P, P])
        rp = dv("rp", [P, 132])
        rm = dv("rm", [P, P])
        ee = dv("ee", [P, 4, 264])
        qkt = dv("qkt", [P, 2, 2 * P])
        qbd = dv("qbd", [P, 2, NH, P])
        kt = dv("kt", [P, P])
        am = dv("am", [P, 2, NH, P])
        s0 = dv("s0", [P, 2, HDV])
        s1 = dv("s1", [P, 2, HDV])
        wa = dv("wa", [P, HDV])
        wb = dv("wb", [P, HDV])

        og = big[:, :].rearrange("p (r k j d) -> p r k j d", r=4, k=2, j=TB)
        arena_at[0] = 0
        xn2t = dv("xn2t", [P, 2, TB * P])
        shift = dv("shift", [P, TB])
        hs = dv("hs", [P, TB * NH])
        hl = dv("hl", [P, TB * NH])
        hr = dv("hr", [P, TB * NH])
        on = dv("on", [P, TB, D])
        on2 = dv("on2", [P, TB, D])
        ont = dv("ont", [P, 2, TB * P])
        x1 = dv("x1", [P, 2, TB, D])
        xn2 = dv("xn2", [P, 2, TB, D])
        arena_at[0] = 8320 + NT * E
        osh = [zeros[:, TB * D * r:TB * D * r + TB * D].rearrange("p (j d) -> p j d", j=TB) for r in range(2)]
        osh.append(dv("osh", [P, TB, D]))
        oa = dv("oa", [P, TB, D])
        osq = dv("osq", [P, TB, D])

        arena_at[0] = 8320
        l8 = dv("l8", [P, NT, E])
        pr = dv("pr", [P, NT, E])
        p8 = dv("p8", [P, 2, NT // 2, E])
        pt = dv("pt", [P, NT * E])
        base = dv("base", [P, 1], I32)
        steps = dv("steps", [P, 3, 3], I32)
        cand = dv("cand", [P, 3], I32)
        cand2 = dv("cand2", [P, 3], I32)
        enough = dv("enough", [P, 3])
        digit4 = dv("digit4", [P, 1])
        add4 = dv("add4", [P, 1], I32)
        cmp = dv("cmp", [P, 3, NT * E])
        reached = dv("reached", [P, 3])
        picked = dv("picked", [P, 2, NT * E])
        incl = dv("incl", [P, 2, NT * E])
        offs = dv("offs", [P, 4])
        place = dv("place", [P, 3, NT * E])
        posi = dv("posi", [P, NT * E], I32)
        digit = dv("digit", [P, 2, NT * E], I32)
        digit_bf = dv("digit_bf", [P, 2, NT * E], BF16)
        oha = gs[:, :, :].rearrange("p t d -> p (t d)")[:, 0:4096].bitcast(BF16).rearrange(
            "p (e c t) -> p e c t", c=32, t=NT)
        ohb = gs[:, :, :].rearrange("p t d -> p (t d)")[:, 4096:8192].bitcast(BF16).rearrange(
            "p (e c t) -> p e c t", c=32, t=NT)
        cidx = sb("cidx", [P, 2, P])
        idxc = sb("idxc", [P, 2, 16], I32)
        idxs = sb("idxs", [P, E, JT], I32)

        w_room = [at[:, 16 * h:16 * h + 16, :].rearrange("p t d -> p (t d)") for at in (xres, gs) for h in range(2)]
        w1s = [r[:, 0:2 * F].rearrange("p (k f) -> p k f", k=2) for r in w_room]
        w2s = [r[:, 2 * F:2 * F + FT * D].rearrange("p (f d) -> p f d", f=FT) for r in w_room]
        ht = big[:, :].rearrange("p (r f t) -> p r f t", r=2, f=FT)
        arena_at[0] = 0
        xe = dv("xe", [P, 3, JT, D + E])
        xet = dv("xet", [P, 2, 2, KTOP])
        yb = dv("yb", [P, JT, D])
        ye = dv("ye", [P, 2, JT, D])

        c_step = sem("c_step")
        c_dve = sem("c_dve")
        wg_in = sem("wg_in")
        w_in = sem("w_in")
        w_in2 = sem("w_in2")
        zero_st = sem("zero_st")
        x_in = sems("x_in", 2)
        a_st = sem("a_st"); a_mv = sem("a_mv"); a_lnv = sem("a_lnv"); a_rstd = sem("a_rstd")
        a_xn = sem("a_xn"); xn_st = sem("xn_st")
        a_tp = sem("a_tp"); a_xt = sem("a_xt"); a_g = sem("a_g"); a_eg = sem("a_eg")
        a_lg = sem("a_lg"); a_1 = sem("a_1"); a_2 = sem("a_2"); a_3 = sem("a_3"); a_gs = sem("a_gs")
        r_step = sem("r_step"); r_sub = sem("r_sub"); r_exp = sem("r_exp"); r_rout = sem("r_rout")
        r_suf = sem("r_suf"); r_read = sem("r_read"); r_idx = sem("r_idx"); scat = sem("scat")
        d_in = sems("d_in", 4)
        d_tp = sem("d_tp"); d_xt = sem("d_xt"); d_qk = sem("d_qk"); d_v = sem("d_v")
        d_qks = sem("d_qks"); d_vs = sem("d_vs"); d_lt = sem("d_lt"); d_lts = sem("d_lts"); d_z = sem("d_z")
        d_ab = sem("d_ab"); d_ex = sem("d_ex"); d_ln = sem("d_ln"); d_g = sem("d_g"); d_r = sem("d_r")
        d_rp = sem("d_rp"); d_rm = sem("d_rm"); d_ep = sem("d_ep"); d_em = sem("d_em")
        d_qkt = sem("d_qkt"); d_qT = sem("d_qT"); d_kT = sem("d_kT"); d_qbd = sem("d_qbd"); d_kts = sem("d_kts")
        d_s = sem("d_s"); d_u1 = sem("d_u1"); d_am = sem("d_am")
        d_s0 = sem("d_s0"); d_w0 = sem("d_w0"); d_s1 = sem("d_s1"); d_w1 = sem("d_w1")
        d_o = sem("d_o"); d_ob = sem("d_ob")
        d_st = sems("d_st", 4)
        f_first = sems("f_first", 2)
        f_sh = sems("f_sh", 3); f_g = sems("f_g", 4)
        f_a0 = sem("f_a0")
        f_oa = sem("f_oa"); f_sq = sem("f_sq"); f_hs = sem("f_hs"); f_hl = sem("f_hl"); f_hr = sem("f_hr")
        f_on = sem("f_on"); f_on2 = sem("f_on2"); f_tp = sem("f_tp"); f_ont = sem("f_ont")
        f_y = sem("f_y"); f_x1 = sem("f_x1"); out_st = sems("out_st", 2)
        f_st = sem("f_st"); f_mv = sem("f_mv"); f_lnv = sem("f_lnv"); f_rstd = sem("f_rstd")
        f_shift = sem("f_shift"); f_xn2 = sem("f_xn2"); xp_st = sems("xp_st", 2); f_tp2 = sem("f_tp2"); f_xt2 = sem("f_xt2")
        f_l = sem("f_l"); f_l8 = sem("f_l8")
        s_step = sem("s_step"); s_sub = sem("s_sub"); s_exp = sem("s_exp"); s_p8 = sem("s_p8"); p8_st = sem("p8_st")
        s_tp = sem("s_tp")
        s_bit = sem("s_bit"); s_cand2 = sem("s_cand2"); s_cmp = sem("s_cmp"); s_cnt = sem("s_cnt")
        s_four = sem("s_four"); s_add = sem("s_add"); s_cand = sem("s_cand"); s_base = sem("s_base")
        s_incl = sem("s_incl"); s_offs = sem("s_offs"); s_place = sem("s_place"); s_back = sem("s_back")
        s_digit = sem("s_digit"); s_oh = sem("s_oh"); s_idx = sem("s_idx"); s_idxc = sem("s_idxc")
        idx_in = sems("idx_in", E)
        b1_t = sem("b1_t"); b1_c = sem("b1_c")
        e_w = sems("e_w", NW); e_x = sems("e_x", 3)
        e_tp = sem("e_tp")
        e_xt = sem("e_xt")
        e_h = sem("e_h"); e_gl = sem("e_gl")
        e_y = sem("e_y"); e_yb = sem("e_yb"); e_ye = sem("e_ye")
        e_st = sem("e_st")

        block = ctx.enter_context(nc.Block())

        @block.gpsimd
        def _(pool):
            done = [0]

            def step(ins):
                done[0] += 1
                ins.then_inc(c_step, 1)
                pool.wait_ge(c_step, done[0])

            def select(ap, pattern, base, mult, op=ALU.is_ge, fill=0.0):
                step(nc.gpsimd.affine_select(out=ap, in_=ap, compare_op=op, fill=fill, base=base,
                                             pattern=pattern, channel_multiplier=mult))

            step(nc.gpsimd.memset(zeros[:, :], 0.0))
            step(nc.gpsimd.memset(ident[:, :], 0.0))
            select(ident[:, :], [[-1, P]], 0, 1, ALU.not_equal, 1.0)
            step(nc.gpsimd.memset(epst[:, :], EPS))
            step(nc.gpsimd.memset(ones[:, :], 1.0))
            step(nc.gpsimd.memset(ones_w[:, :], 1.0))
            step(nc.gpsimd.memset(after[:, :], 1.0))
            select(after[:, :], [[-1, P]], -1, 1)
            step(nc.gpsimd.iota(lane[:, :], pattern=[[-1, P]], base=P, channel_multiplier=1))
            for j in range(P // 32):
                blk = relm[:, 32 * j:32 * j + 32]
                step(nc.gpsimd.memset(blk, (1.0 if j % 2 else -1.0) / GN))
                select(blk, [[0, 32]], -32 * j, 1)
                select(blk, [[0, 32]], 32 * j + 31, -1)
                if j % 2:
                    select(blk, [[1, 32]], 32 * j, -1)
                else:
                    select(blk, [[-1, 32]], -32 * j - 1, 1)
            step(nc.gpsimd.memset(spanm[:, :], 0.0))
            for c, (lo, hi) in enumerate(((0, 32), (32, 96), (96, 128))):
                step(nc.gpsimd.memset(spanm[:, c:c + 1], 1.0 / GN))
                select(spanm[:, c:c + 1], [[0, 1]], -lo, 1)
                select(spanm[:, c:c + 1], [[0, 1]], hi - 1, -1)
            step(nc.gpsimd.memset(headm[:, :, :], float(HDK) ** -0.5))
            select(headm[:, :, :], [[-HDK, NH], [0, P]], 0, 1)
            select(headm[:, :, :], [[HDK, NH], [0, P]], HDK - 1, -1)
            step(nc.gpsimd.memset(causal[:, :], 1.0))
            for c in range(2):
                select(causal[CH * c:CH * c + CH, :], [[1, CH]], 0, -1)
            for h in range(2):
                step(nc.gpsimd.iota(ibuf[:, HALF_B * h:HALF_B * h + HALF_B, :, :],
                                    pattern=[[M * CAP, HALF_B], [0, TB], [CAP, M]],
                                    base=CAP - 1, channel_multiplier=0))
            step(nc.gpsimd.tensor_copy(lastrow[:, :, :, :], ibuf[:, :, :, :]))
            ib = ibuf[:, :, :, :].rearrange("p a b c -> p (a b c)")
            step(nc.gpsimd.iota(ib[:, 32:33], pattern=[[0, 1]], base=0, channel_multiplier=1))
            step(nc.gpsimd.tensor_copy(pidx[:, :], ib[:, 32:33]))
            step(nc.gpsimd.iota(ib[:, :], pattern=[[0, E // 2], [1, 2], [2, NT // 2]], base=0,
                                channel_multiplier=0))
            for h in range(2):
                step(nc.gpsimd.tensor_copy(tile_no[:, P * h:P * h + P], ib[:, :]))
            for m in range(M):
                step(nc.gpsimd.memset(keyw[:, m:m + 1], float(M - m)))
            step(nc.gpsimd.memset(qks[:, :, QKL:288], 0.0))
            step(nc.gpsimd.memset(qks[:, :, QKL:QKL + 1], 1.0))
            step(nc.gpsimd.memset(am[:, :, :, :], 0.0))
            assert done[0] == CONST_STEPS, done[0]

            pool.wait_ge(c_dve, 2)
            nc.gpsimd.tensor_copy(below[:, :], same[:, :]).then_inc(c_step, 1)
            pool.wait_ge(c_step, CONST_STEPS + 1)
            nc.gpsimd.affine_select(out=below[:, :], in_=below[:, :], compare_op=ALU.is_ge, fill=0.0, base=-1,
                                    pattern=[[1, P]], channel_multiplier=-1).then_inc(c_step, 1)

            pool.wait_ge(r_idx, 4)
            pool.wait_ge(zero_st, 16 * 4)
            for t in range(NT):
                for k in range(2):
                    nc.gpsimd.indirect_dma_start(
                        x_c, bass.IndirectOffsetOnAxis(sidx[:, k, t:t + 1], 0), xn[:, t, :], None,
                        bounds_check=ROWS - 1, oob_is_err=False).then_inc(scat, 16)

            for b in range(B):
                if b % HALF_B == 0:
                    for r in range(4):
                        pool.wait_ge(d_st[r], 16 * (NU_SH + (NU - NU_SH) // 2 * (b // HALF_B + 1)) // 4)
                if b == 0:
                    for c in range(2):
                        pool.dma_start(osh[c], o_s[S * c:S * c + S, :].rearrange("(t p) d -> p t d", p=P))\
                            .then_inc(f_first[c], 16)
                if b >= 4:
                    pool.wait_ge(f_oa, b - 3)
                for j in range(TB):
                    for k in range(2):
                        t = b * TB + j
                        nc.gpsimd.indirect_dma_start(
                            og[:, b % 4, k, j, :], None, o_m[b // HALF_B],
                            bass.IndirectOffsetOnAxis(gidx[:, k, t:t + 1], 0),
                            bounds_check=HALF_ROWS - 1, oob_is_err=False).then_inc(f_g[b % 4], 16)

            et = lambda a: a.rearrange("p (e t) -> p e t", e=E)
            pool.wait_ge(s_digit, 1)
            for c in range(POOL_DIGITS):
                ins = nc.gpsimd.tensor_scalar(oha[:, :, c, :], et(digit_bf[:, 0, :]), float(c), None, ALU.is_equal)
            ins.then_inc(s_oh, 1)

            pool.wait_ge(p8_st, 32)
            for r in range(2):
                pool.wait_ge(xp_st[r], 16 * B // 2)
                pool.wait_ge(out_st[r], 16 * B // 2)

            def gather(e):
                pool.wait_ge(idx_in[e], 16)
                if e >= 3:
                    pool.wait_ge(e_tp, 2 * (e - 2))
                    pool.wait_ge(e_ye, JT * (e - 2))
                for j in range(JT):
                    nc.gpsimd.indirect_dma_start(
                        xe[:, e % 3, j, :], None, x_p, bass.IndirectOffsetOnAxis(idxs[:, e, j:j + 1], 0),
                        bounds_check=B * S - 1, oob_is_err=False).then_inc(e_x[e % 3], 16)

            gather(0)
            gather(1)
            gather(2)
            for e in range(E):
                if e:
                    pool.wait_ge(e_st, 16 * JT * e)
                for j in range(JT):
                    pool.wait_ge(e_ye, JT * e + j + 1)
                    nc.gpsimd.indirect_dma_start(
                        outf, bass.IndirectOffsetOnAxis(idxs[:, e, j:j + 1], 0), ye[:, e % 2, j, :], None,
                        bounds_check=B * S - 1, oob_is_err=True, compute_op=ALU.add).then_inc(e_st, 16)
                if e + 3 < E:
                    gather(e + 3)
            pool.wait_ge(e_st, 16 * JT * E)

        @block.sync
        def _(sp):
            def load_x(b):
                if b >= 2:
                    sp.wait_ge(x_in[b % 2], 16 * (b // 2))
                sp.dma_start(xres[:, TB * b:TB * b + TB, :],
                             xf[S * b:S * b + S, :].rearrange("(t p) d -> p t d", p=P)).then_inc(x_in[b % 2], 16)

            for b in range(B):
                load_x(b)
            kp = lambda w: w.rearrange("(k p) n -> p k n", p=P)
            for m in range(NS):
                wk, wvm, wl, w2, bb = ((w_ks, w_vs, w_gk1s, w_gk2s, b_gks) if m == SHARED else
                                       (w_k[m], w_v[m], w_gk1[m], w_gk2[m], b_gk[m]))
                sp.dma_start(wqk[:, m, :, 0:P], kp(w_q)).then_inc(w_in, 16)
                sp.dma_start(wqk[:, m, :, P:2 * P], kp(wk)).then_inc(w_in, 16)
                sp.dma_start(wqk[:, m, :, 2 * P:QKL], kp(wl)).then_inc(w_in, 16)
                sp.dma_start(wv[:, m, :, :], kp(wvm)).then_inc(w_in, 16)
                sp.dma_start(w2g[0:LOW, m, :], w2).then_inc(w_in, 16)
                sp.dma_start(w2g[LOW:LOW + 1, m, :], bb.rearrange("(a n) -> a n", a=1)).then_inc(w_in, 16)
            sp.dma_start(wo[:, :, :], kp(w_o)).then_inc(w_in2, 16)
            sp.dma_start(wsb[:, :, :], kp(Ws)).then_inc(w_in2, 16)
            sp.dma_start(bsb[:, :], bs.rearrange("(a n) -> a n", a=1).to_broadcast([P, E])).then_inc(w_in2, 16)
            sp.dma_start(b1r[:, :], b1.rearrange("e (f p) -> (e f) p", p=P)).then_inc(w_in2, 16)
            sp.dma_start(b2b[:, :, :], b2.rearrange("(a e) n -> a e n", a=1).to_broadcast([P, E, D]))\
                .then_inc(w_in2, 16)
            sp.wait_ge(c_step, 1)
            for q in range(4):
                sp.dma_start(x_c[NU_SH * P + 2048 * q:NU_SH * P + 2048 * q + 2048, :]
                              .rearrange("(p a) d -> p (a d)", p=P).rearrange("p (c d) -> p c d", c=2),
                              zeros[:, :].unsqueeze(1).to_broadcast([P, 2, 2048])).then_inc(zero_st, 16)
            with sp.Fori(0, B) as b:
                sp.wait_ge(a_xn, b * TB + TB)
                sp.dma_start(x_c[bass.ds(b * S, S), :].rearrange("(t p) d -> p t d", p=P),
                             xn[:, bass.ds(b * TB, TB), :]).then_inc(xn_st, 16)
            sp.wait_ge(xn_st, 16 * B)

            def slot(unit):
                u = unit(0)
                if u:
                    if u.c == NU_SH:
                        sp.wait_ge(scat, 16 * 2 * NT)
                    if u.c >= 4:
                        sp.wait_ge(d_tp, u.n - 3)
                    sp.dma_start(xin[:, u.r4, :], x_c[bass.ds(u.n * P, P), :]).then_inc(d_in[u.r4], 16)
                u = unit(7)
                if u:
                    sp.wait_ge(d_ob, u.n + 1)
                    to, first = (o_s, 0) if u.stream == SHARED else (o_m[u.half], NU_SH * P + u.half * HALF_ROWS)
                    sp.dma_start(to[bass.ds(u.n * P - first, P), :], ob[:, u.r4, :]).then_inc(d_st[u.r4], 16)

            unit_slots(sp, slot, NU + 6, peeled=HALF_B - 1)

            def load_osh(b):
                if b >= 3:
                    sp.wait_ge(f_oa, b - 2)
                sp.dma_start(osh[b % 3], o_s[S * b:S * b + S, :].rearrange("(t p) d -> p t d", p=P))\
                    .then_inc(f_sh[b % 3], 16)

            for r in range(4):
                sp.wait_ge(d_st[r], 16 * (NU // 4))
            for b in range(B + 2):
                if b + 2 < B:
                    load_osh(b + 2)
                if b < B:
                    sp.wait_ge(f_x1, 2 * b + 2)
                    sp.dma_start(outf[S * b:S * b + S, :].rearrange("(t p) d -> p t d", p=P), x1[:, b % 2, :, :])\
                        .then_inc(out_st[b % 2], 16)
                if b >= 2:
                    c = b - 2
                    sp.wait_ge(f_xn2, TB * c + TB)
                    sp.dma_start(x_p[S * c:S * c + S, 0:D].rearrange("(t p) d -> p t d", p=P), xn2[:, c % 2, :, :])\
                        .then_inc(xp_st[c % 2], 16)

            def load_w(e):
                if e == 2:
                    sp.wait_ge(e_tp, 2)
                if e >= NW:
                    sp.wait_ge(e_y, JT * (e - NW + 1))
                sp.dma_start(w1s[e % NW], W1[e].rearrange("(k p) f -> p k f", p=P)).then_inc(e_w[e % NW], 16)
                sp.dma_start(w2s[e % NW], W2[e].rearrange("(f p) d -> p f d", p=P)).then_inc(e_w[e % NW], 16)

            load_w(0)
            load_w(1)
            sp.wait_ge(s_p8, 1)
            for h in range(2):
                sp.dma_start(x_p[:, D:D + E].rearrange("(q h p) e -> h p q e", h=2, p=P)[h], p8[:, h, :, :],
                             allow_slow_non_contiguous=True).then_inc(p8_st, 16)
            sp.wait_ge(s_idxc, 4)
            for e in range(E):
                sp.dma_start(idxs[:, e, :], idxc[32 * (e % 4):32 * (e % 4) + 32, e // 4, :]
                             .rearrange("p (l j) -> p l j", j=JT)).then_inc(idx_in[e], 16)
            for e in range(2, E):
                load_w(e)

        @block.scalar
        def _(act):
            act.preload_act_table_set("natural_log_exp_and_others")
            kp = lambda w: w.rearrange("(k p) n -> p k n", p=P)
            act.dma_start(wgg[:, :, 0:D], kp(w_g)).then_inc(wg_in, 16)
            act.dma_start(wgg[:, :, D:D + M], kp(w_gate)).then_inc(wg_in, 16)
            act.dma_start(nwb[:, :].rearrange("p (h v) -> p h v", h=NH),
                          norm_w.rearrange("(a b n) -> a b n", a=1, b=1).to_broadcast([P, NH, HDV]))\
                .then_inc(wg_in, 16)
            act.wait_ge(c_step, FIRST_STEPS)

            def a_copy(t, j):
                act.wait_ge(a_tp, t + 1)
                if not (isinstance(t, int) and t < 2):
                    act.wait_ge(a_g, t - 1)
                nc.scalar.activation(xta[:, j % 2, :, :], bank[j % 2][:, 0:D].rearrange("p (k t) -> p k t", k=2),
                                     ACT.Copy).then_inc(a_xt, 1)

            def a_slot(b_std, b_tile):
                if b_std is not None:
                    act.wait_ge(a_mv, b_std * TB + TB)
                    nc.scalar.activation(lnv[:, :], mv[:, :, 1], ACT.Ln, bias=epst[:, 0:1]).then_inc(a_lnv, 1)
                    act.wait_ge(a_lnv, b_std + 1)
                    nc.scalar.activation(rstd[:, :], lnv[:, :], ACT.Exp, scale=-0.5).then_inc(a_rstd, 1)
                if b_tile is not None:
                    for j in range(TB):
                        t = b_tile * TB + j
                        if b_std is not None or j + 1 < TB:
                            a_copy(t + 1, j + 1)
                        act.wait_ge(a_g, t + 1)
                        nc.scalar.activation(eg[:, :], bank[2 + j % 2][:, 0:D], ACT.Exp, scale=-1.0)\
                            .then_inc(a_eg, 1)
                        act.wait_ge(a_eg, t + 1)
                        nc.scalar.activation(eg1[:, :], eg[:, :], ACT.Ln, bias=1.0).then_inc(a_1, 1)
                        act.wait_ge(a_1, t + 1)
                        if not (isinstance(t, int) and t < 2):
                            act.wait_ge(a_3, t - 1)
                        nc.scalar.activation(eg2[:, j % 2, :], eg1[:, :], ACT.Exp, scale=-1.0).then_inc(a_2, 1)

            a_slot(0, None)
            a_copy(0, 0)
            a_slot(1, 0)
            with act.Fori(2, B) as b:
                a_slot(b, b - 1)
            a_slot(None, B - 1)
            act.wait_ge(r_sub, 1)
            nc.scalar.activation(rt[1][:, :, :], rt[0][:, :, :], ACT.Exp).then_inc(r_exp, 1)

            def slot(unit):
                u = unit(0)
                if u:
                    act.wait_ge(d_tp, u.n + 1)
                    if u.c >= 2:
                        act.wait_ge(d_v, u.n - 1)
                    nc.scalar.activation(xt[:, u.r2, :, :], bank[0][:, 0:D].rearrange("p (k t) -> p k t", k=2),
                                         ACT.Copy).then_inc(d_xt, 1)
                u = unit(2)
                if u:
                    act.wait_ge(d_z, u.n + 1)
                    nc.scalar.activation(zab[:, :], bank[3][:, 0:P], ACT.Abs).then_inc(d_ab, 1)
                    act.wait_ge(d_ab, u.n + 1)
                    nc.scalar.activation(zex[:, :], zab[:, :], ACT.Exp, scale=-1.0).then_inc(d_ex, 1)
                    act.wait_ge(d_ex, u.n + 1)
                    if u.c >= 1:
                        act.wait_ge(d_g, u.n)
                    nc.scalar.activation(zln[:, :], zex[:, :], ACT.Ln, bias=1.0).then_inc(d_ln, 1)
                u = unit(1)
                if u:
                    act.wait_ge(d_qk, u.n + 1)
                    if u.c >= 2:
                        act.wait_ge(d_qkt, u.n - 1)
                    nc.scalar.activation(qks[:, u.r2, 0:QKL], bank[1][:, 0:QKL], ACT.Copy).then_inc(d_qks, 1)
                    act.wait_ge(d_v, u.n + 1)
                    if u.c >= 4:
                        act.wait_ge(d_o, u.n - 3)
                    nc.scalar.activation(vv[:, u.r4, :], bank[2][:, 0:D], ACT.Copy).then_inc(d_vs, 1)
                u = unit(3)
                if u:
                    act.wait_ge(d_kT, u.n + 1)
                    if u.c >= 1:
                        act.wait_ge(d_u1, u.n)
                    nc.scalar.activation(kt[:, :], bank[0][:, 0:P], ACT.Copy).then_inc(d_kts, 1)
                u = unit(2)
                if u:
                    act.wait_ge(d_rp, u.n + 1)
                    if u.c >= 4:
                        act.wait_ge(d_w1, u.n - 2)
                        act.wait_ge(d_qkt, u.n - 3)
                    nc.scalar.activation(ee[:, u.r4, 0:132], rp[:, :], ACT.Exp).then_inc(d_ep, 1)
                    act.wait_ge(d_rm, u.n + 1)
                    nc.scalar.activation(ee[:, u.r4, 132:260], rm[:, :], ACT.Exp, scale=-1.0).then_inc(d_em, 1)
                u = unit(1)
                if u:
                    act.wait_ge(d_lt, u.n + 1)
                    if u.c >= 2:
                        act.wait_ge(d_z, u.n - 1)
                    nc.scalar.activation(lowt[0:32, u.r2, :], bank[3][0:32, P:2 * P], ACT.Copy).then_inc(d_lts, 1)

            unit_slots(act, slot, NU + 3)

            def squares(b):
                act.wait_ge(f_oa, b + 1)
                nc.scalar.activation(osq[:, :, :], oa[:, :, :], ACT.Square).then_inc(f_sq, 1)

            def head_rstd(b):
                act.wait_ge(f_hs, b + 1)
                nc.scalar.activation(hl[:, :], hs[:, :], ACT.Ln, bias=epst[:, 0:1], scale=1.0 / HDV)\
                    .then_inc(f_hl, 1)
                act.wait_ge(f_hl, b + 1)
                nc.scalar.activation(hr[:, :], hl[:, :], ACT.Exp, scale=-0.5).then_inc(f_hr, 1)

            def row_rstd(b):
                act.wait_ge(f_mv, b * TB + TB)
                nc.scalar.activation(lnv[:, :], mv[:, :, 1], ACT.Ln, bias=epst[:, 0:1]).then_inc(f_lnv, 1)
                act.wait_ge(f_lnv, b + 1)
                nc.scalar.activation(rstd[:, :], lnv[:, :], ACT.Exp, scale=-0.5).then_inc(f_rstd, 1)

            def norm2(b):
                act.wait_ge(f_shift, b + 1)
                if b >= 2:
                    act.wait_ge(xp_st[b % 2], 16 * (b // 2))
                    act.wait_ge(f_tp2, 2 * b - 2)
                for j in range(TB):
                    nc.scalar.activation(xn2[:, b % 2, j, :], x1[:, b % 2, j, :], ACT.Identity,
                                         bias=shift[:, j:j + 1], scale=rstd[:, j:j + 1]).then_inc(f_xn2, 1)

            def out_t(b):
                for k in range(2):
                    act.wait_ge(f_tp, 2 * b + k + 1)
                    nc.scalar.activation(ont[:, k, :], bank[k][:, :], ACT.Copy).then_inc(f_ont, 1)

            def norm_t(b):
                if b == 0:
                    for r in range(4):
                        act.wait_ge(d_st[r], 16 * (NU // 4))
                for k in range(2):
                    act.wait_ge(f_tp2, 2 * b + k + 1)
                    nc.scalar.activation(xn2t[:, k, :], bank[4 + k][:, :], ACT.Copy).then_inc(f_xt2, 1)

            for b in range(B + 3):
                if b < B:
                    squares(b)
                if 2 <= b < B + 2:
                    row_rstd(b - 2)
                if b < B:
                    head_rstd(b)
                if 2 <= b < B + 2:
                    norm2(b - 2)
                for c in routed(b):
                    norm_t(c)
                if b < B:
                    out_t(b)
            act.wait_ge(s_sub, 1)
            nc.scalar.activation(pr[:, :, :], l8[:, :, :], ACT.Exp).then_inc(s_exp, 1)

            act.wait_ge(b1_t, 1)
            nc.scalar.activation(b1c[:, :], bank[7][:, 0:E * FT], ACT.Copy).then_inc(b1_c, 1)
            act.wait_ge(b1_c, 1)

            def rows_t(e, r):
                for k in range(2):
                    act.wait_ge(e_tp, 2 * e + k + 1)
                    nc.scalar.activation(xet[:, r, k, :], bank[k][:, :], ACT.Copy).then_inc(e_xt, 1)

            def e_slot(e, r, first, last, col):
                if not first:
                    act.wait_ge(e_y, JT * (e - 1))
                for f in range(FT):
                    act.wait_ge(e_h, FT * e + f + 1)
                    nc.scalar.activation(ht[:, r, f, :], bank[2 + f % 4][:, :], ACT.Gelu_apprx_tanh,
                                         bias=b1c[:, col(f)]).then_inc(e_gl, 1)
                    if f == 3 and not last:
                        rows_t(e + 1, 1 - r)

            rows_t(0, 0)
            for e in range(E):
                e_slot(e, e % 2, e < 2, e == E - 1, lambda f: slice(e * FT + f, e * FT + f + 1))

        @block.vector
        def _(dve):
            def norm_tiles(src, dst, b, st_sem, mv_sem, rs_sem, xn_sem):
                for j in range(TB):
                    nc.vector.bn_stats(st6[:, j, :], src(j)).then_inc(st_sem, 1)
                dve.wait_ge(st_sem, b * TB + TB)
                nc.vector.memset(held[:, :], 0.0)
                for j in range(TB):
                    nc.vector.bn_aggr(mv[:, j, :], st6[:, j, :]).then_inc(mv_sem, 1)
                dve.wait_ge(rs_sem, b + 1)
                for j in range(TB):
                    nc.vector.tensor_scalar(dst(j), src(j), mv[:, j, 0:1], rstd[:, j:j + 1],
                                            ALU.subtract, ALU.mult).then_inc(xn_sem, 1)

            def gate_tiles(b):
                for j in range(TB):
                    t = b * TB + j
                    pg = bank[2 + j % 2]
                    dve.wait_ge(a_2, t + 1)
                    nc.vector.tensor_copy(lg[:, t, :], pg[:, D:D + M]).then_inc(a_lg, 1)
                    if not (isinstance(t, int) and t < 2):
                        dve.wait_ge(a_gs, t - 1)
                    nc.vector.tensor_tensor(eg3[:, j % 2, :], pg[:, 0:D], eg2[:, j % 2, :], ALU.mult).then_inc(a_3, 1)
                    dve.wait_ge(a_3, t + 1)
                    nc.vector.tensor_tensor(gs[:, t, :], eg3[:, j % 2, :], nwb[:, :], ALU.mult).then_inc(a_gs, 1)

            def load_wait(r, n):
                dve.wait_ge(x_in[r], 16 * n)

            def norm_a(b):
                norm_tiles(lambda j: xres[:, b * TB + j, :], lambda j: xn[:, b * TB + j, :], b,
                           a_st, a_mv, a_rstd, a_xn)

            load_wait(0, 1)
            norm_a(0)
            dve.wait_ge(wg_in, 16 * 3)
            load_wait(1, 1)
            norm_a(1)
            gate_tiles(0)
            with dve.Fori(1, B // 2) as i:
                load_wait(0, i + 1)
                norm_a(i * 2)
                gate_tiles(i * 2 - 1)
                load_wait(1, i + 1)
                norm_a(i * 2 + 1)
                gate_tiles(i * 2)
            gate_tiles(B - 1)

            dve.wait_ge(c_step, CONST_STEPS)
            nc.vector.tensor_scalar(lane[:, :], lane[:, :], E - 1, None, ALU.bitwise_and).then_inc(c_dve, 1)
            dve.wait_ge(c_dve, 1)
            nc.vector.tensor_scalar(same[:, :], lane[:, :], 0.0, None, ALU.is_equal).then_inc(c_dve, 1)

            done = [0]

            def step(ins):
                done[0] += 1
                ins.then_inc(r_step, 1)
                dve.wait_ge(r_step, done[0])

            per_m = lambda a: a.unsqueeze(2).to_broadcast([P, NT, M])
            dve.wait_ge(a_lg, NT)
            step(nc.vector.tensor_reduce(rs[0][:, :], lg[:, :, :], AX.X, ALU.max))
            nc.vector.tensor_tensor(rt[0][:, :, :], lg[:, :, :], per_m(rs[0][:, :]), ALU.subtract).then_inc(r_sub, 1)
            dve.wait_ge(r_exp, 1)
            step(nc.vector.tensor_reduce(rs[1][:, :], rt[1][:, :, :], AX.X, ALU.add))
            step(nc.vector.reciprocal(rs[2][:, :], rs[1][:, :]))
            step(nc.vector.tensor_tensor(rt[2][:, :, :], rt[1][:, :, :], per_m(rs[2][:, :]), ALU.mult))
            prob, value = rt[2], [rs[3], rs[4]]
            pick = [rt[4], rt[5]]
            keyb = keyw[:, :].unsqueeze(1).to_broadcast([P, NT, M])
            for k in range(2):
                step(nc.vector.tensor_reduce(value[k][:, :], prob[:, :, :], AX.X, ALU.max))
                step(nc.vector.tensor_tensor(rt[3][:, :, :], prob[:, :, :], per_m(value[k][:, :]), ALU.is_equal))
                step(nc.vector.tensor_tensor(rt[6][:, :, :], rt[3][:, :, :], keyb, ALU.mult))
                step(nc.vector.tensor_reduce(rs[5][:, :], rt[6][:, :, :], AX.X, ALU.max))
                step(nc.vector.tensor_tensor(pick[k][:, :, :], rt[6][:, :, :], per_m(rs[5][:, :]), ALU.is_equal))
                if k == 0:
                    step(nc.vector.scalar_tensor_tensor(rt[7][:, :, :], pick[0][:, :, :], -4.0, prob[:, :, :],
                                                        ALU.mult, ALU.add))
                    prob = rt[7]
            nc.vector.tensor_tensor(rt[8][:, :, :], pick[0][:, :, :], pick[1][:, :, :], ALU.add).then_inc(r_rout, 1)
            step(nc.vector.tensor_tensor(rs[6][:, :], value[0][:, :], value[1][:, :], ALU.add))
            step(nc.vector.reciprocal(rs[7][:, :], rs[6][:, :]))
            dve.wait_ge(r_suf, 1)
            suf = bank[4][:, 0:NT * M].rearrange("p (t m) -> p t m", m=M)
            step(nc.vector.tensor_scalar(rt[0][:, :, :], suf, float(CAP - 1), None, ALU.is_le))
            lastr = lastrow[:, :, :, :].rearrange("p b j m -> p (b j) m")
            step(nc.vector.tensor_tensor(rt[1][:, :, :], lastr, suf, ALU.subtract))
            nc.vector.memset(held[:, :], 0.0).then_inc(r_read, 1)
            def assign(k):
                step(nc.vector.tensor_tensor(rt[2][:, :, :], pick[k][:, :, :], rt[0][:, :, :], ALU.mult))
                step(nc.vector.tensor_reduce(rs[8][:, :], rt[2][:, :, :], AX.X, ALU.add))
                step(nc.vector.tensor_tensor(rt[3][:, :, :], rt[2][:, :, :], rt[1][:, :, :], ALU.mult))
                step(nc.vector.tensor_reduce(rs[9][:, :], rt[3][:, :, :], AX.X, ALU.add))
                step(nc.vector.tensor_tensor(rs[10][:, :], value[k][:, :], rs[7][:, :], ALU.mult))
                step(nc.vector.tensor_tensor(wt[:, k, :], rs[10][:, :], rs[8][:, :], ALU.mult))
                nc.vector.tensor_copy(gidx[:, k, :], rs[9][:, :]).then_inc(r_idx, 1)
                for h in range(2):
                    tiles = slice(NT // 2 * h, NT // 2 * h + NT // 2)
                    step(nc.vector.tensor_scalar(rs[10][:, tiles], rs[8][:, tiles], -OUT_OF_RANGE,
                                                 OUT_OF_RANGE + NU_SH * P + HALF_ROWS * h, ALU.mult, ALU.add))
                step(nc.vector.tensor_tensor(rs[11][:, :], rs[10][:, :], rs[9][:, :], ALU.add))
                nc.vector.tensor_copy(sidx[:, k, :], rs[11][:, :]).then_inc(r_idx, 1)

            def slot(unit):
                u = unit(2)
                if u:
                    dve.wait_ge(d_ln, u.n + 1)
                    if u.c >= 1:
                        dve.wait_ge(d_r, u.n)
                    nc.vector.scalar_tensor_tensor(gg[:, :], bank[3][:, 0:P], 0.0, zln[:, :],
                                                   ALU.min, ALU.subtract).then_inc(d_g, 1)
                u = unit(3)
                if u:
                    dve.wait_ge(d_qT, u.n + 1)
                    if u.c >= 2:
                        dve.wait_ge(d_o, u.n - 1)
                    nc.vector.tensor_tensor(qbd[:, u.r2, :, :],
                                            bank[5][:, 0:P].unsqueeze(1).to_broadcast([P, NH, P]),
                                            headm[:, :, :], ALU.mult).then_inc(d_qbd, 1)
                u = unit(2)
                if u:
                    dve.wait_ge(d_r, u.n + 1)
                    if u.c >= 1:
                        dve.wait_ge(d_ep, u.n)
                        dve.wait_ge(d_em, u.n)
                    nc.vector.tensor_scalar(rp[:, :], bank[4][:, 0:132], EXP_LIM, None, ALU.min).then_inc(d_rp, 1)
                    dve.wait_ge(d_rp, u.n + 1)
                    nc.vector.tensor_scalar(rm[:, :], rp[:, 0:P], -EXP_LIM, None, ALU.max).then_inc(d_rm, 1)
                    dve.wait_ge(d_em, u.n + 1)
                    dve.wait_ge(d_qks, u.n + 1)
                    if u.c >= 2:
                        dve.wait_ge(d_u1, u.n - 1)
                    nc.vector.tensor_tensor(
                        qkt[:, u.r2, :].rearrange("p (a c) -> p a c", a=2),
                        qks[:, u.r2, 0:2 * P].rearrange("p (a c) -> p a c", a=2),
                        ee[:, u.r4, :].rearrange("p (a c) -> p a c", a=2)[:, :, 0:P], ALU.mult).then_inc(d_qkt, 1)
                u = unit(4)
                if u:
                    dve.wait_ge(d_o, u.n + 1)
                    if u.c >= 4:
                        dve.wait_ge(d_st[u.r4], u.quad * 16)
                    nc.vector.tensor_copy(ob[:, u.r4, :], bank[7][:, 0:D]).then_inc(d_ob, 1)
                u = unit(3)
                if u:
                    dve.wait_ge(d_s, u.n + 1)
                    for c in range(2):
                        for lo, t0, t1 in HALVES:
                            h = slice(CH * c, CH * c + lo)
                            ins = nc.vector.tensor_tensor(
                                am[h, u.r2, :, CH * c + t0:CH * c + t1],
                                bank[6][h, 0:NH * CH].rearrange("p (h t) -> p h t", h=NH)[:, :, t0:t1],
                                causal[h, t0:t1].unsqueeze(1).to_broadcast([lo, NH, t1 - t0]), ALU.mult)
                    ins.then_inc(d_am, 1)
                    if u.first:
                        nc.vector.memset(s0[:, u.r2, :], 0.0).then_inc(d_s0, 1)
                    else:
                        dve.wait_ge(d_w1, u.n)
                        dve.wait_ge(d_ep, u.n + 1)
                        nc.vector.tensor_scalar(s0[:, u.r2, :], wb[:, :], ee[:, u.r4, P:P + 1],
                                                ee[:, (u.r4 - 1) % 4, P + 2:P + 3], ALU.mult, ALU.mult)\
                            .then_inc(d_s0, 1)
                    dve.wait_ge(d_s0, u.n + 1)
                    nc.vector.tensor_tensor(wa[:, :], bank[6][:, 256:256 + HDV], s0[:, u.r2, :], ALU.add)\
                        .then_inc(d_w0, 1)
                    dve.wait_ge(d_w0, u.n + 1)
                    nc.vector.tensor_scalar(s1[:, u.r2, :], wa[:, :], ee[:, u.r4, P + 1:P + 2], None, ALU.mult)\
                        .then_inc(d_s1, 1)
                    dve.wait_ge(d_s1, u.n + 1)
                    dve.wait_ge(d_u1, u.n + 1)
                    nc.vector.tensor_tensor(wb[:, :], bank[5][:, 256:256 + HDV], s1[:, u.r2, :], ALU.add)\
                        .then_inc(d_w1, 1)

            def slot_and_routing(unit):
                slot(unit)
                u = unit(0)
                if u and u.c in ASSIGN_SLOTS:
                    assign(ASSIGN_SLOTS.index(u.c))

            unit_slots(dve, slot_and_routing, NU + 3)

            def combine(b):
                if b < 2:
                    dve.wait_ge(f_first[b], 16)
                else:
                    dve.wait_ge(f_sh[b % 3], 16 * (b // 3 + (b % 3 == 2)))
                dve.wait_ge(f_g[b % 4], 16 * 2 * TB * (b // 4 + 1))
                if b:
                    dve.wait_ge(f_sq, b)
                    dve.wait_ge(f_on, b)
                for j in range(TB):
                    t = b * TB + j
                    nc.vector.scalar_tensor_tensor(oa[:, j, :], og[:, b % 4, 0, j, :], wt[:, 0, t:t + 1],
                                                   osh[b % 3][:, j, :], ALU.mult, ALU.add).then_inc(f_a0, 1)
                for j in range(TB):
                    t = b * TB + j
                    dve.wait_ge(f_a0, t + 1)
                    ins = nc.vector.scalar_tensor_tensor(oa[:, j, :], og[:, b % 4, 1, j, :], wt[:, 1, t:t + 1],
                                                         oa[:, j, :], ALU.mult, ALU.add)
                ins.then_inc(f_oa, 1)

            def head_squares(b):
                dve.wait_ge(f_sq, b + 1)
                nc.vector.tensor_reduce(hs[:, :], osq[:, :, :].rearrange("p j (h v) -> p (j h) v", h=NH),
                                        AX.X, ALU.add).then_inc(f_hs, 1)

            def gated(b):
                dve.wait_ge(f_hr, b + 1)
                nc.vector.tensor_tensor(on[:, :, :].rearrange("p j (h v) -> p (j h) v", h=NH),
                                        oa[:, :, :].rearrange("p j (h v) -> p (j h) v", h=NH),
                                        hr[:, :].unsqueeze(2).to_broadcast([P, TB * NH, HDV]), ALU.mult)\
                    .then_inc(f_on, 1)
                dve.wait_ge(f_on, b + 1)
                if b:
                    dve.wait_ge(f_tp, 2 * b)
                nc.vector.tensor_tensor(on2[:, :, :], on[:, :, :], gs[:, b * TB:b * TB + TB, :], ALU.mult)\
                    .then_inc(f_on2, 1)

            def residual(b):
                if b >= 2:
                    dve.wait_ge(out_st[b % 2], 16 * (b // 2))
                for q in range(2):
                    dve.wait_ge(f_y, 2 * b + q + 1)
                    nc.vector.tensor_tensor(x1[:, b % 2, 2 * q:2 * q + 2, :],
                                            bank[2 + q][:, :].rearrange("p (j d) -> p j d", j=2),
                                            xres[:, b * TB + 2 * q:b * TB + 2 * q + 2, :], ALU.add).then_inc(f_x1, 1)

            def row_stats(b):
                dve.wait_ge(f_x1, 2 * b + 2)
                if b:
                    dve.wait_ge(f_xn2, TB * b)
                for j in range(TB):
                    nc.vector.bn_stats(st6[:, j, :], x1[:, b % 2, j, :]).then_inc(f_st, 1)
                dve.wait_ge(f_st, b * TB + TB)
                for j in range(TB):
                    nc.vector.bn_aggr(mv[:, j, :], st6[:, j, :]).then_inc(f_mv, 1)

            def norm_shift(b):
                dve.wait_ge(f_rstd, b + 1)
                nc.vector.scalar_tensor_tensor(shift[:, :], mv[:, :, 0], -1.0, rstd[:, :], ALU.mult, ALU.mult)\
                    .then_inc(f_shift, 1)

            def router(b):
                dve.wait_ge(f_l, b + 1)
                nc.vector.tensor_tensor(l8[:, b * TB:b * TB + TB, :],
                                        bank[6 + b % 2][:, 0:TB * E].rearrange("p (j e) -> p j e", e=E),
                                        bsb[:, :].unsqueeze(1).to_broadcast([P, TB, E]), ALU.add).then_inc(f_l8, 1)

            dve.wait_ge(w_in2, 16 * 5)
            for b in range(B + 4):
                if b < B:
                    combine(b)
                if 2 <= b < B + 2:
                    row_stats(b - 2)
                if b < B:
                    head_squares(b)
                if b >= 4:
                    router(b - 4)
                if 2 <= b < B + 2:
                    norm_shift(b - 2)
                if b < B:
                    gated(b)
                if 1 <= b <= B:
                    residual(b - 1)

            done[0] = 0

            def sstep(ins):
                done[0] += 1
                ins.then_inc(s_step, 1)
                dve.wait_ge(s_step, done[0])

            per_e = lambda a: a.unsqueeze(2).to_broadcast([P, NT, E])
            dve.wait_ge(f_l8, B)
            sstep(nc.vector.tensor_reduce(rs[0][:, :], l8[:, :, :], AX.X, ALU.max))
            nc.vector.tensor_tensor(l8[:, :, :], l8[:, :, :], per_e(rs[0][:, :]), ALU.subtract).then_inc(s_sub, 1)
            dve.wait_ge(s_exp, 1)
            sstep(nc.vector.tensor_reduce(rs[1][:, :], pr[:, :, :], AX.X, ALU.add))
            sstep(nc.vector.reciprocal(rs[2][:, :], rs[1][:, :]))
            by_h = lambda a: a.rearrange("p (q h) e -> p h q e", h=2)
            nc.vector.tensor_tensor(p8[:, :, :, :], by_h(pr[:, :, :]), by_h(per_e(rs[2][:, :])), ALU.mult)\
                .then_inc(s_p8, 1)

            nc.vector.memset(base[:, :], 0).then_inc(s_base, 1)
            for c in range(3):
                nc.vector.memset(steps[:, 0, c:c + 1], (c + 1) << 28)
                ins = nc.vector.memset(cand[:, c:c + 1], (c + 1) << 28)
            ins.then_inc(s_cand, 1)
            dve.wait_ge(s_cand, 1)
            nc.vector.memset(cand2[:, :], 0).then_inc(s_bit, 1)
            dve.wait_ge(s_tp, 1)
            nc.vector.tensor_copy(pt[:, :], bank[0][:, 0:NT * E]).then_inc(s_tp, 1)
            dve.wait_ge(s_tp, 2)

            def search(n, r):
                r1 = (r + 1) % 3
                dve.wait_ge(s_cand, n + 1)
                for c in range(3):
                    ins = nc.vector.tensor_scalar(cmp[:, c, :], pt[:, :], cand[:, c:c + 1].bitcast(F32), None,
                                                  ALU.is_ge, ALU.add, accum_out=reached[:, c:c + 1])
                ins.then_inc(s_cmp, 1)
                dve.wait_ge(s_bit, n + 1)
                nc.vector.tensor_scalar(steps[:, r1, :], steps[:, r, :], 2, None, ALU.logical_shift_right)\
                    .then_inc(s_bit, 1)
                dve.wait_ge(s_bit, n + 2)
                dve.wait_ge(s_base, n + 1)
                nc.vector.tensor_tensor(cand2[:, :], base[:, :].to_broadcast([P, 3]), steps[:, r1, :],
                                        ALU.bitwise_xor).then_inc(s_cand2, 1)
                dve.wait_ge(s_cnt, n + 1)
                nc.vector.tensor_scalar(enough[:, :], bank[1][:, 0:3], float(KTOP), None, ALU.is_ge, ALU.add,
                                        accum_out=digit4[:, :]).then_inc(s_four, 1)
                dve.wait_ge(s_four, n + 1)
                nc.vector.scalar_tensor_tensor(add4[:, :], digit4[:, :], 1.0, steps[:, r, 0:1],
                                               ALU.mult, ALU.mult).then_inc(s_add, 1)
                dve.wait_ge(s_add, n + 1)
                dve.wait_ge(s_cand2, n + 1)
                nc.vector.tensor_tensor(cand[:, :], cand2[:, :], add4[:, :].to_broadcast([P, 3]), ALU.bitwise_xor)\
                    .then_inc(s_cand, 1)
                nc.vector.tensor_tensor(base[:, :], base[:, :], add4[:, :], ALU.bitwise_xor).then_inc(s_base, 1)

            with dve.Fori(0, 5) as i:
                for r in range(3):
                    search(i * 3 + r, r)
            dve.wait_ge(s_cand, 16)
            dve.wait_ge(s_bit, 16)
            dve.wait_ge(s_base, 16)

            thr = base[:, :].bitcast(F32)
            sstep(nc.vector.tensor_scalar(picked[:, 0, :], pt[:, :], thr, None, ALU.is_gt))
            sstep(nc.vector.tensor_scalar(picked[:, 1, :], pt[:, :], thr, None, ALU.is_equal))
            for k in range(2):
                nc.vector.tensor_tensor_scan(incl[:, k, :], ones_w[:, :], picked[:, k, :], 0.0, ALU.mult, ALU.add)\
                    .then_inc(s_incl, 1)
            dve.wait_ge(s_offs, 1)
            sstep(nc.vector.tensor_copy(offs[:, 0:3], bank[1][:, 4:7]))
            sstep(nc.vector.tensor_tensor(offs[:, 3:4], offs[:, 1:2], offs[:, 2:3], ALU.add))
            sstep(nc.vector.scalar_tensor_tensor(place[:, 0, :], incl[:, 0, :], offs[:, 0:1], picked[:, 0, :],
                                                 ALU.add, ALU.mult))
            sstep(nc.vector.scalar_tensor_tensor(place[:, 1, :], incl[:, 1, :], offs[:, 3:4], picked[:, 1, :],
                                                 ALU.add, ALU.mult))
            sstep(nc.vector.scalar_tensor_tensor(place[:, 2, :], place[:, 1, :], float(KTOP), place[:, 1, :],
                                                 ALU.is_le, ALU.mult))
            nc.vector.tensor_tensor(place[:, 0, :], place[:, 0, :], place[:, 2, :], ALU.add).then_inc(s_place, 1)
            dve.wait_ge(s_back, 1)
            et = lambda a: a.rearrange("p (e t) -> p e t", e=E)
            sstep(nc.vector.tensor_scalar(et(posi[:, :]), bank[2][:, 0:NT * E].rearrange("p (t e) -> p e t", e=E),
                                          -1.0, None, ALU.add))
            sstep(nc.vector.tensor_scalar(digit[:, 0, :], posi[:, :], 4, None, ALU.arith_shift_right))
            sstep(nc.vector.tensor_scalar(digit[:, 1, :], posi[:, :], 15, None, ALU.bitwise_and))
            nc.vector.tensor_copy(digit_bf[:, :, :], digit[:, :, :]).then_inc(s_digit, 1)
            dve.wait_ge(s_digit, 1)
            for c in range(16):
                nc.vector.tensor_scalar(ohb[:, :, c, :], et(digit_bf[:, 1, :]), float(c), pidx[:, 0:1],
                                        ALU.is_equal, ALU.mult)
                nc.vector.scalar_tensor_tensor(ohb[:, :, 16 + c, :], et(digit_bf[:, 1, :]), float(c),
                                               et(tile_no[:, :]), ALU.is_equal, ALU.mult)
            for c in range(POOL_DIGITS, 32):
                ins = nc.vector.tensor_scalar(oha[:, :, c, :], et(digit_bf[:, 0, :]), float(c), None, ALU.is_equal)
            ins.then_inc(s_oh, 1)
            dve.wait_ge(s_idx, 1)
            sstep(nc.vector.tensor_copy(cidx[:, :, :], bank[3][:, 0:256].rearrange("p (g c) -> p g c", g=2)))
            for e in range(4):
                q = slice(32 * e, 32 * e + 32)
                nc.vector.scalar_tensor_tensor(idxc[q, :, :], cidx[q, :, 32 * e + 16:32 * e + 32], float(P),
                                               cidx[q, :, 32 * e:32 * e + 16], ALU.mult, ALU.add)\
                    .then_inc(s_idxc, 1)

            for e in range(E):
                r = e % 2
                if e:
                    dve.wait_ge(e_ye, JT * e)
                for j in range(JT):
                    n = JT * e + j
                    dve.wait_ge(e_y, n + 1)
                    nc.vector.tensor_tensor(yb[:, j, :], bank[6 + j % 2][:, 0:D], b2b[:, e, :], ALU.add)\
                        .then_inc(e_yb, 1)
                    dve.wait_ge(e_yb, n + 1)
                    if e >= 2 and j == 0:
                        dve.wait_ge(e_st, 16 * JT * (e - 1))
                    nc.vector.tensor_scalar(ye[:, r, j, :], yb[:, j, :], xe[:, e % 3, j, D + e:D + e + 1], None,
                                            ALU.mult).then_inc(e_ye, 1)

        @block.tensor
        def _(pe):
            pe.wait_ge(c_step, FIRST_STEPS)
            pe.wait_ge(wg_in, 16 * 3)

            def a_transpose(t):
                pe.wait_ge(a_xn, t + 1)
                if t >= 2:
                    pe.wait_ge(a_xt, t - 1)
                for k in range(2):
                    ins = nc.tensor.transpose(bank[t % 2][:, P * k:P * k + P], xn[:, t, P * k:P * k + P],
                                              ident[:, :])
                ins.then_inc(a_tp, 1)

            def a_product(t):
                pe.wait_ge(a_xt, t + 1)
                if t >= 2:
                    pe.wait_ge(a_3, t - 1)
                for k in range(2):
                    ins = nc.tensor.matmul(bank[2 + t % 2][:, 0:D + M], xta[:, t % 2, k, :], wgg[:, k, :],
                                           start=(k == 0), stop=(k == 1))
                ins.then_inc(a_g, 1)

            a_transpose(0)
            for t in range(NT):
                if t + 1 < NT:
                    a_transpose(t + 1)
                a_product(t)
            pe.wait_ge(c_step, CONST_STEPS)
            pe.wait_ge(w_in, 16 * W_IN)

            def mm(out_, l, r, a=True, z=True):
                return nc.tensor.matmul(out_, l, r, start=a, stop=z, skip_group_check=True)

            def slot(unit):
                u = unit(0)
                if u:
                    pe.wait_ge(d_in[u.r4], 16 * u.quad + 16)
                    if u.c >= 4:
                        pe.wait_ge(d_kts, u.n - 3)
                    elif u.c >= 1:
                        pe.wait_ge(d_xt, u.n)
                    for k in range(2):
                        ins = nc.tensor.transpose(bank[0][:, P * k:P * k + P], xin[:, u.r4, P * k:P * k + P],
                                                  ident[:, :])
                    ins.then_inc(d_tp, 1)
                u = unit(2)
                if u:
                    pe.wait_ge(d_lts, u.n + 1)
                    mm(bank[3][:, 0:P], lowt[0:LOW + 1, u.r2, :], w2g[0:LOW + 1, u.stream, :]).then_inc(d_z, 1)
                u = unit(1)
                if u:
                    pe.wait_ge(d_xt, u.n + 1)
                    if u.c >= 1:
                        pe.wait_ge(d_qks, u.n)
                        pe.wait_ge(d_vs, u.n)
                    for k in range(2):
                        ins = mm(bank[1][:, 0:QKL], xt[:, u.r2, k, :], wqk[:, u.stream, k, :], k == 0, k == 1)
                    ins.then_inc(d_qk, 1)
                    for k in range(2):
                        ins = mm(bank[2][:, 0:D], xt[:, u.r2, k, :], wv[:, u.stream, k, :], k == 0, k == 1)
                    ins.then_inc(d_v, 1)
                u = unit(3)
                if u:
                    pe.wait_ge(d_qkt, u.n + 1)
                    if u.c >= 1:
                        pe.wait_ge(d_w1, u.n)
                    nc.tensor.transpose(bank[5][:, 0:P], qkt[:, u.r2, 0:P], ident[:, :]).then_inc(d_qT, 1)
                    if unit(0):
                        pe.wait_ge(d_xt, u.n + 4)
                    else:
                        pe.wait_ge(d_kts, u.n)
                    nc.tensor.transpose(bank[0][:, 0:P], qkt[:, u.r2, P:2 * P], ident[:, :]).then_inc(d_kT, 1)
                u = unit(2)
                if u:
                    pe.wait_ge(d_g, u.n + 1)
                    if u.c >= 1:
                        pe.wait_ge(d_rm, u.n)
                    mm(bank[4][:, 0:P], relm[:, :], gg[:, :])
                    mm(bank[4][:, P:P + 4], gg[:, :], spanm[:, :]).then_inc(d_r, 1)
                u = unit(1)
                if u:
                    pe.wait_ge(d_qks, u.n + 1)
                    if u.c >= 1:
                        pe.wait_ge(d_g, u.n)
                    nc.tensor.transpose(bank[3][0:32, P:2 * P], qks[:, u.r2, 2 * P:2 * P + 32], ident[:, :])\
                        .then_inc(d_lt, 1)
                u = unit(4)
                if u:
                    pe.wait_ge(d_am, u.n + 1)
                    pe.wait_ge(d_s1, u.n + 1)
                    if u.c >= 1:
                        pe.wait_ge(d_ob, u.n)
                    for g in range(NH):
                        mm(bank[7][:, HDV * g:HDV * g + HDV], am[:, u.r2, g, :],
                           vv[:, u.r4, HDV * g:HDV * g + HDV], g == 0, False)
                    for c in range(2):
                        if c == 0 and u.first:
                            continue
                        h = slice(CH * c, CH * c + CH)
                        for g in range(NH):
                            ins = mm(bank[7][h, HDV * g:HDV * g + HDV], qbd[:, u.r2, g, h],
                                     (s1 if c else s0)[:, u.r2, :], False, True)
                    ins.then_inc(d_o, 1)
                u = unit(3)
                if u:
                    pe.wait_ge(d_qbd, u.n + 1)
                    pe.wait_ge(d_kts, u.n + 1)
                    if u.c >= 1:
                        pe.wait_ge(d_w0, u.n)
                    for c in range(2):
                        for lo, t0, t1 in HALVES:
                            h = slice(CH * c, CH * c + lo)
                            mm(bank[6][h, 0:NH * CH].rearrange("p (h t) -> p h t", h=NH)[:, :, t0:t1],
                               kt[:, h], qbd[:, u.r2, :, CH * c + t0:CH * c + t1])
                    for c in range(2):
                        h = slice(CH * c, CH * c + CH)
                        for g in range(NH):
                            ins = mm(bank[6 - c][HDK * g:HDK * g + HDK, 256:256 + HDV],
                                     qkt[h, u.r2, P + HDK * g:P + HDK * g + HDK],
                                     vv[h, u.r4, HDV * g:HDV * g + HDV])
                        ins.then_inc(d_u1 if c else d_s, 1)

            def counts():
                pe.wait_ge(r_rout, 1)
                cnt = bank[4][:, 0:NT * M]
                rflat = rt[8][:, :, :].rearrange("p t m -> p (t m)")
                nc.tensor.matmul(cnt, after[:, :], rflat, start=True, stop=False, skip_group_check=True)
                r4 = rflat.rearrange("p (b j m) -> p b j m", b=B, m=M)
                c4 = cnt.rearrange("p (b j m) -> p b j m", b=B, m=M)
                for d in range(1, TB):
                    ins = nc.tensor.matmul(c4[:, :, 0:TB - d, :], ones[:, :], r4[:, :, d:TB, :], start=False,
                                           stop=(d == TB - 1), skip_group_check=True)
                ins.then_inc(r_suf, 1)
                pe.wait_ge(r_read, 1)

            def slot_and_routing(unit):
                slot(unit)
                u = unit(0)
                if u and u.c == 1:
                    counts()

            unit_slots(pe, slot_and_routing, NU + 3)
            pe.wait_ge(d_ob, NU)

            pe.wait_ge(w_in2, 16 * 5)

            def project(b):
                pe.wait_ge(f_on2, b + 1)
                for k in range(2):
                    if b:
                        pe.wait_ge(f_ont, 2 * b)
                    for j in range(TB):
                        ins = nc.tensor.transpose(bank[k][:, P * j:P * j + P], on2[:, j, P * k:P * k + P],
                                                  ident[:, :])
                    ins.then_inc(f_tp, 1)
                pe.wait_ge(f_ont, 2 * b + 2)
                if b:
                    pe.wait_ge(f_x1, 2 * b)
                for j in range(TB):
                    for k in range(2):
                        ins = mm(bank[2 + j // 2][:, D * (j % 2):D * (j % 2) + D], ont[:, k, P * j:P * j + P],
                                 wo[:, k, :], k == 0, k == 1)
                    if j % 2:
                        ins.then_inc(f_y, 1)

            def route(b):
                pe.wait_ge(f_xn2, b * TB + TB)
                for k in range(2):
                    for j in range(TB):
                        ins = nc.tensor.transpose(bank[4 + k][:, P * j:P * j + P],
                                                  xn2[:, b % 2, j, P * k:P * k + P], ident[:, :])
                    ins.then_inc(f_tp2, 1)
                pe.wait_ge(f_xt2, 2 * b + 2)
                if b >= 2:
                    pe.wait_ge(f_l8, b - 1)
                for j in range(TB):
                    for k in range(2):
                        ins = mm(bank[6 + b % 2][:, E * j:E * j + E], xn2t[:, k, P * j:P * j + P], wsb[:, k, :],
                                 k == 0, k == 1)
                ins.then_inc(f_l, 1)

            for b in range(B):
                for c in routed(b):
                    route(c)
                project(b)
            route(B - 2)
            route(B - 1)
            pe.wait_ge(f_l8, B)
            nc.tensor.transpose(bank[7][:, 0:E * FT], b1r[:, :], ident[0:E * FT, 0:E * FT]).then_inc(b1_t, 1)

            pe.wait_ge(s_p8, 1)
            for h in range(2):
                ins = nc.tensor.transpose(bank[0][:, P * h:P * h + P], p8[:, h, :, :].rearrange("p q e -> p (q e)"), ident[:, :])
            ins.then_inc(s_tp, 1)
            with pe.Fori(0, 15) as i:
                pe.wait_ge(s_cmp, i + 1)
                mm(bank[1][:, 0:3], same[:, :], reached[:, :]).then_inc(s_cnt, 1)
            pe.wait_ge(s_incl, 2)
            pe.wait_ge(c_step, CONST_STEPS + 2)
            mm(bank[1][:, 4:6], below[:, :], incl[:, :, NT * E - 1:NT * E].rearrange("p k a -> p (k a)"))
            mm(bank[1][:, 6:7], same[:, :], incl[:, 0, NT * E - 1:NT * E]).then_inc(s_offs, 1)
            pe.wait_ge(s_place, 1)
            for h in range(2):
                ins = nc.tensor.transpose(bank[2][:, P * h:P * h + P], place[:, 0, P * h:P * h + P], ident[:, :])
            ins.then_inc(s_back, 1)
            pe.wait_ge(s_oh, 2)
            for t in range(NT):
                for g in range(2):
                    ins = mm(bank[3][:, P * g:P * g + P],
                             oha[:, 4 * g:4 * g + 4, :, t].rearrange("p e c -> p (e c)"),
                             ohb[:, 4 * g:4 * g + 4, :, t].rearrange("p e c -> p (e c)"),
                             t == 0 and g == 0, t == NT - 1)
            ins.then_inc(s_idx, 1)
            pe.wait_ge(b1_c, 1)
            pe.wait_ge(s_idxc, 4)

            def rows_t(e):
                pe.wait_ge(e_x[e % 3], 16 * JT * (e // 3 + 1))
                if e >= 1:
                    pe.wait_ge(e_xt, 2 * e)
                if e >= 2:
                    pe.wait_ge(e_h, FT * (e - 1))
                for k in range(2):
                    for j in range(JT):
                        ins = nc.tensor.transpose(bank[k][:, P * j:P * j + P], xe[:, e % 3, j, P * k:P * k + P],
                                                  ident[:, :])
                    ins.then_inc(e_tp, 1)

            def hidden(e, r):
                pe.wait_ge(e_w[e % NW], 32 * (e // NW + 1))
                pe.wait_ge(e_xt, 2 * e + 2)
                for f in range(FT):
                    if e or f >= 4:
                        pe.wait_ge(e_gl, FT * e + f - 3)
                    for k in range(2):
                        ins = mm(bank[2 + f % 4][:, :], w1s[e % NW][:, k, P * f:P * f + P], xet[:, r, k, :],
                                 k == 0, k == 1)
                    ins.then_inc(e_h, 1)
                    if f == 3 and e + 1 < E:
                        rows_t(e + 1)

            def output(e, r):
                pe.wait_ge(e_gl, FT * e + FT)
                for j in range(JT):
                    n = JT * e + j
                    if n >= 2:
                        pe.wait_ge(e_yb, n - 1)
                    for f in range(FT):
                        ins = mm(bank[6 + j % 2][:, 0:D], ht[:, r, f, P * j:P * j + P], w2s[e % NW][:, f, :],
                                 f == 0, f == FT - 1)
                    ins.then_inc(e_y, 1)

            rows_t(0)
            hidden(0, 0)
            for e in range(1, E):
                hidden(e, e % 2)
                output(e - 1, (e - 1) % 2)
            output(E - 1, (E - 1) % 2)


CONST_STEPS = 56
FIRST_STEPS = 4
W_IN = 6 * NS

_INS = ['x', 'w_gate', 'w_q', 'w_k', 'w_v', 'w_gk1', 'w_gk2', 'b_gk', 'w_ks', 'w_vs', 'w_gk1s', 'w_gk2s', 'b_gks',
        'w_g', 'w_o', 'norm_w']
_INS = ['L0_attn_' + n for n in _INS] + ['L0_ffn_' + n for n in ['Ws', 'bs', 'W1', 'b1', 'W2', 'b2']]
_OUTS = [((B, S, D), 'float32')]


def kernel(**inputs):
    import numpy as _np
    import concourse.bacc as _bacc
    from concourse import mybir as _mybir
    from concourse.bass_utils import run_bass_kernel_spmd as _run

    nc = _bacc.Bacc("TRN2", target_bir_lowering=False, num_devices=1)
    arrays, args = {}, []
    for name in _INS:
        a = _np.ascontiguousarray(inputs[name])
        arrays[f"in_{name}_dram"] = a
        args.append(nc.dram_tensor(f"in_{name}_dram", a.shape, _mybir.dt.from_np(a.dtype), kind="ExternalInput").ap())
    for i, (shape, dtype) in enumerate(_OUTS):
        dt = _mybir.dt.from_np(_np.dtype(dtype))
        args.append(nc.dram_tensor(f"out_{i}_dram", shape, dt, kind="ExternalOutput").ap())
    build(nc, *args)
    r = _run(nc, [arrays], core_ids=[0])
    got = tuple(r.results[0][f"out_{i}_dram"] for i in range(len(_OUTS)))
    return got[0]
```
